# Optimizing a Trainium2 kernel written in Bass

```python
import numpy as np
import jax
import jax.numpy as jnp

def _softmax(x, axis=-1):
    return jax.nn.softmax(x, axis=axis)

def _gelu(x):
    return jax.nn.gelu(x, approximate=True)

def _silu(x):
    return jax.nn.silu(x)

def _sigmoid(x):
    return jax.nn.sigmoid(x)

def _layernorm(x, axis=-1, eps=1e-05):
    m = jnp.mean(x, axis=axis, keepdims=True)
    v = jnp.var(x, axis=axis, keepdims=True)
    return (x - m) / jnp.sqrt(v + eps)

def _scatter_add(tgt, idx, src, axis=0):
    return tgt.at[idx].add(src)

def _segment_sum(src, seg, n):
    return jax.ops.segment_sum(src, seg, n)
kernel_name = 'mk_gnn_ffn_d2_gnn_r8_1ed52c'

def setup_inputs(seed: int=0):
    np.random.seed(seed)
    _w = jnp.asarray

    def _rec_inputs():
        import jax
        import jax.numpy as jnp
        _gk = jax.random.key(seed)
        x = -0.0003713 + 1 * jax.random.normal(jax.random.fold_in(_gk, 1), (6250, 256), jnp.float32)
        _s = jax.random.randint(jax.random.fold_in(_gk, 2), (50000,), 0, 6250, jnp.int32)
        _d = jax.random.randint(jax.random.fold_in(_gk, 3), (50000,), 0, 6250, jnp.int32)
        _loop = jnp.arange(6250, dtype=jnp.int32)
        src = jnp.concatenate([_s, _d, _loop])
        dst = jnp.concatenate([_d, _s, _loop])
        _o = jnp.argsort(dst, stable=True)
        src = src[_o]
        dst = dst[_o]
        edge_weight = jax.random.uniform(jax.random.fold_in(_gk, 12), (106250,), jnp.float32, 0.0, 0.999998)
        return (x, src, dst, edge_weight)
    x, src, dst, edge_weight = _rec_inputs()

    def _L0_gnn_setup():
        import jax, jax.numpy as jnp
        import numpy as np
        N_NODES = 6250
        N_EDGES = 37500
        D = 256
        EPS = 1e-12

        def _gcn_layer(x, W, b, src, dst, norm, n_nodes):
            xt = x @ W
            msg = xt[src] * norm[:, None]
            agg = jax.ops.segment_sum(msg, dst, num_segments=n_nodes)
            return jax.nn.relu(agg + b)
        key = jax.random.key(seed)
        ks = jax.random.split(key, 10)
        h5_all = jax.random.normal(ks[0], (N_NODES, D), dtype=jnp.float32)
        edge_index = jax.random.randint(ks[1], (2, N_EDGES), 0, N_NODES, dtype=jnp.int64)
        edge_weight = jax.random.uniform(ks[2], (N_EDGES,), dtype=jnp.float32)
        s = 1.0 / np.sqrt(D)
        W6 = jax.random.normal(ks[3], (D, D), dtype=jnp.float32) * s
        b6 = jnp.zeros((D,), dtype=jnp.float32)
        W7 = jax.random.normal(ks[4], (D, D), dtype=jnp.float32) * s
        b7 = jnp.zeros((D,), dtype=jnp.float32)
        Wp = jax.random.normal(ks[5], (D, D), dtype=jnp.float32) * s
        bp = jnp.zeros((D,), dtype=jnp.float32)
        return {'h5_all': h5_all, 'edge_index': edge_index, 'edge_weight': edge_weight, 'W6': W6, 'b6': b6, 'W7': W7, 'b7': b7, 'Wp': Wp, 'bp': bp}
    _L0_gnn_all = _L0_gnn_setup()
    _L0_gnn_in = {k: v for k, v in _L0_gnn_all.items() if k in ('W6', 'b6', 'W7', 'b7', 'Wp', 'bp')}
    del _L0_gnn_all

    def _L0_ffn_setup():
        import math
        import jax, jax.numpy as jnp
        import numpy as np
        CAPACITY_FACTOR = 1.25
        TOP_K = 2
        LN_EPS = 1e-05

        def _layer_norm(x, gamma, beta):
            mu = jnp.mean(x, axis=-1, keepdims=True)
            var = jnp.var(x, axis=-1, keepdims=True)
            return (x - mu) * jax.lax.rsqrt(var + LN_EPS) * gamma + beta
        key = jax.random.key(seed)
        ks = jax.random.split(key, 4)
        B, S, D, F, E = (8, 512, 256, 512, 8)
        x = jax.random.normal(ks[0], (B, S, D), dtype=jnp.float32)
        Wr = jax.random.normal(ks[1], (D, E), dtype=jnp.float32) / np.sqrt(D)
        br = jnp.zeros((E,), jnp.float32)
        W1 = jax.random.normal(ks[2], (E, D, F), dtype=jnp.float32) / np.sqrt(D)
        b1 = jnp.zeros((E, F), jnp.float32)
        W2 = jax.random.normal(ks[3], (E, F, D), dtype=jnp.float32) / np.sqrt(F)
        b2 = jnp.zeros((E, D), jnp.float32)
        gamma = jnp.ones((D,), jnp.float32)
        beta = jnp.zeros((D,), jnp.float32)
        return {'x': x, 'Wr': Wr, 'br': br, 'W1': W1, 'b1': b1, 'W2': W2, 'b2': b2, 'gamma': gamma, 'beta': beta}
    _L0_ffn_all = _L0_ffn_setup()
    _L0_ffn_in = {k: v for k, v in _L0_ffn_all.items() if k in ('Wr', 'br', 'W1', 'b1', 'W2', 'b2', 'gamma', 'beta')}
    del _L0_ffn_all

    def _L1_gnn_setup():
        import jax, jax.numpy as jnp
        import numpy as np
        N = 1250
        E = 37500
        D = 256
        key = jax.random.key(seed)
        k1, k2, k3, k4 = jax.random.split(key, 4)
        x = jax.random.normal(k1, (N, D), dtype=jnp.float32)
        edge_index = jax.random.randint(k2, (2, E), 0, N, dtype=jnp.int32)
        s = 1.0 / np.sqrt(D)
        W1 = jax.random.uniform(k3, (D, D), jnp.float32, -s, s)
        b1 = jnp.zeros((D,), jnp.float32)
        W2 = jax.random.uniform(k4, (D, D), jnp.float32, -s, s)
        b2 = jnp.zeros((D,), jnp.float32)
        return {'x': x, 'W1': W1, 'b1': b1, 'W2': W2, 'b2': b2, 'edge_index': edge_index}
    _L1_gnn_all = _L1_gnn_setup()
    _L1_gnn_in = {k: v for k, v in _L1_gnn_all.items() if k in ('W1', 'b1', 'W2', 'b2')}
    del _L1_gnn_all

    def _L1_ffn_setup():
        import math
        import jax, jax.numpy as jnp
        import numpy as np
        CAPACITY_FACTOR = 1.25
        key = jax.random.key(seed)
        ks = jax.random.split(key, 5)
        B, L, D, F, E = (8, 1024, 256, 1024, 8)
        h = jax.random.normal(ks[0], (B, L, D), dtype=jnp.float32)
        gate_w = jax.random.normal(ks[1], (D, E), dtype=jnp.float32) * 0.02
        gate_b = jnp.zeros((E,), dtype=jnp.float32)
        w1 = jax.random.normal(ks[2], (E, D, F), dtype=jnp.float32) * (1.0 / math.sqrt(D))
        b1 = jnp.zeros((E, F), dtype=jnp.float32)
        w2 = jax.random.normal(ks[3], (E, F, D), dtype=jnp.float32) * (1.0 / math.sqrt(F))
        b2 = jnp.zeros((E, D), dtype=jnp.float32)
        return {'h': h, 'gate_w': gate_w, 'gate_b': gate_b, 'w1': w1, 'b1': b1, 'w2': w2, 'b2': b2}
    _L1_ffn_all = _L1_ffn_setup()
    _L1_ffn_in = {k: v for k, v in _L1_ffn_all.items() if k in ('gate_w', 'gate_b', 'w1', 'b1', 'w2', 'b2')}
    del _L1_ffn_all
    return {'x': x, 'src': src, 'dst': dst, 'edge_weight': edge_weight, 'L0_gnn_W6': _L0_gnn_in['W6'], 'L0_gnn_b6': _L0_gnn_in['b6'], 'L0_gnn_W7': _L0_gnn_in['W7'], 'L0_gnn_b7': _L0_gnn_in['b7'], 'L0_gnn_Wp': _L0_gnn_in['Wp'], 'L0_gnn_bp': _L0_gnn_in['bp'], 'L0_ffn_Wr': _L0_ffn_in['Wr'], 'L0_ffn_br': _L0_ffn_in['br'], 'L0_ffn_W1': _L0_ffn_in['W1'], 'L0_ffn_b1': _L0_ffn_in['b1'], 'L0_ffn_W2': _L0_ffn_in['W2'], 'L0_ffn_b2': _L0_ffn_in['b2'], 'L0_ffn_gamma': _L0_ffn_in['gamma'], 'L0_ffn_beta': _L0_ffn_in['beta'], 'L1_gnn_W1': _L1_gnn_in['W1'], 'L1_gnn_b1': _L1_gnn_in['b1'], 'L1_gnn_W2': _L1_gnn_in['W2'], 'L1_gnn_b2': _L1_gnn_in['b2'], 'L1_ffn_gate_w': _L1_ffn_in['gate_w'], 'L1_ffn_gate_b': _L1_ffn_in['gate_b'], 'L1_ffn_w1': _L1_ffn_in['w1'], 'L1_ffn_b1': _L1_ffn_in['b1'], 'L1_ffn_w2': _L1_ffn_in['w2'], 'L1_ffn_b2': _L1_ffn_in['b2']}

def reference(x, src, dst, edge_weight, L0_gnn_W6, L0_gnn_b6, L0_gnn_W7, L0_gnn_b7, L0_gnn_Wp, L0_gnn_bp, L0_ffn_Wr, L0_ffn_br, L0_ffn_W1, L0_ffn_b1, L0_ffn_W2, L0_ffn_b2, L0_ffn_gamma, L0_ffn_beta, L1_gnn_W1, L1_gnn_b1, L1_gnn_W2, L1_gnn_b2, L1_ffn_gate_w, L1_ffn_gate_b, L1_ffn_w1, L1_ffn_b1, L1_ffn_w2, L1_ffn_b2):
    import jax
    import jax.numpy as jnp

    def _L0_gnn_ref(h5_all, edge_index, edge_weight, W6, b6, W7, b7, Wp, bp):
        import jax, jax.numpy as jnp
        import numpy as np
        N_NODES = 6250
        N_EDGES = 37500
        D = 256
        EPS = 1e-12

        def _gcn_layer(x, W, b, src, dst, norm, n_nodes):
            xt = x @ W
            msg = xt[src] * norm[:, None]
            agg = jax.ops.segment_sum(msg, dst, num_segments=n_nodes)
            return jax.nn.relu(agg + b)
        src, dst = (edge_index[0], edge_index[1])
        deg_out = jax.ops.segment_sum(edge_weight, src, num_segments=N_NODES)
        deg_in = jax.ops.segment_sum(edge_weight, dst, num_segments=N_NODES)
        norm = edge_weight * jax.lax.rsqrt(deg_out[src] * deg_in[dst] + EPS)
        h6 = _gcn_layer(h5_all, W6, b6, src, dst, norm, N_NODES)
        h7 = _gcn_layer(h6, W7, b7, src, dst, norm, N_NODES)
        out = h7 @ Wp + bp
        return out

    def _L0_ffn_ref(x, Wr, br, W1, b1, W2, b2, gamma, beta):
        import math
        import jax, jax.numpy as jnp
        import numpy as np
        CAPACITY_FACTOR = 1.25
        TOP_K = 2
        LN_EPS = 1e-05

        def _layer_norm(x, gamma, beta):
            mu = jnp.mean(x, axis=-1, keepdims=True)
            var = jnp.var(x, axis=-1, keepdims=True)
            return (x - mu) * jax.lax.rsqrt(var + LN_EPS) * gamma + beta
        B, S, D = x.shape
        E = Wr.shape[1]
        N = B * S
        K = TOP_K
        logits = jnp.mean(x, axis=1) @ Wr + br
        routing_weights = jax.nn.softmax(logits, axis=-1)
        capacity = float(math.ceil(N * CAPACITY_FACTOR / E))
        expected_loads = routing_weights.sum(axis=0) * (N / B)
        scale = jnp.where(expected_loads > capacity, capacity / expected_loads, 1.0)
        routing_weights = jax.nn.softmax(routing_weights * scale, axis=-1)
        rw_tok = jnp.broadcast_to(routing_weights[:, None, :], (B, S, E)).reshape(N, E)
        top_w, top_i = jax.lax.top_k(rw_tok, K)
        top_w = jax.nn.softmax(top_w, axis=-1)
        xf = x.reshape(N, D)
        h = jax.nn.gelu(jnp.einsum('nd,edf->enf', xf, W1) + b1[:, None, :], approximate=False)
        y = jnp.einsum('enf,efd->end', h, W2) + b2[:, None, :]
        w_dense = jnp.zeros((N, E), x.dtype).at[jnp.arange(N)[:, None], top_i].add(top_w)
        out = jnp.einsum('ne,end->nd', w_dense, y).reshape(B, S, D)
        out = _layer_norm(out + x, gamma, beta)
        return out

    def _L1_gnn_ref(x, W1, b1, W2, b2, edge_index):
        import jax, jax.numpy as jnp
        import numpy as np
        N = 1250
        E = 37500
        D = 256
        n = x.shape[0]
        loops = jnp.arange(n, dtype=edge_index.dtype)
        src = jnp.concatenate([edge_index[0], loops])
        dst = jnp.concatenate([edge_index[1], loops])
        deg = jax.ops.segment_sum(jnp.ones(src.shape[0], x.dtype), dst, num_segments=n)
        dinv = jnp.where(deg > 0, jax.lax.rsqrt(jnp.maximum(deg, 1e-12)), 0.0)
        norm = dinv[src] * dinv[dst]

        def gcn_conv(h, W, b):
            m = (h @ W)[src] * norm[:, None]
            return jax.ops.segment_sum(m, dst, num_segments=n) + b
        x1 = gcn_conv(x, W1, b1)
        x1 = x1 / jnp.maximum(jnp.linalg.norm(x1, axis=-1, keepdims=True), 1e-12)
        x2 = gcn_conv(x1, W2, b2)
        return x2 + x

    def _L1_ffn_ref(h, gate_w, gate_b, w1, b1, w2, b2):
        import math
        import jax, jax.numpy as jnp
        import numpy as np
        CAPACITY_FACTOR = 1.25
        B, L, D = h.shape
        E = gate_w.shape[1]
        T = B * L
        C = max(1, math.ceil(CAPACITY_FACTOR * T / E))
        x = h.reshape(T, D)
        logits = x @ gate_w + gate_b
        probs = jax.nn.softmax(logits, axis=-1)
        idx = jnp.argmax(probs, axis=-1)
        prb = jnp.take_along_axis(probs, idx[:, None], axis=1)[:, 0]
        one_hot = jax.nn.one_hot(idx, E, dtype=jnp.float32)
        pos = (jnp.cumsum(one_hot, axis=0) * one_hot).sum(-1).astype(jnp.int32) - 1
        kept = pos < C
        pos_safe = jnp.where(kept, pos, C)
        buf = jnp.zeros((E, C, D), dtype=h.dtype).at[idx, pos_safe].set(x, mode='drop')
        hmid = jax.nn.relu(jnp.einsum('ecd,edf->ecf', buf, w1) + b1[:, None, :])
        ybuf = jnp.einsum('ecf,efd->ecd', hmid, w2) + b2[:, None, :]
        pos_g = jnp.minimum(pos, C - 1)
        y_tok = ybuf[idx, pos_g] * (prb * kept)[:, None]
        y = y_tok.reshape(B, L, D)
        y = jnp.nan_to_num(y, nan=0.0, posinf=10000.0, neginf=-10000.0)
        return y
    edge_index = jnp.stack([src, dst])
    x = x + _L0_gnn_ref(_layernorm(x, axis=-1), edge_index, edge_weight, L0_gnn_W6, L0_gnn_b6, L0_gnn_W7, L0_gnn_b7, L0_gnn_Wp, L0_gnn_bp)
    x = x + _L0_ffn_ref(_layernorm(x, axis=-1)[None], L0_ffn_Wr, L0_ffn_br, L0_ffn_W1, L0_ffn_b1, L0_ffn_W2, L0_ffn_b2, L0_ffn_gamma, L0_ffn_beta)[0]
    x = x + _L1_gnn_ref(_layernorm(x, axis=-1), L1_gnn_W1, L1_gnn_b1, L1_gnn_W2, L1_gnn_b2, edge_index)
    x = x + _L1_ffn_ref(_layernorm(x, axis=-1)[None], L1_ffn_gate_w, L1_ffn_gate_b, L1_ffn_w1, L1_ffn_b1, L1_ffn_w2, L1_ffn_b2)[0]
    return x

_drawn_inputs = setup_inputs


def setup_inputs(seed=0):
    import zlib

    import numpy as np

    out = dict(_drawn_inputs(seed))
    spreads = {'L0_gnn_b6': (0.0, 0.1),
     'L0_gnn_b7': (0.0, 0.1),
     'L0_gnn_bp': (0.0, 0.1),
     'L0_ffn_br': (0.0, 0.1),
     'L0_ffn_b1': (0.0, 0.349),
     'L0_ffn_b2': (0.0, 0.1),
     'L0_ffn_gamma': (1.0, 0.2),
     'L0_ffn_beta': (0.0, 0.1),
     'L1_gnn_b1': (0.0, 0.8),
     'L1_gnn_b2': (0.0, 0.1),
     'L1_ffn_gate_b': (0.0, 0.33),
     'L1_ffn_b1': (0.0, 0.8),
     'L1_ffn_b2': (0.0, 0.8)}
    factors = {'L1_gnn_W1': 7.181, 'L1_gnn_W2': 6.131}
    for name, (base, spread) in spreads.items():
        noise = np.random.default_rng([zlib.crc32(name.encode()), seed]).standard_normal(out[name].shape)
        drawn = base * np.exp(spread * noise) if base else spread * noise
        out[name] = jnp.asarray(drawn.astype(out[name].dtype))
    for name, factor in factors.items():
        out[name] = (out[name] * factor).astype(out[name].dtype)
    return out
```

```python
import concourse.bass as bass
from concourse import mybir
from contextlib import ExitStack

N = 6250
D = 256
NE = 106250
P = 128
NT = -(-N // P)
NP = NT * P
LAST = N - (NT - 1) * P
U = 7
NI = NT // U
KC = D // P
ROW1 = D + 4
G = 16
NB = -(-NE // (P * P))
NC = -(-(-(-NE // P)) // G) * G
GI = NC // G
Q = 4
BK = 4
MS = 4
EC = NB * P
E0, F0 = 8, 512
E1, F1 = 8, 1024
FC0, FC1 = F0 // P, F1 // P
CAP = -(-(5 * N) // (4 * E1))
RB = -(-CAP // P)
LASTR = CAP - (RB - 1) * P
HALF = (CAP + 1) // 2
DUMP = E1 * CAP
CLEAR = -(-DUMP // (16 * P))
GT = U * P
EPS_LN = 1e-5
EPS_DEG = 1e-12


class Count:

    def __init__(self, sem, base=0):
        self.sem, self.base, self.k, self.i, self.per = sem, base, 0, None, 0

    def tell(self, ins, n=1):
        ins.then_inc(self.sem, n)
        self.k += n
        return ins

    def now(self, back=0):
        v = self.base + self.k - back
        return v if self.i is None else v + self.per * self.i

    def enter(self, i, per):
        self.base += self.k
        self.k, self.i, self.per = 0, i, per

    def check(self):
        assert self.k == self.per, (self.k, self.per)

    def leave(self, trips):
        self.base += self.per * trips
        self.k, self.i = 0, None


def gnn_ffn(nc, x, src, dst, edge_weight, W6, b6, W7, b7, Wp, bp, Wr, br, W1a, b1a, W2a, b2a, gamma, beta,
            G1, g1, G2, g2, gate_w, gate_b, w1, b1, w2, b2, out):
    f32, i32, u32, i16, u8 = (mybir.dt.float32, mybir.dt.int32, mybir.dt.uint32, mybir.dt.int16, mybir.dt.uint8)
    ALU, ACT, AX, ENG = mybir.AluOpType, mybir.ActivationFunctionType, mybir.AxisListType, mybir.EngineType

    def ts(t, w):
        return bass.ds(t * w, w)

    def a_tile(t):
        return t.with_bounds(min_val=0, max_val=NT - 1)

    tab1 = nc.dram_tensor("tab1", [NP, ROW1], f32).ap()
    tab2 = nc.dram_tensor("tab2", [NP, D], f32).ap()
    tab3 = nc.dram_tensor("tab3", [NP, D], f32).ap()
    tab4 = nc.dram_tensor("tab4", [NP, D], f32).ap()
    slots_x = nc.dram_tensor("slots_x", [DUMP + NP, D], f32).ap()
    slots_y = nc.dram_tensor("slots_y", [DUMP, D], f32).ap()
    meta_d = nc.dram_tensor("meta_d", [2, EC], i32).ap()
    tab1_v = tab1.rearrange("(t p) d -> p t d", p=P)

    ctx = ExitStack()
    with ctx:
        def sb(name, shape, dt=f32):
            return ctx.enter_context(nc.sbuf_tensor(name, shape, dt))

        def sem(name):
            return ctx.enter_context(nc.semaphore(name))

        X = sb("X", [P, NT * D])
        ACC = sb("ACC", [P, NT * D])
        WORK = sb("WORK", [P, 14336])
        SRC = sb("SRC", [P, EC], i32)
        DST = sb("DST", [P, EC])
        EW = sb("EW", [P, EC])
        NRM = sb("NRM", [P, EC])
        XIN = sb("XIN", [P, U * D])
        XT = sb("XT", [P, U * D])
        WA = sb("WA", [P, KC * D])
        WB = sb("WB", [P, KC * D])
        WC = sb("WC", [P, KC * D])
        BA = sb("BA", [P, D])
        BB = sb("BB", [P, D])
        BC = sb("BC", [P, D])
        GAM = sb("GAM", [P, D])
        BET = sb("BET", [P, D])
        IDN = sb("IDN", [P, P])
        ONE = sb("ONE", [P, P])
        TRI = sb("TRI", [P, P])
        META = sb("META", [1, 2 * EC], i32)
        VALID = sb("VALID", [P, NT])
        MV = sb("MV", [P, NT * 2])
        RS = sb("RS", [P, NT])
        SD = sb("SD", [P, NT])
        DEGI = sb("DEGI", [P, NT])
        DINV = sb("DINV", [P, NT])
        DOX = sb("DOX", [P, NT * 4])
        ST7 = sb("ST7", [P, U * 6])
        MV7 = sb("MV7", [P, U * 2])
        R7 = sb("R7", [P, U])
        NR7 = sb("NR7", [P, U])
        SSQ = sb("SSQ", [P, NT])
        NRV = sb("NRV", [P, NT])
        IDX = sb("IDX", [P, G], i32)
        IDS = sb("IDS", [P, NT], i32)
        IDY = sb("IDY", [P, NT], i32)
        NTM = sb("NTM", [P, 2 * MS])
        EPSL = sb("EPSL", [P, 1])
        EPSD = sb("EPSD", [P, 1])
        ZERO = sb("ZERO", [P, 1])
        SM = sb("SM", [1, 128])
        EXI = sb("EXI", [1, 4], i32)
        WAB = sb("WAB", [P, 2])
        MNT = sb("MNT", [P, KC])
        WRS = sb("WRS", [P, KC * E0])
        GWS = sb("GWS", [P, KC * E1])
        CNT = sb("CNT", [P, NT])
        GBS = sb("GBS", [P, E1])
        B1S = sb("B1S", [P, 2 * FC0])
        B1L = sb("B1L", [P, E1 * FC1])

        PS = [ctx.enter_context(nc.psum_tensor(f"PS{b}", [P, 512], f32)) for b in range(8)]

        def slot_t(u):
            return PS[u % BK][:, 0:D]

        def slot_o(u):
            return PS[BK + u % BK][:, 0:D]

        def gap(u):
            return BK if u >= BK else U - last_use(u) + u

        def last_use(u):
            return max(v for v in range(U) if v % BK == u % BK)

        at = [0]

        def carve(n):
            at[0] += n
            return ACC[:, at[0] - n:at[0]]
        E_SRC, E_DST = carve(EC).bitcast(i32), carve(EC).bitcast(i32)
        E_W, E_SF, E_DF = carve(EC), carve(EC), carve(EC)
        S_HI, S_LO, D_HI, D_LO = carve(EC), carve(EC), carve(EC), carve(EC)
        T_I = carve(EC).bitcast(i32)
        HS = 4
        SLO, DLO = carve(HS * P), carve(HS * P)
        SHW, DHW = carve(HS * NT), carve(HS * 2 * NT)
        assert at[0] <= NT * D
        ROWS = [WORK[:, j * ROW1:(j + 1) * ROW1] for j in range(G)]
        DIB = WORK[:, G * ROW1:G * ROW1 + NP]
        IOTA = WORK[:, G * ROW1 + NP:G * ROW1 + NP + NP // 2].bitcast(i16)
        ZB = WORK[:, 13568:13568 + D]
        ROWDG = [WORK[:, 2048:2560], WORK[:, 2560:3072]]
        MM = XIN[:, 0:MS * P]
        RC = XIN[:, MS * P:2 * MS * P]
        SQ = XT[:, 0:MS * P]
        M0 = XT[:, MS * P:2 * MS * P]
        SQX = XT[:, 2 * MS * P:(2 * MS + 1) * P]
        TT = WORK[:, 0:U * D]
        TU = WORK[:, U * D:2 * U * D]
        W1S = WORK[:, 0:2 * KC * F0]
        W2S = WORK[:, 2048:2048 + 2 * FC0 * D]
        XT0 = WORK[:, 4096:4096 + KC * GT]
        H0 = WORK[:, 5888:5888 + 2 * FC0 * GT]
        B2P = ACC[:, 0:2 * D]
        YT = ACC[:, 512:512 + U * D]
        YN = ACC[:, 2560:2560 + U * D]
        H1 = WORK[:, 0:FC1 * CAP]
        XT1 = WORK[:, 7824:7824 + KC * CAP]
        YS = WORK[:, 9780:9780 + 2 * RB * D]
        W1L = ACC[:, 0:2 * KC * F1]
        W2L = ACC[:, 4096:4096 + 2 * FC1 * D]
        RBF = ACC[:, 8192:8192 + 2 * RB * D]
        B2L = [GAM, BET]
        YV = WORK[:, 0:U * D]
        YC = WORK[:, U * D:2 * U * D]
        YE = WORK[:, 2 * U * D:3 * U * D]
        YM = WORK[:, 3 * U * D:4 * U * D].bitcast(i32)
        NX = NT * E1
        LG, TA, OH, CU, TO, PA, PB_, E8, E8I = (WORK[:, k * NX:(k + 1) * NX] for k in range(9))
        MX, SE, PRB, IXF, POS, KEP, SLT, DMP, NIDI, NID = (WORK[:, 9 * NX + k * 64:9 * NX + k * 64 + NT]
                                                          for k in range(10))
        SCL = NRM[:, 0:NT]

        s_pad, s_const = sem("pads_set"), sem("constants_ready")
        s_x, s_e, s_w, s_par = sem("x_loaded"), sem("edges_loaded"), sem("weights_loaded"), sem("parameters_loaded")
        s_ef, s_et, s_es = sem("edges_as_floats"), sem("edges_transposed"), sem("edge_columns_ready")
        s_meta, s_metad, s_metal = sem("chunk_tiles_ready"), sem("chunk_tiles_stored"), sem("chunk_tiles_loaded")
        s_hot, s_hist, s_histd = sem("onehots_ready"), sem("onehots_used"), sem("histograms_done")
        s_deg, s_cnt, s_root = sem("degrees_ready"), sem("counts_ready"), sem("count_roots_ready")
        s_diag, s_dib, s_dibd = sem("diagonals_ready"), sem("degree_rows_summed"), sem("degree_rows_ready")
        s_dost, s_accz, s_zf = sem("degree_column_stored"), sem("sums_cleared"), sem("slots_cleared")
        s_var, s_std = sem("variances_ready"), sem("deviations_ready")
        s_xin, s_xtp, s_xt = sem("tile_in"), sem("tile_transposed"), sem("transposed_tile_copied")
        s_mm, s_od, s_stg = sem("product_ready"), sem("product_taken"), sem("tile_stored")
        s_st = [sem(f"store_{u}") for u in range(U)]
        s_free, s_tick = sem("rows_used"), sem("pool_ticks")
        s_row = [sem(f"rows_gathered_{j}") for j in range(G)]
        s_idx = [sem(f"indices_staged_{q}") for q in range(G // Q)]
        s_m, s_me = sem("selection_ready"), sem("selection_more")
        s_p, s_pe = sem("sums_ready"), sem("sums_more")
        s_q, s_qe = sem("root_ready"), sem("root_more")
        s_xr, s_xn = sem("reciprocal_more"), sem("norm_more")
        s_mean, s_rl, s_e1, s_x1 = sem("mean_ready"), sem("route_logits"), sem("exp_input"), sem("exp_done")
        s_ex, s_wab, s_wabp = sem("experts_chosen"), sem("expert_weights_row"), sem("expert_weights_spread")
        s_fw, s_fws = sem("chosen_experts_loaded"), sem("chosen_experts_scaled")
        s_up, s_hid = sem("up_product"), sem("hidden_ready")
        s_v7, s_d7 = sem("variances_of_7"), sem("deviations_of_7")
        s_w2, s_io, s_sq, s_nr = sem("second_weights_loaded"), sem("iota_ready"), sem("squares_ready"), sem("norms_ready")
        s_gate, s_glog = sem("gate_read"), sem("gate_logits_ready")
        s_b1 = sem("second_biases_loaded")
        s_wfree, s_nid = sem("work_free"), sem("numbers_ready")
        s_ei, s_eo = sem("gate_exp_input"), sem("gate_exp_done")
        s_oh, s_cum, s_ix = sem("choices_ready"), sem("positions_summed"), sem("slots_known")
        s_sc = [sem(f"scattered_{u}") for u in range(U)]
        s_lw = [sem(f"expert_loaded_{k}") for k in range(2)]
        s_1t, s_1x, s_1u = sem("rows_transposed"), sem("rows_copied"), sem("up1_product")
        s_1h, s_1d, s_1y = sem("hidden1_ready"), sem("down1_product"), sem("y_staged")
        s_ys = [sem(f"y_stored_{k}") for k in range(2)]
        s_yg = [sem(f"y_gathered_{u}") for u in range(U)]
        s_yu, s_fin, s_out = sem("y_used"), sem("tile_final"), sem("out_stored")
        s_vtick = sem("vector_ticks")
        s_dv = sem("vector_steps")
        dve = Count(s_dv)

        block = ctx.enter_context(nc.Block())

        T1, T2, T3, RT, FA, T4, T5, SG, SX = range(9)
        seq_in = {k: NT * n for n, k in enumerate([T1, T2, T3, RT, FA, T4, T5, SG])}
        seq_xt = {k: NT * n for n, k in enumerate([T1, T2, T3, FA, T4, T5, SG])}
        seq_mm = {k: NT * n for n, k in enumerate([T1, T2, T3, FA, T4, T5])}
        seq_st = {k: NT * n for n, k in enumerate([T1, T2, T4, T5])}
        NU = 2 * FC0 * 2
        NU1 = FC1 * 2
        PARTS = ((0, RB - 1, P), (RB - 1, RB, LASTR))
        ND = -(-NT // 4)

        def per_tile(v, width):
            return v.rearrange("p (t a) -> p t a", a=1).to_broadcast([P, NT, width])

        def by_expert(v):
            return v.rearrange("p (t e) -> p t e", e=E1)

        def by_block(v):
            return v.rearrange("p (c n) -> p c n", c=KC)

        @block.sync
        def _(sp):
            full = NT - 1
            sp.wait_ge(s_pad, 4)
            nb, blk = NE // (P * P), P * P
            rest = NE - nb * blk
            rr, tail = rest // P, rest % P
            for sb_t, dr in ((E_SRC, src), (E_DST, dst), (E_W, edge_weight)):
                sp.dma_start(sb_t[:, 0:nb * P].rearrange("p (k j) -> p k j", j=P),
                             dr[0:nb * blk].rearrange("(k p j) -> p k j", p=P, j=P)).then_inc(s_e, 16)
                sp.dma_start(sb_t[0:rr, nb * P:nb * P + P],
                             dr[nb * blk:nb * blk + rr * P].rearrange("(p j) -> p j", j=P)).then_inc(s_e, 16)
                sp.dma_start(sb_t[rr:rr + 1, nb * P:nb * P + tail],
                             dr[nb * blk + rr * P:NE].rearrange("(p j) -> p j", p=1)).then_inc(s_e, 16)
            sp.dma_start(X[:, 0:full * D].rearrange("p (t d) -> p t d", d=D),
                         x[0:full * P, :].rearrange("(t p) d -> p t d", p=P)).then_inc(s_x, 16)
            sp.dma_start(X[0:LAST, full * D:NT * D], x[full * P:N, :]).then_inc(s_x, 16)
            for sb_t, dr in ((WA, W6), (WB, W7), (WC, Wp)):
                sp.dma_start(sb_t[:, :].rearrange("p (k d) -> p k d", k=KC),
                             dr.rearrange("(k p) d -> p k d", p=P)).then_inc(s_w, 16)
            for sb_t, dr in ((BA, b6), (BB, b7), (BC, bp), (GAM, gamma), (BET, beta)):
                sp.dma_start(sb_t[:, :], dr.rearrange("(a d) -> a d", a=1).to_broadcast([P, D])).then_inc(s_par, 16)
            sp.dma_start(GBS[:, :], gate_b.rearrange("(a d) -> a d", a=1).to_broadcast([P, E1])).then_inc(s_par, 16)
            sp.dma_start(WRS[:, :].rearrange("p (k e) -> p k e", k=KC),
                         Wr.rearrange("(k p) e -> p k e", p=P)).then_inc(s_par, 16)
            sp.dma_start(GWS[:, :].rearrange("p (k e) -> p k e", k=KC),
                         gate_w.rearrange("(k p) e -> p k e", p=P)).then_inc(s_par, 16)
            sp.dma_start(SM[0:1, 8:8 + E0], br.rearrange("(a e) -> a e", a=1)).then_inc(s_par, 16)

            sp.wait_ge(s_meta, 1)
            with nc.allow_non_contiguous_dma(reason="2 x 896 elements, once"):
                for k in range(2):
                    sp.dma_start(meta_d[k:k + 1, :].rearrange("a (k p) -> p (a k)", p=P),
                                 T_I[:, k * NB:(k + 1) * NB]).then_inc(s_metad, 16)
            sp.wait_ge(s_metad, 32)
            sp.dma_start(META[0:1, :].rearrange("a (r c) -> a r c", r=2),
                         meta_d.rearrange("(a r) c -> a r c", a=1)).then_inc(s_metal, 16)

            sp.sem_inc(s_stg, U)

            def store_table(k, tab, source):
                n, m = seq_mm[k], seq_st[k] // U
                with sp.Fori(0, NI) as i:
                    for u in range(U):
                        sp.wait_ge(s_od, U + n + U * i + u + 1)
                        sp.dma_start(tab[bass.ds((U * i + u) * P, P), 0:D], source(i, u)).then_inc(s_st[u], 16)
                    for u in range(U):
                        sp.wait_ge(s_st[u], 16 * (m + i + 1))
                        sp.sem_inc(s_stg, 1)

            def staged(i, u):
                return TT[:, u * D:(u + 1) * D]

            def in_acc(i, u):
                return ACC[:, ts(U * i + u, D)]

            def stage_indices(layer):
                n = NC * layer
                with sp.Fori(0, GI) as i:
                    for q in range(G // Q):
                        sp.wait_ge(s_free, n + G * i + Q * (q + 1))
                        sp.dma_start(IDX[:, q * Q:(q + 1) * Q], SRC[:, bass.ds(G * i + q * Q, Q)])\
                            .then_inc(s_idx[q], 16)

            store_table(T1, tab1, staged)
            sp.wait_ge(s_deg, 1)
            sp.dma_start(tab1_v[:, :, D:ROW1], DOX[:, :].rearrange("p (t c) -> p t c", c=4)).then_inc(s_dost, 16)
            sp.wait_ge(s_const, 11)
            for k in range(CLEAR):
                sp.dma_start(slots_x[k * 16 * P:(k + 1) * 16 * P, :].rearrange("(t p) d -> p t d", p=P),
                             ZB.rearrange("p (a d) -> p a d", a=1).to_broadcast([P, 16, D])).then_inc(s_zf, 16)
            with nc.allow_non_contiguous_dma(reason="8192 elements, once"):
                for e in range(E1):
                    sp.dma_start(B1L[:, e * FC1:(e + 1) * FC1], b1[e].rearrange("(f p) -> p f", p=P))\
                        .then_inc(s_b1, 16)
            stage_indices(0)
            store_table(T2, tab2, staged)
            stage_indices(1)

            sp.wait_ge(s_ex, 1)
            _, chosen = nc.values_load_multi_w_load_instructions(
                EXI[0:1, 0:2], engines=(ENG.SP,), min_val=0, max_val=E0 - 1,
                skip_runtime_bounds_check_because="an argmax over the experts")
            for k, e in enumerate(chosen):
                sp.dma_start(W1S[:, k * KC * F0:(k + 1) * KC * F0].rearrange("p (k f) -> p k f", k=KC),
                             W1a[bass.ds(e, 1), :, :].rearrange("e (k p) f -> p (e k) f", p=P)).then_inc(s_fw, 16)
                sp.dma_start(W2S[:, k * FC0 * D:(k + 1) * FC0 * D].rearrange("p (k f) -> p k f", k=FC0),
                             W2a[bass.ds(e, 1), :, :].rearrange("e (k p) f -> p (e k) f", p=P)).then_inc(s_fw, 16)
                sp.dma_start(B2P[:, k * D:(k + 1) * D], b2a[bass.ds(e, 1), :].to_broadcast([P, D])).then_inc(s_fw, 16)
                with nc.allow_non_contiguous_dma(reason="512 elements, once"):
                    sp.dma_start(B1S[:, k * FC0:(k + 1) * FC0],
                                 b1a[bass.ds(e, 1), :].rearrange("e (f p) -> p (e f)", p=P)).then_inc(s_fw, 16)
            for sb_t, dr in ((WA, G1), (WB, G2)):
                sp.dma_start(sb_t[:, :].rearrange("p (k d) -> p k d", k=KC),
                             dr.rearrange("(k p) d -> p k d", p=P)).then_inc(s_w2, 16)
            for sb_t, dr in ((BA, g1), (BB, g2)):
                sp.dma_start(sb_t[:, :], dr.rearrange("(a d) -> a d", a=1).to_broadcast([P, D])).then_inc(s_w2, 16)

            store_table(T4, tab3, in_acc)
            stage_indices(2)
            store_table(T5, tab4, in_acc)
            stage_indices(3)

            def store_y(e):
                k = e % 2
                sp.wait_ge(s_1y, RB * (e + 1))
                for r0, r1, rows in PARTS:
                    sp.dma_start(slots_y[e * CAP + r0 * P:e * CAP + (r1 - 1) * P + rows, :]
                                 .rearrange("(r p) d -> p r d", p=rows),
                                 YS[0:rows, (k * RB + r0) * D:(k * RB + r1) * D].rearrange("p (r d) -> p r d", d=D))\
                        .then_inc(s_ys[k], 16)

            for u in range(U):
                sp.wait_ge(s_sc[u], 16 * NI)
            for e in range(E1):
                k = e % 2
                if e >= 2:
                    store_y(e - 2)
                for r0, r1, rows in PARTS:
                    sp.dma_start(RBF[0:rows, (k * RB + r0) * D:(k * RB + r1) * D].rearrange("p (r d) -> p r d", d=D),
                                 slots_x[e * CAP + r0 * P:e * CAP + (r1 - 1) * P + rows, :]
                                 .rearrange("(r p) d -> p r d", p=rows)).then_inc(s_lw[k], 16)
                sp.dma_start(W1L[:, k * KC * F1:(k + 1) * KC * F1].rearrange("p (k f) -> p k f", k=KC),
                             w1[e].rearrange("(k p) f -> p k f", p=P)).then_inc(s_lw[k], 16)
                sp.dma_start(W2L[:, k * FC1 * D:(k + 1) * FC1 * D].rearrange("p (k f) -> p k f", k=FC1),
                             w2[e].rearrange("(k p) f -> p k f", p=P)).then_inc(s_lw[k], 16)
                sp.dma_start(B2L[k][:, :], b2[e:e + 1, :].to_broadcast([P, D])).then_inc(s_lw[k], 16)
            store_y(E1 - 2)
            store_y(E1 - 1)

            for t in range(NT):
                sp.wait_ge(s_fin, t + 1)
                rows = P if t < NT - 1 else LAST
                sp.dma_start(out[t * P:t * P + rows, :], X[0:rows, t * D:(t + 1) * D]).then_inc(s_out, 16)
            sp.wait_ge(s_out, 16 * NT)

        @block.gpsimd
        def _(po):
            for tile, value in ((IDN, 0.0), (ONE, 1.0), (EPSL, EPS_LN), (EPSD, EPS_DEG), (ZERO, 0.0), (VALID, 1.0)):
                po.memset(tile[:, :], value).then_inc(s_const, 1)
            po.memset(ZB, 0.0).then_inc(s_const, 1)
            po.iota(IOTA, pattern=[[1, NP]], base=0, channel_multiplier=0).then_inc(s_const, 1)
            po.wait_ge(s_const, 8)
            po.affine_select(out=IDN[:, :], in_=IDN[:, :], compare_op=ALU.not_equal, fill=1.0, base=0,
                             pattern=[[-1, P]], channel_multiplier=1).then_inc(s_const, 1)
            po.affine_select(out=TRI[:, :], in_=ONE[:, :], compare_op=ALU.is_ge, fill=0.0, base=0,
                             pattern=[[1, P]], channel_multiplier=-1).then_inc(s_const, 1)
            po.affine_select(out=VALID[:, NT - 1:NT], in_=VALID[:, NT - 1:NT], compare_op=ALU.is_ge, fill=0.0,
                             base=LAST - 1, pattern=[[0, 1]], channel_multiplier=-1).then_inc(s_const, 1)

            def hold(semaphore, value):
                po.wait_ge(semaphore, value)
                po.sem_inc(s_tick, 1)

            def gather_edges(layer, tab, width):
                n = NC * layer
                with po.Fori(0, GI) as i:
                    for j in range(G):
                        if j % Q == 0:
                            hold(s_idx[j // Q], 16 * (GI * layer + i + 1))
                        hold(s_free, n + G * i + j + 1)
                        po.indirect_dma_start(
                            out=ROWS[j][:, 0:width], out_offset=None, in_=tab[:, :],
                            in_offset=bass.IndirectOffsetOnAxis(ap=IDX[:, j:j + 1].bitcast(u32), axis=0))\
                            .then_inc(s_row[j], 16)

            def table_stored(k):
                po.wait_ge(s_stg, U + seq_st[k] + NT)

            po.wait_ge(s_histd, 1)
            po.memset(ACC[:, :], 0.0).then_inc(s_accz, 1)
            table_stored(T1)
            po.wait_ge(s_dost, 16)
            po.wait_ge(s_dibd, ND)
            gather_edges(0, tab1, ROW1)
            po.wait_ge(s_xin, seq_in[T2] + NT)
            po.memset(ACC[:, :], 0.0).then_inc(s_accz, 1)
            table_stored(T2)
            gather_edges(1, tab2, D)
            po.wait_ge(s_od, U + seq_mm[FA] + NT)
            po.iota(IOTA, pattern=[[1, NP]], base=0, channel_multiplier=0).then_inc(s_io, 1)
            table_stored(T4)
            gather_edges(2, tab3, D)
            table_stored(T5)
            gather_edges(3, tab4, D)

            po.wait_ge(s_wfree, 1)
            po.iota(NIDI.bitcast(i32), pattern=[[P, NT]], base=0, channel_multiplier=1).then_inc(s_nid, 1)
            po.iota(E8I.bitcast(i32), pattern=[[0, NT], [1, E1]], base=0, channel_multiplier=0).then_inc(s_nid, 1)

            po.wait_ge(s_zf, 16 * CLEAR)
            for t in range(NT):
                po.wait_ge(s_xin, seq_in[SG] + NT + t + 1)
                po.indirect_dma_start(
                    out=slots_x[:, :], out_offset=bass.IndirectOffsetOnAxis(ap=IDS[:, t:t + 1].bitcast(u32), axis=0),
                    in_=XIN[:, (t % U) * D:(t % U + 1) * D], in_offset=None).then_inc(s_sc[t % U], 16)

            for k in range(2):
                po.wait_ge(s_ys[k], 16 * 2 * (E1 // 2))
            for t in range(NT):
                if t >= U:
                    po.wait_ge(s_yu, t - U + 1)
                po.indirect_dma_start(
                    out=XIN[:, (t % U) * D:(t % U + 1) * D], out_offset=None, in_=slots_y[:, :],
                    in_offset=bass.IndirectOffsetOnAxis(ap=IDY[:, t:t + 1].bitcast(u32), axis=0))\
                    .then_inc(s_yg[t % U], 16)

        @block.tensor
        def _(pe):
            pe.wait_ge(s_const, 11)
            pe.wait_ge(s_e, 144)
            pe.wait_ge(s_ef, 2)
            for a, blk in enumerate((E_SF, E_DF, E_W)):
                for k in range(NB):
                    last = pe.transpose(PS[2 * a + k // 4][:, (k % 4) * P:(k % 4 + 1) * P], blk[:, k * P:(k + 1) * P],
                                        IDN[:, :])
                last.then_inc(s_et, 1)

            pe.sem_inc(s_xtp, U)
            pe.sem_inc(s_mm, U)

            def transpose_tile(k, i, u):
                n, m = seq_in[k] + U * i + u, seq_xt[k] + U * i + u
                pe.wait_ge(s_xin, n + 1)
                pe.wait_ge(s_xt, U + m + 1 - gap(u))
                for c in range(KC):
                    last = pe.transpose(slot_t(u)[:, c * P:(c + 1) * P], XIN[:, u * D + c * P:u * D + (c + 1) * P],
                                        IDN[:, :])
                last.then_inc(s_xtp, 1)

            def dense_pass(k, w):
                with pe.Fori(0, NI) as i:
                    for u in range(U):
                        transpose_tile(k, i, u)
                    for u in range(U):
                        pe.wait_ge(s_xt, U + seq_xt[k] + U * i + u + 1)
                        pe.wait_ge(s_od, U + seq_mm[k] + U * i + u + 1 - gap(u))
                        for c in range(KC):
                            last = pe.matmul(slot_o(u), XT[:, u * D + c * P:u * D + (c + 1) * P],
                                             w[:, c * D:(c + 1) * D], start=(c == 0), stop=(c == KC - 1))
                        last.then_inc(s_mm, 1)
                pe.wait_ge(s_xt, U + seq_xt[k] + NT)

            pe.wait_ge(s_es, 1)
            pe.wait_ge(s_w, 48)
            dense_pass(T1, WA)

            HSRC, HDST = PS[0][:, 0:NT], PS[1][:, 0:2 * NT]
            pe.matmul(HSRC, ZB[:, 0:P], ZB[:, 0:NT], start=True, stop=False)
            pe.matmul(HDST, ZB[:, 0:P], ZB[:, 0:2 * NT], start=True, stop=False)
            pe.sem_inc(s_hist, HS)
            with pe.Fori(0, NC // HS) as i:
                for j in range(HS):
                    pe.wait_ge(s_hot, HS * i + j + 1)
                    pe.matmul(HSRC, SLO[:, j * P:(j + 1) * P], SHW[:, j * NT:(j + 1) * NT], start=False, stop=False)
                    pe.matmul(HDST, DLO[:, j * P:(j + 1) * P], DHW[:, j * 2 * NT:(j + 1) * 2 * NT],
                              start=False, stop=False).then_inc(s_hist, 1)
            pe.matmul(HSRC, ZB[:, 0:P], ZB[:, 0:NT], start=False, stop=True)
            pe.matmul(HDST, ZB[:, 0:P], ZB[:, 0:2 * NT], start=False, stop=True).then_inc(s_histd, 1)

            for g in range(ND):
                w = P * min(4, NT - 4 * g)
                pe.wait_ge(s_diag, g + 1)
                if g >= 2:
                    pe.wait_ge(s_dibd, g - 1)
                pe.matmul(PS[2 + g % 2][:, 0:w], ONE[:, :], ROWDG[g % 2][:, 0:w], start=True, stop=True)\
                    .then_inc(s_dib, 1)

            more = pe.alloc_register("more_sums")
            pe.reg_mov(more, 2)
            pe.sem_inc(s_pe, 1)

            def sum_edges(layer):
                n = NC * layer
                with pe.Fori(0, GI) as i:
                    for j in range(G):
                        if j % 8 == 0:
                            _, extra = nc.values_load_multi_w_load_instructions(
                                META[0:1, bass.ds(EC + G * i + j, 8)], engines=(ENG.PE,), min_val=0, max_val=NT,
                                skip_runtime_bounds_check_because="a count of node tiles")
                        m = j % MS
                        pe.wait_ge(s_row[j], 16 * (GI * layer + i + 1))
                        pe.wait_ge(s_m, MS + n + G * i + j + 1)
                        pe.matmul(PS[m][:, 0:D], MM[:, m * P:(m + 1) * P], ROWS[j][:, 0:D], start=True, stop=True)\
                            .then_inc(s_p, 1)
                        with pe.If(extra[j % 8] > 0):
                            with pe.Fori(0, extra[j % 8]):
                                pe.wait_ge(s_me, pe.snap(more))
                                pe.matmul(PS[m][:, 0:D], MM[:, m * P:(m + 1) * P], ROWS[j][:, 0:D],
                                          start=True, stop=True).then_inc(s_pe, 1)
                                pe.reg_add(more, more, 1)
                            pe.nop()

            pe.wait_ge(s_metal, 16)
            sum_edges(0)
            dense_pass(T2, WB)
            sum_edges(1)
            dense_pass(T3, WC)

            with pe.Fori(0, NI) as i:
                for u in range(U):
                    pe.wait_ge(s_xin, seq_in[RT] + U * i + u + 1)
                    for c in range(KC):
                        last = pe.matmul(PS[0][:, bass.ds(c * 64 + U * i + u, 1)],
                                         XIN[:, u * D + c * P:u * D + (c + 1) * P],
                                         VALID[:, bass.ds(U * i + u, 1)], start=True, stop=True)
                    last.then_inc(s_xtp, 1)
            pe.wait_ge(s_par, 144)
            pe.wait_ge(s_mean, 1)
            for c in range(KC):
                last = pe.matmul(PS[1][0:1, 0:E0], MNT[:, c:c + 1], WRS[:, c * E0:(c + 1) * E0],
                                 start=(c == 0), stop=(c == KC - 1))
            last.then_inc(s_rl, 1)
            pe.wait_ge(s_wab, 1)
            pe.matmul(PS[2][:, 0:2], ONE[0:1, :], SM[0:1, 120:122], start=True, stop=True).then_inc(s_wabp, 1)

            pe.wait_ge(s_fws, 1)
            pe.sem_inc(s_hid, NU)
            with pe.Fori(0, NI) as i:
                pe.wait_ge(s_hid, NU * i + NU)
                for u in range(U):
                    transpose_tile(FA, i, u)
                pe.wait_ge(s_xt, U + seq_xt[FA] + U * i + U)
                for q in range(NU):
                    fe, hf = q // 2, q % 2
                    if q >= 4:
                        pe.wait_ge(s_hid, NU * i + NU + q - 3)
                    for c in range(KC):
                        w = ((fe // FC0) * KC + c) * F0 + (fe % FC0) * P
                        last = pe.matmul(PS[q % 4][:, 0:GT // 2], W1S[:, w:w + P],
                                         XT0[:, c * GT + hf * (GT // 2):c * GT + (hf + 1) * (GT // 2)],
                                         start=(c == 0), stop=(c == KC - 1))
                    last.then_inc(s_up, 1)
                pe.wait_ge(s_hid, NU * i + 2 * NU)
                for u in range(U):
                    pe.wait_ge(s_od, U + seq_mm[FA] + U * i + u + 1 - gap(u))
                    for fe in range(2 * FC0):
                        last = pe.matmul(slot_o(u), H0[:, fe * GT + u * P:fe * GT + (u + 1) * P],
                                         W2S[:, fe * D:(fe + 1) * D], start=(fe == 0), stop=(fe == 2 * FC0 - 1))
                    last.then_inc(s_mm, 1)

            pe.wait_ge(s_w2, 64)
            dense_pass(T4, WA)
            sum_edges(2)
            dense_pass(T5, WB)
            sum_edges(3)

            pe.wait_ge(s_free, G + 4 * NC)
            pe.sem_inc(s_gate, U)
            with pe.Fori(0, NI) as i:
                for u in range(U):
                    transpose_tile(SG, i, u)
                for u in range(U):
                    pe.wait_ge(s_xt, U + seq_xt[SG] + U * i + u + 1)
                    for c in range(KC):
                        last = pe.matmul(PS[4][:, bass.ds((U * i + u) * E1, E1)],
                                         XT[:, u * D + c * P:u * D + (c + 1) * P],
                                         GWS[:, c * E1:(c + 1) * E1], start=(c == 0), stop=(c == KC - 1))
                    last.then_inc(s_gate, 1)
            pe.wait_ge(s_oh, 1)
            pe.matmul(PS[5][:, 0:NX], TRI[:, :], OH, start=True, stop=True)
            pe.matmul(PS[6][:, 0:NX], ONE[:, :], OH, start=True, stop=True).then_inc(s_cum, 1)

            for e in range(E1):
                k = e % 2
                pe.wait_ge(s_lw[k], 80 * (e // 2 + 1))
                if e:
                    pe.wait_ge(s_1h, NU1 * e)
                for r in range(RB):
                    rows = min(P, CAP - r * P)
                    if r >= BK:
                        pe.wait_ge(s_1x, RB * e + r - BK + 1)
                    for c in range(KC):
                        last = pe.transpose(PS[r % BK][:, c * P:c * P + rows],
                                            RBF[0:rows, (k * RB + r) * D + c * P:(k * RB + r) * D + (c + 1) * P],
                                            IDN[0:rows, 0:rows])
                    last.then_inc(s_1t, 1)
                pe.wait_ge(s_1x, RB * (e + 1))
                for q in range(NU1):
                    f, h0, hn = q // 2, (q % 2) * HALF, (HALF, CAP - HALF)[q % 2]
                    if q >= 4:
                        pe.wait_ge(s_1h, NU1 * e + q - 3)
                    for c in range(KC):
                        w = (k * KC + c) * F1 + f * P
                        last = pe.matmul(PS[q % 4][:, 0:hn], W1L[:, w:w + P],
                                         XT1[:, c * CAP + h0:c * CAP + h0 + hn],
                                         start=(c == 0), stop=(c == KC - 1))
                    last.then_inc(s_1u, 1)
                pe.wait_ge(s_1h, NU1 * (e + 1))
                for r in range(RB):
                    rows = min(P, CAP - r * P)
                    if e or r >= BK:
                        pe.wait_ge(s_1y, RB * e + r - BK + 1)
                    for f in range(FC1):
                        last = pe.matmul(PS[BK + r % BK][0:rows, 0:D],
                                         H1[:, f * CAP + r * P:f * CAP + r * P + rows],
                                         W2L[:, (k * FC1 + f) * D:(k * FC1 + f + 1) * D],
                                         start=(f == 0), stop=(f == FC1 - 1))
                    last.then_inc(s_1d, 1)

        @block.scalar
        def _(ac):
            ac.sem_inc(s_xt, U)

            def deviation(n):
                ac.wait_ge(s_var, n)
                ac.activation(SD[:, :].rearrange("p (t a) -> p t a", a=1),
                              MV[:, :].rearrange("p (t c) -> p t c", c=2)[:, :, 1:2],
                              ACT.Sqrt, bias=EPSL[:, :]).then_inc(s_std, 1)

            def copy_transposed(k, i, func, into):
                for u in range(U):
                    ac.wait_ge(s_xtp, U + seq_in[k] + U * i + u + 1)
                    if k in (T1, T2, T3, T4, T5):
                        ac.wait_ge(s_mm, seq_mm[k] + U * i + u + 1)
                    if k == SG:
                        ac.wait_ge(s_gate, U * i + u + 1)
                    ac.activation(into(u), by_block(slot_t(u)), func).then_inc(s_xt, 1)

            def to_slot(u):
                return by_block(XT[:, u * D:(u + 1) * D])

            def stage_products(k, i):
                for u in range(U):
                    ac.wait_ge(s_mm, U + seq_mm[k] + U * i + u + 1)
                    ac.wait_ge(s_stg, seq_st[k] + U * i + u + 1)
                    ac.activation(TT[:, u * D:(u + 1) * D], slot_o(u), ACT.Copy).then_inc(s_od, 1)

            ac.sem_inc(s_od, U)
            ac.wait_ge(s_const, 11)
            deviation(1)
            with ac.Fori(0, NI) as i:
                copy_transposed(T1, i, ACT.Copy, to_slot)
                stage_products(T1, i)

            ac.wait_ge(s_cnt, 1)
            ac.activation(DINV[:, :], CNT[:, :], ACT.Sqrt).then_inc(s_root, 1)
            for g in range(ND):
                w = P * min(4, NT - 4 * g)
                ac.wait_ge(s_dib, g + 1)
                ac.activation(DIB[:, g * 4 * P:g * 4 * P + w], PS[2 + g % 2][:, 0:w], ACT.Copy).then_inc(s_dibd, 1)

            ac.wait_ge(s_metal, 16)
            ac.wait_ge(s_dibd, ND)
            more = ac.alloc_register("more_roots")
            ac.reg_mov(more, 1)
            with ac.Fori(0, GI) as i:
                for j in range(G):
                    if j % 8 == 0:
                        _, first = nc.values_load_multi_w_load_instructions(
                            META[0:1, bass.ds(G * i + j, 8)], engines=(ENG.Activation,), min_val=0, max_val=NT - 1,
                            skip_runtime_bounds_check_because="a node tile")
                        _, extra = nc.values_load_multi_w_load_instructions(
                            META[0:1, bass.ds(EC + G * i + j, 8)], engines=(ENG.Activation,), min_val=0, max_val=NT,
                            skip_runtime_bounds_check_because="a count of node tiles")
                    m = j % MS
                    root = SQ[:, m * P:(m + 1) * P]
                    ac.wait_ge(s_row[j], 16 * (i + 1))
                    ac.wait_ge(s_m, G * i + j + 1)
                    ac.activation(root, DIB[:, ts(first[j % 8], P)], ACT.Sqrt,
                                  bias=EPSD[:, :], scale=ROWS[j][:, D:D + 1]).then_inc(s_q, 1)
                    with ac.If(extra[j % 8] > 0):
                        with ac.Fori(0, extra[j % 8]) as k:
                            ac.wait_ge(s_me, ac.snap(more))
                            ac.activation(SQX, DIB[:, ts(a_tile(first[j % 8] + k + 1), P)], ACT.Sqrt,
                                          bias=EPSD[:, :], scale=ROWS[j][:, D:D + 1]).then_inc(s_qe, 1)
                            ac.reg_add(more, more, 1)
                        ac.nop()

            with ac.Fori(0, NI) as i:
                copy_transposed(T2, i, ACT.Relu, to_slot)
                stage_products(T2, i)
            with ac.Fori(0, NI) as i:
                copy_transposed(T3, i, ACT.Relu, to_slot)
            deviation(2)

            ac.wait_ge(s_e1, 1)
            ac.activation(SM[0:1, 24:32], SM[0:1, 16:24], ACT.Exp, bias=SM[0:1, 1:2]).then_inc(s_x1, 1)
            ac.wait_ge(s_e1, 2)
            ac.activation(SM[0:1, 48:56], SM[0:1, 40:48], ACT.Exp, bias=SM[0:1, 3:4]).then_inc(s_x1, 1)
            ac.wait_ge(s_e1, 3)
            ac.activation(SM[0:1, 113:114], SM[0:1, 112:113], ACT.Exp).then_inc(s_x1, 1)

            def to_block(u):
                return by_block(XT0)[:, :, u * P:(u + 1) * P]

            def gelus(i):
                for q in range(NU):
                    fe, hf = q // 2, q % 2
                    ac.wait_ge(s_up, NU * i + q + 1)
                    ac.activation(H0[:, fe * GT + hf * (GT // 2):fe * GT + (hf + 1) * (GT // 2)],
                                  PS[q % 4][:, 0:GT // 2], ACT.Gelu, bias=B1S[:, fe:fe + 1]).then_inc(s_hid, 1)

            def deviation_of_7(n):
                ac.wait_ge(s_v7, n)
                ac.activation(NR7[:, :].rearrange("p (u a) -> p u a", a=1),
                              MV7[:, :].rearrange("p (u c) -> p u c", c=2)[:, :, 1:2],
                              ACT.Sqrt, bias=EPSL[:, :]).then_inc(s_d7, 1)

            ac.wait_ge(s_fw, 128)
            copy_transposed(FA, 0, ACT.Copy, to_block)
            gelus(0)
            with ac.Fori(1, NI) as i:
                copy_transposed(FA, i, ACT.Copy, to_block)
                gelus(i)
                deviation_of_7(i)
            deviation_of_7(NI)
            deviation(3)

            with ac.Fori(0, NI) as i:
                copy_transposed(T4, i, ACT.Copy, to_slot)
            with ac.Fori(0, NI) as i:
                copy_transposed(T5, i, ACT.Copy, to_slot)
                ac.wait_ge(s_sq, i + 1)
                ac.activation(NRV[:, ts(i, U)], SSQ[:, ts(i, U)], ACT.Sqrt).then_inc(s_nr, 1)
            deviation(4)
            with ac.Fori(0, NI) as i:
                copy_transposed(SG, i, ACT.Copy, to_slot)
            ac.wait_ge(s_ei, 1)
            ac.activation(TA, TA, ACT.Exp).then_inc(s_eo, 1)

            for e in range(E1):
                for r in range(RB):
                    ac.wait_ge(s_1t, RB * e + r + 1)
                    if e and r == 0:
                        ac.wait_ge(s_1u, NU1 * e)
                    rows = min(P, CAP - r * P)
                    ac.activation(by_block(XT1)[:, :, r * P:r * P + rows],
                                  by_block(PS[r % BK][:, 0:D])[:, :, 0:rows], ACT.Copy)\
                        .then_inc(s_1x, 1)
                if e:
                    ac.wait_ge(s_1d, RB * e)
                else:
                    ac.wait_ge(s_b1, 16 * E1)
                for q in range(NU1):
                    f, h0, hn = q // 2, (q % 2) * HALF, (HALF, CAP - HALF)[q % 2]
                    ac.wait_ge(s_1u, NU1 * e + q + 1)
                    ac.activation(H1[:, f * CAP + h0:f * CAP + h0 + hn],
                                  PS[q % 4][:, 0:hn], ACT.Relu, bias=B1L[:, e * FC1 + f:e * FC1 + f + 1])\
                        .then_inc(s_1h, 1)

        @block.vector
        def _(ve):
            def settle():
                ve.wait_ge(s_dv, dve.now())

            def hold(semaphore, value):
                ve.wait_ge(semaphore, value)
                ve.sem_inc(s_vtick, 1)

            step = dve.tell

            def loop(start, trips, per, body):
                with ve.Fori(start, trips) as i:
                    dve.enter(i - start if start else i, per)
                    body(i)
                    dve.check()
                dve.leave(trips - start)

            def tile(v, i, u):
                return v[:, ts(U * i + u, D)]

            def slot(v, u):
                return v[:, u * D:(u + 1) * D]

            def normalized(into, i, u):
                t = U * i + u
                return ve.tensor_scalar(into, tile(X, i, u), MV[:, bass.ds(2 * t, 1)], RS[:, bass.ds(t, 1)],
                                        ALU.subtract, ALU.mult)

            def moments(i):
                hold(s_dv, dve.now())
                for u in range(U):
                    last = ve.bn_stats(ST7[:, u * 6:(u + 1) * 6], tile(X, i, u))
                step(last)
                hold(s_dv, dve.now())
                for u in range(U):
                    last = ve.bn_aggr(MV7[:, 2 * u:2 * u + 2], ST7[:, u * 6:(u + 1) * 6])
                step(last)
                settle()
                step(ve.tensor_copy(MV[:, ts(i, 2 * U)], MV7[:, :]))

            def reciprocal_deviation(n):
                settle()
                ve.sem_inc(s_var, 1)
                ve.wait_ge(s_std, n)
                step(ve.reciprocal(RS[:, :], SD[:, :]))
                settle()

            def feed(k, i, make):
                for u in range(U):
                    ve.wait_ge(s_xtp, seq_in[k] + U * i + u + 1)
                    make(slot(XIN, u), i, u).then_inc(s_xin, 1)

            def feed_normalized(k, i):
                feed(k, i, normalized)

            def fed(k, i, consume):
                with_next = i is not None
                return with_next

            ve.memset(X[:, (NT - 1) * D:NT * D], 0.0).then_inc(s_pad, 1)
            ve.memset(E_SRC[:, (NB - 1) * P:NB * P], 0).then_inc(s_pad, 1)
            ve.memset(E_DST[:, (NB - 1) * P:NB * P], NP - 1).then_inc(s_pad, 1)
            ve.memset(E_W[:, (NB - 1) * P:NB * P], 0.0).then_inc(s_pad, 1)
            step(ve.memset(NRM[:, :], 0.0))
            step(ve.memset(DOX[:, :], 0.0))
            ve.sem_inc(s_free, G)
            ve.sem_inc(s_m, MS)
            ve.sem_inc(s_me, 1)
            ve.sem_inc(s_xn, 1)

            ve.wait_ge(s_e, 144)
            ve.tensor_copy(E_SF, E_SRC).then_inc(s_ef, 1)
            ve.tensor_copy(E_DF, E_DST).then_inc(s_ef, 1)
            ve.wait_ge(s_ef, 2)
            df3 = E_DF.rearrange("p (k j) -> p k j", j=P)
            ve.tensor_reduce(S_HI[:, 0:NB], df3, AX.X, ALU.min)
            step(ve.tensor_reduce(S_HI[:, NB:2 * NB], df3, AX.X, ALU.max))
            settle()
            step(ve.tensor_copy(D_HI[:, 0:2 * NB].bitcast(i32), S_HI[:, 0:2 * NB]))
            settle()
            step(ve.tensor_scalar(T_I[:, 0:2 * NB], D_HI[:, 0:2 * NB].bitcast(i32), 7, None, ALU.arith_shift_right))
            settle()
            ve.tensor_tensor(T_I[:, NB:2 * NB], T_I[:, NB:2 * NB], T_I[:, 0:NB], ALU.subtract).then_inc(s_meta, 1)

            for a, (into, n) in enumerate(((SRC, 1), (DST, 2), (EW, 3))):
                ve.wait_ge(s_et, n)
                ve.tensor_copy(into[:, 0:4 * P], PS[2 * a][:, :])
                last = ve.tensor_copy(into[:, 4 * P:NB * P], PS[2 * a + 1][:, 0:(NB - 4) * P])
            last.then_inc(s_es, 1)
            ve.wait_ge(s_es, 1)
            DSI = S_HI.bitcast(i32)
            ve.wait_ge(s_metad, 32)
            step(ve.tensor_scalar(T_I, SRC[:, :], 7, None, ALU.arith_shift_right))
            settle()
            step(ve.tensor_copy(S_HI, T_I))
            settle()
            step(ve.tensor_scalar(T_I, SRC[:, :], P - 1, None, ALU.bitwise_and))
            settle()
            step(ve.tensor_copy(S_LO, T_I))
            step(ve.tensor_copy(E_SRC, DST[:, :]))
            settle()
            step(ve.tensor_scalar(T_I, E_SRC, 7, None, ALU.arith_shift_right))
            settle()
            step(ve.tensor_copy(D_HI, T_I))
            settle()
            step(ve.tensor_scalar(T_I, E_SRC, P - 1, None, ALU.bitwise_and))
            settle()
            step(ve.tensor_copy(D_LO, T_I))

            ve.wait_ge(s_x, 32)
            settle()
            loop(0, NI, 3, moments)
            ve.wait_ge(s_const, 11)
            reciprocal_deviation(1)
            loop(0, NI, 0, lambda i: feed_normalized(T1, i))

            def onehots(i):
                for j in range(HS):
                    c = bass.ds(HS * i + j, 1)
                    ve.wait_ge(s_hist, HS * i + j + 1)
                    ve.tensor_scalar(SLO[:, j * P:(j + 1) * P], IOTA[:, 0:P], S_LO[:, c], None, ALU.is_equal)
                    ve.tensor_scalar(SHW[:, j * NT:(j + 1) * NT], IOTA[:, 0:NT], S_HI[:, c], EW[:, c],
                                     ALU.is_equal, ALU.mult)
                    ve.tensor_scalar(DLO[:, j * P:(j + 1) * P], IOTA[:, 0:P], D_LO[:, c], None, ALU.is_equal)
                    w = 2 * NT * j
                    ve.tensor_scalar(DHW[:, w:w + NT], IOTA[:, 0:NT], D_HI[:, c], EW[:, c], ALU.is_equal, ALU.mult)
                    ve.tensor_scalar(DHW[:, w + NT:w + 2 * NT], IOTA[:, 0:NT], D_HI[:, c], None, ALU.is_equal)\
                        .then_inc(s_hot, 1)

            loop(0, NC // HS, 0, onehots)
            ve.wait_ge(s_histd, 1)
            ve.tensor_copy(DOX[:, :].rearrange("p (t c) -> p t c", c=4)[:, :, 0:1],
                           PS[0][:, 0:NT].rearrange("p (t a) -> p t a", a=1))
            step(ve.tensor_copy(DEGI[:, :], PS[1][:, 0:NT]))
            settle()
            ve.sem_inc(s_deg, 1)
            ve.tensor_scalar(CNT[:, :], PS[1][:, NT:2 * NT], 1.0, 1e-12, ALU.add, ALU.max).then_inc(s_cnt, 1)
            ve.wait_ge(s_stg, U + seq_st[T1] + NT)
            for g in range(ND):
                tiles = min(4, NT - 4 * g)
                if g >= 2:
                    ve.wait_ge(s_dib, g - 1)
                ve.tensor_tensor(
                    ROWDG[g % 2][:, 0:tiles * P].rearrange("p (t n) -> p t n", n=P),
                    IDN[:, :].rearrange("p (a n) -> p a n", a=1).to_broadcast([P, tiles, P]),
                    DEGI[:, 4 * g:4 * g + tiles].rearrange("p (t a) -> p t a", a=1).to_broadcast([P, tiles, P]),
                    ALU.mult).then_inc(s_diag, 1)
            ve.wait_ge(s_root, 1)
            step(ve.reciprocal(DINV[:, :], DINV[:, :]))

            z = ve.alloc_register("more_selections")
            ve.reg_mov(z, 1)

            def sum_edges(layer, scalar2, roots):
                n = NC * layer

                def chunks(i):
                    def select(m, c, t, signal, root_count, reciprocal_count):
                        where = slot_p(MM, m)
                        if not roots:
                            if scalar2 is None:
                                ins = ve.tensor_scalar(where, IOTA[:, ts(t, P)], DST[:, c], None, ALU.is_equal)
                            else:
                                ins = ve.tensor_scalar(where, IOTA[:, ts(t, P)], DST[:, c], scalar2[:, c],
                                                       ALU.is_equal, ALU.mult)
                            ins.then_inc(signal, 1)
                            return
                        ve.tensor_scalar(slot_p(M0, m), IOTA[:, ts(t, P)], DST[:, c], EW[:, c],
                                         ALU.is_equal, ALU.mult)
                        ve.wait_ge(*root_count)
                        recip = ve.reciprocal(slot_p(RC, m), slot_p(SQ, m) if signal is s_m else SQX)
                        if signal is s_m:
                            step(recip)
                            settle()
                        else:
                            recip.then_inc(s_xr, 1)
                            ve.wait_ge(*reciprocal_count)
                        col = m if signal is s_m else MS + m
                        ve.scalar_tensor_tensor(where, slot_p(M0, m), 1.0, slot_p(RC, m), ALU.mult, ALU.mult,
                                                accum_out=NTM[:, col:col + 1]).then_inc(signal, 1)

                    def collect(j, first, extra):
                        m, c = j % MS, bass.ds(G * i + j, 1)
                        count = n + G * i + j
                        if roots:
                            ve.wait_ge(s_m, MS + count + 1)
                            step(ve.tensor_tensor(NRM[:, c], NRM[:, c], NTM[:, m:m + 1], ALU.add))
                        with ve.If(extra > 0):
                            if roots:
                                hold(s_dv, dve.now())
                            with ve.Fori(0, extra) as k:
                                so_far = ve.snap(z)
                                ve.wait_ge(s_p, count + 1)
                                ve.wait_ge(s_free, G + count)
                                ve.wait_ge(s_pe, so_far)
                                a = ACC[:, ts(a_tile(first + k), D)]
                                ve.tensor_tensor(a, a, PS[m][:, 0:D], ALU.add)
                                select(m, c, a_tile(first + k + 1), s_me, (s_qe, so_far), (s_xr, so_far))
                                if roots:
                                    ve.wait_ge(s_me, so_far + 1)
                                    ve.wait_ge(s_xn, so_far)
                                    ve.tensor_tensor(NRM[:, c], NRM[:, c], NTM[:, MS + m:MS + m + 1], ALU.add)\
                                        .then_inc(s_xn, 1)
                                ve.reg_add(z, z, 1)
                            if roots:
                                hold(s_xn, ve.snap(z))
                            hold(s_pe, ve.snap(z))
                        a = ACC[:, ts(a_tile(first + extra), D)]
                        ve.wait_ge(s_p, count + 1)
                        ve.wait_ge(s_free, G + count)
                        ve.tensor_tensor(a, a, PS[m][:, 0:D], ALU.add).then_inc(s_free, 1)

                    before = None
                    for j in range(G):
                        if j % 8 == 0:
                            _, firsts = nc.values_load_multi_w_load_instructions(
                                META[0:1, bass.ds(G * i + j, 8)], engines=(ENG.DVE,), min_val=0, max_val=NT - 1,
                                skip_runtime_bounds_check_because="a node tile")
                            _, extras = nc.values_load_multi_w_load_instructions(
                                META[0:1, bass.ds(EC + G * i + j, 8)], engines=(ENG.DVE,), min_val=0, max_val=NT,
                                skip_runtime_bounds_check_because="a count of node tiles")
                        select(j % MS, bass.ds(G * i + j, 1), firsts[j % 8], s_m, (s_q, G * i + j + 1), None)
                        if before is not None:
                            collect(*before)
                        before = (j, firsts[j % 8], extras[j % 8])
                        if j % 8 == 7:
                            collect(*before)
                            before = None

                loop(0, GI, 2 * G if roots else 0, chunks)

            def slot_p(v, m):
                return v[:, m * P:(m + 1) * P]

            ve.wait_ge(s_metal, 16)
            ve.wait_ge(s_accz, 1)
            ve.wait_ge(s_xtp, U + seq_in[T1] + NT)
            sum_edges(0, None, True)
            ve.wait_ge(s_free, G + NC)

            ve.wait_ge(s_par, 144)

            def plus(bias):
                return lambda into, i, u: ve.tensor_tensor(into, tile(ACC, i, u), bias[:, :], ALU.add)

            loop(0, NI, 0, lambda i: feed(T2, i, plus(BA)))
            ve.wait_ge(s_accz, 2)
            ve.wait_ge(s_xtp, U + seq_in[T2] + NT)
            sum_edges(1, NRM, False)
            ve.wait_ge(s_free, G + 2 * NC)

            def ahead(k, make, take, per):
                feed(k, 0, make)

                def body(i):
                    feed(k, i + 1, make)
                    take(i)
                loop(0, NI - 1, per, body)
                take(NI - 1)

            def take_t3(i):
                for u in range(U):
                    ve.wait_ge(s_mm, U + seq_mm[T3] + U * i + u + 1)
                    ve.tensor_tensor(slot(TT, u), slot_o(u), BC[:, :], ALU.add).then_inc(s_od, 1)
                for u in range(U):
                    ve.wait_ge(s_od, U + seq_mm[T3] + U * i + u + 1)
                    last = ve.tensor_tensor(tile(X, i, u), tile(X, i, u), slot(TT, u), ALU.add)
                step(last)
                moments(i)

            ahead(T3, plus(BB), take_t3, 4)
            reciprocal_deviation(2)

            loop(0, NI, 0, lambda i: feed_normalized(RT, i))
            ve.wait_ge(s_xtp, U + seq_in[RT] + NT)
            step(ve.tensor_reduce(MNT[:, :], PS[0][:, 0:2 * 64].rearrange("p (c t) -> p c t", c=KC)[:, :, 0:NT],
                                  AX.X, ALU.add))
            settle()
            ve.tensor_scalar(MNT[:, :], MNT[:, :], 1.0 / N, None, ALU.mult).then_inc(s_mean, 1)

            def row(a, w=1):
                return SM[0:1, a:a + w]

            def softmax(logits, exps, probs, top, neg, total, turn):
                step(ve.tensor_reduce(row(top), logits, AX.X, ALU.max))
                settle()
                ve.tensor_scalar(row(neg), row(top), -1.0, None, ALU.mult).then_inc(s_e1, 1)
                ve.wait_ge(s_x1, turn)
                step(ve.tensor_reduce(row(total), exps, AX.X, ALU.add))
                settle()
                step(ve.reciprocal(row(total), row(total)))
                settle()
                step(ve.tensor_scalar(probs, exps, row(total), None, ALU.mult))
                settle()

            ve.wait_ge(s_rl, 1)
            step(ve.tensor_tensor(row(16, E0), PS[1][0:1, 0:E0], row(8, E0), ALU.add))
            settle()
            softmax(row(16, E0), row(24, E0), row(32, E0), 0, 1, 4, 1)
            step(ve.tensor_scalar(row(56, E0), row(32, E0), float(N), 1e-30, ALU.mult, ALU.max))
            settle()
            step(ve.reciprocal(row(64, E0), row(56, E0)))
            settle()
            step(ve.tensor_scalar(row(72, E0), row(64, E0), float(CAP), 1.0, ALU.mult, ALU.min))
            settle()
            step(ve.tensor_tensor(row(40, E0), row(32, E0), row(72, E0), ALU.mult))
            settle()
            softmax(row(40, E0), row(48, E0), row(80, E0), 2, 3, 5, 2)
            step(ve.tensor_scalar(row(96, E0), IOTA[0:1, 0:E0], -1.0, float(E0), ALU.mult, ALU.add))
            for k in range(2):
                step(ve.tensor_reduce(row(110 + k), row(80, E0), AX.X, ALU.max))
                settle()
                step(ve.scalar_tensor_tensor(row(88, E0), row(80, E0), row(110 + k), row(96, E0),
                                             ALU.is_equal, ALU.mult))
                settle()
                step(ve.tensor_reduce(row(114 + k), row(88, E0), AX.X, ALU.max))
                settle()
                step(ve.tensor_scalar(row(116 + k), row(114 + k), -1.0, float(E0), ALU.mult, ALU.add))
                step(ve.tensor_scalar(row(88, E0), row(96, E0), row(114 + k), -2.0, ALU.is_equal, ALU.mult))
                settle()
                step(ve.tensor_tensor(row(80, E0), row(80, E0), row(88, E0), ALU.add))
                settle()
            ve.tensor_copy(EXI[0:1, 0:2], row(116, 2)).then_inc(s_ex, 1)
            ve.tensor_tensor(row(112), row(111), row(110), ALU.subtract).then_inc(s_e1, 1)
            ve.wait_ge(s_x1, 3)
            step(ve.tensor_scalar(row(118), row(113), 1.0, None, ALU.add))
            settle()
            step(ve.reciprocal(row(120), row(118)))
            settle()
            ve.tensor_tensor(row(121), row(120), row(113), ALU.mult).then_inc(s_wab, 1)
            ve.wait_ge(s_wabp, 1)
            step(ve.tensor_copy(WAB[:, :], PS[2][:, 0:2]))
            settle()
            ve.wait_ge(s_fw, 128)
            for k in range(2):
                w2s = W2S[:, k * FC0 * D:(k + 1) * FC0 * D]
                ve.tensor_scalar(w2s, w2s, WAB[:, k:k + 1], None, ALU.mult)
            step(ve.tensor_scalar(BC[:, :], B2P[:, 0:D], WAB[:, 0:1], None, ALU.mult))
            settle()
            ve.scalar_tensor_tensor(BC[:, :], B2P[:, D:2 * D], WAB[:, 1:2], BC[:, :], ALU.mult, ALU.add)\
                .then_inc(s_fws, 1)
            ve.wait_ge(s_fws, 1)

            def take_ffn(i):
                for u in range(U):
                    ve.wait_ge(s_mm, U + seq_mm[FA] + U * i + u + 1)
                    ve.tensor_tensor(slot(YT, u), slot_o(u), BC[:, :], ALU.add).then_inc(s_od, 1)
                    last = normalized(slot(YN, u), i, u)
                step(last)
                settle()
                for u in range(U):
                    last = ve.tensor_tensor(slot(YT, u), slot(YT, u), slot(YN, u), ALU.add)
                step(last)
                hold(s_dv, dve.now())
                for u in range(U):
                    last = ve.bn_stats(ST7[:, u * 6:(u + 1) * 6], slot(YT, u))
                step(last)
                hold(s_dv, dve.now())
                for u in range(U):
                    last = ve.bn_aggr(MV7[:, 2 * u:2 * u + 2], ST7[:, u * 6:(u + 1) * 6])
                last.then_inc(s_v7, 1)
                ve.wait_ge(s_v7, i + 1)
                ve.wait_ge(s_d7, i + 1)
                step(ve.reciprocal(R7[:, :], NR7[:, :]))
                settle()
                for u in range(U):
                    last = ve.tensor_scalar(slot(YT, u), slot(YT, u), MV7[:, 2 * u:2 * u + 1], R7[:, u:u + 1],
                                            ALU.subtract, ALU.mult)
                step(last)
                settle()
                for other, op in ((GAM, ALU.mult), (BET, ALU.add)):
                    for u in range(U):
                        last = ve.tensor_tensor(slot(YT, u), slot(YT, u), other[:, :], op)
                    step(last)
                    settle()
                for u in range(U):
                    last = ve.tensor_tensor(tile(X, i, u), tile(X, i, u), slot(YT, u), ALU.add)
                step(last)
                moments(i)

            ahead(FA, normalized, take_ffn, 11)
            reciprocal_deviation(3)

            def take_t4(i):
                for u in range(U):
                    ve.wait_ge(s_mm, U + seq_mm[T4] + U * i + u + 1)
                    ve.tensor_scalar(tile(ACC, i, u), slot_o(u), DINV[:, bass.ds(U * i + u, 1)], None, ALU.mult)\
                        .then_inc(s_od, 1)

            ahead(T4, normalized, take_t4, 0)
            ve.wait_ge(s_io, 1)
            ve.wait_ge(s_stg, U + seq_st[T4] + NT)
            ve.wait_ge(s_xtp, U + seq_in[T4] + NT)
            sum_edges(2, None, False)
            ve.wait_ge(s_free, G + 3 * NC)

            def hidden(into, i, u):
                return ve.scalar_tensor_tensor(into, tile(ACC, i, u), DINV[:, bass.ds(U * i + u, 1)], BA[:, :],
                                               ALU.mult, ALU.add)

            def squares(i):
                for u in range(U):
                    ve.wait_ge(s_xin, seq_in[T5] + U * i + u + 1)
                    last = ve.scalar_tensor_tensor(slot(TT, u), slot(XIN, u), 1.0, slot(XIN, u), ALU.mult, ALU.mult,
                                                   accum_out=SSQ[:, bass.ds(U * i + u, 1)])
                last.then_inc(s_sq, 1)

            def take_t5(i):
                ve.wait_ge(s_nr, i + 1)
                nr = NRV[:, ts(i, U)]
                step(ve.tensor_scalar(nr, nr, 1e-12, None, ALU.max))
                hold(s_dv, dve.now())
                step(ve.reciprocal(nr, nr))
                settle()
                step(ve.tensor_tensor(nr, nr, DINV[:, ts(i, U)], ALU.mult))
                settle()
                for u in range(U):
                    ve.wait_ge(s_mm, U + seq_mm[T5] + U * i + u + 1)
                    ve.tensor_scalar(tile(ACC, i, u), slot_o(u), NRV[:, bass.ds(U * i + u, 1)], None, ALU.mult)\
                        .then_inc(s_od, 1)

            feed(T5, 0, hidden)
            squares(0)

            def body_t5(i):
                ve.wait_ge(s_sq, i + 1)
                feed(T5, i + 1, hidden)
                squares(i + 1)
                take_t5(i)
            loop(0, NI - 1, 3, body_t5)
            take_t5(NI - 1)
            ve.wait_ge(s_stg, U + seq_st[T5] + NT)
            ve.wait_ge(s_xtp, U + seq_in[T5] + NT)
            sum_edges(3, None, False)
            ve.wait_ge(s_free, G + 4 * NC)

            def finish_gnn(i):
                for u in range(U):
                    normalized(slot(TT, u), i, u)
                    last = ve.scalar_tensor_tensor(slot(TU, u), tile(ACC, i, u), DINV[:, bass.ds(U * i + u, 1)],
                                                   BB[:, :], ALU.mult, ALU.add)
                step(last)
                settle()
                for u in range(U):
                    last = ve.tensor_tensor(slot(TT, u), slot(TT, u), slot(TU, u), ALU.add)
                step(last)
                settle()
                for u in range(U):
                    last = ve.tensor_tensor(tile(X, i, u), tile(X, i, u), slot(TT, u), ALU.add)
                step(last)
                moments(i)

            loop(0, NI, 6, finish_gnn)
            reciprocal_deviation(4)
            ve.sem_inc(s_wfree, 1)

            loop(0, NI, 0, lambda i: feed_normalized(SG, i))
            ve.wait_ge(s_nid, 2)
            step(ve.tensor_copy(NID, NIDI.bitcast(i32)))
            step(ve.tensor_copy(E8, E8I.bitcast(i32)))
            ve.wait_ge(s_gate, U + NT)
            step(ve.tensor_tensor(by_expert(LG), by_expert(PS[4][:, 0:NX]),
                                  GBS[:, :].rearrange("p (a e) -> p a e", a=1).to_broadcast([P, NT, E1]), ALU.add))
            settle()
            step(ve.tensor_reduce(MX, by_expert(LG), AX.X, ALU.max))
            settle()
            ve.tensor_tensor(by_expert(TA), by_expert(LG), per_tile(MX, E1), ALU.subtract).then_inc(s_ei, 1)
            step(ve.tensor_tensor(by_expert(OH), by_expert(LG), per_tile(MX, E1), ALU.is_equal))
            step(ve.tensor_scalar(PA, E8, -1.0, float(E1), ALU.mult, ALU.add))
            settle()
            step(ve.tensor_tensor(OH, OH, PA, ALU.mult))
            settle()
            step(ve.tensor_reduce(IXF, by_expert(OH), AX.X, ALU.max))
            settle()
            step(ve.tensor_scalar(IXF, IXF, -1.0, float(E1), ALU.mult, ALU.add))
            settle()
            step(ve.tensor_tensor(by_expert(OH), by_expert(E8), per_tile(IXF, E1), ALU.is_equal))
            settle()
            ve.tensor_tensor(by_expert(OH), by_expert(OH), per_tile(VALID[:, :], E1), ALU.mult).then_inc(s_oh, 1)
            ve.wait_ge(s_eo, 1)
            step(ve.tensor_reduce(SE, by_expert(TA), AX.X, ALU.add))
            settle()
            step(ve.reciprocal(PRB, SE))
            ve.wait_ge(s_cum, 1)
            step(ve.tensor_copy(TO, PS[6][:, 0:NX]))
            step(ve.tensor_copy(PA, PS[6][:, 0:NX]))
            settle()
            a, b, shift = PA, PB_, 1
            while shift < NT:
                w = shift * E1
                ve.tensor_copy(b[:, 0:w], a[:, 0:w])
                step(ve.tensor_tensor(b[:, w:NX], a[:, w:NX], a[:, 0:NX - w], ALU.add))
                settle()
                a, b, shift = b, a, 2 * shift
            step(ve.tensor_tensor(a, a, TO, ALU.subtract))
            settle()
            step(ve.tensor_tensor(CU, a, PS[5][:, 0:NX], ALU.add))
            settle()
            step(ve.tensor_tensor(CU, CU, OH, ALU.mult))
            settle()
            step(ve.tensor_reduce(POS, by_expert(CU), AX.X, ALU.add))
            settle()
            step(ve.tensor_scalar(KEP, POS, float(CAP), None, ALU.is_le))
            step(ve.tensor_scalar(SLT, POS, -1.0, 0.0, ALU.add, ALU.max))
            settle()
            step(ve.tensor_tensor(KEP, KEP, VALID[:, :], ALU.mult))
            step(ve.tensor_scalar(SLT, SLT, float(CAP - 1), None, ALU.min))
            settle()
            step(ve.scalar_tensor_tensor(SLT, IXF, float(CAP), SLT, ALU.mult, ALU.add))
            step(ve.tensor_scalar(DMP, NID, float(DUMP), None, ALU.add))
            settle()
            step(ve.tensor_copy(IDY[:, :], SLT))
            step(ve.tensor_tensor(SLT, SLT, DMP, ALU.subtract))
            step(ve.tensor_tensor(SCL, PRB, KEP, ALU.mult))
            settle()
            step(ve.tensor_tensor(SLT, SLT, KEP, ALU.mult))
            settle()
            step(ve.tensor_tensor(SLT, SLT, DMP, ALU.add))
            settle()
            step(ve.tensor_copy(IDS[:, :], SLT))
            settle()
            ve.sem_inc(s_ix, 1)
            for t in range(NT):
                if t >= U:
                    ve.wait_ge(s_sc[t % U], 16 * (t // U))
                normalized(slot(XIN, t % U), 0, t).then_inc(s_xin, 1)

            for e in range(E1):
                k = e % 2
                for r in range(RB):
                    rows = min(P, CAP - r * P)
                    ve.wait_ge(s_1d, RB * e + r + 1)
                    if r == 0 and e >= 2:
                        ve.wait_ge(s_ys[k], 32 * (e // 2))
                    ve.tensor_tensor(YS[0:rows, (k * RB + r) * D:(k * RB + r + 1) * D],
                                     PS[BK + r % BK][0:rows, 0:D], B2L[k][0:rows, :], ALU.add)\
                        .then_inc(s_1y, 1)

            ve.wait_ge(s_1y, RB * E1)
            for g in range(NI):
                for u in range(U):
                    t = U * g + u
                    ve.wait_ge(s_yg[u], 16 * (g + 1))
                    ve.tensor_scalar(slot(YV, u), slot(XIN, u), SCL[:, t:t + 1], None, ALU.mult).then_inc(s_yu, 1)
                ve.wait_ge(s_yu, U * (g + 1))
                for u in range(U):
                    ve.tensor_scalar(slot(YC, u), slot(YV, u), -1e4, 1e4, ALU.max, ALU.min)
                    ve.tensor_tensor(slot(YE, u), slot(YV, u), slot(YV, u), ALU.is_equal)
                    last = ve.tensor_scalar(slot(YM, u), slot(YV, u), 0.0, 0.0, ALU.mult, ALU.is_equal)
                step(last)
                settle()
                for u in range(U):
                    last = ve.tensor_tensor(slot(YC, u), slot(YC, u), slot(YE, u), ALU.mult)
                step(last)
                settle()
                for u in range(U):
                    last = ve.copy_predicated(slot(YC, u), slot(YM, u), slot(YV, u))
                step(last)
                settle()
                for u in range(U):
                    t = U * g + u
                    ve.tensor_tensor(X[:, t * D:(t + 1) * D], X[:, t * D:(t + 1) * D], slot(YC, u), ALU.add)\
                        .then_inc(s_fin, 1)


_INS = ['x', 'src', 'dst', 'edge_weight', 'L0_gnn_W6', 'L0_gnn_b6', 'L0_gnn_W7', 'L0_gnn_b7', 'L0_gnn_Wp', 'L0_gnn_bp',
        'L0_ffn_Wr', 'L0_ffn_br', 'L0_ffn_W1', 'L0_ffn_b1', 'L0_ffn_W2', 'L0_ffn_b2', 'L0_ffn_gamma', 'L0_ffn_beta',
        'L1_gnn_W1', 'L1_gnn_b1', 'L1_gnn_W2', 'L1_gnn_b2', 'L1_ffn_gate_w', 'L1_ffn_gate_b', 'L1_ffn_w1', 'L1_ffn_b1',
        'L1_ffn_w2', 'L1_ffn_b2']


def kernel(**inputs):
    import numpy as _np
    import concourse.bacc as _bacc
    from concourse import mybir as _mybir
    from concourse.bass_utils import run_bass_kernel_spmd as _run

    nc = _bacc.Bacc("TRN2", target_bir_lowering=False, num_devices=1)
    arrays, args = {}, []
    for name in _INS:
        a = _np.ascontiguousarray(inputs[name])
        arrays[f"in_{name}"] = a
        args.append(nc.dram_tensor(f"in_{name}", a.shape, _mybir.dt.from_np(a.dtype), kind="ExternalInput").ap())
    args.append(nc.dram_tensor("out_x", (N, D), _mybir.dt.float32, kind="ExternalOutput").ap())
    gnn_ffn(nc, *args)
    r = _run(nc, [arrays], core_ids=[0])
    return r.results[0]["out_x"]
```

```python
import concourse.bass as bass
from concourse import mybir
from contextlib import ExitStack

N = 6250
D = 256
NE = 106250
P = 128
NT = -(-N // P)
NP = NT * P
LAST = N - (NT - 1) * P
U = 7
NI = NT // U
KC = D // P
ROW1 = D + 4
G = 16
NB = -(-NE // (P * P))
NC = -(-(-(-NE // P)) // G) * G
GI = NC // G
Q = 4
NG = -(-NE // (P * P)) * P // Q
BK = 4
EC = NB * P
E0, F0 = 8, 512
E1, F1 = 8, 1024
FC0, FC1 = F0 // P, F1 // P
CAP = -(-(5 * N) // (4 * E1))
RB = -(-CAP // P)
LASTR = CAP - (RB - 1) * P
HALF = (CAP + 1) // 2
DUMP = E1 * CAP
CLEAR = -(-DUMP // (16 * P))
GT = U * P
EPS_LN = 1e-5
EPS_DEG = 1e-12


class Count:

    def __init__(self, sem, base=0):
        self.sem, self.base, self.k, self.i, self.per = sem, base, 0, None, 0

    def tell(self, ins, n=1):
        ins.then_inc(self.sem, n)
        self.k += n
        return ins

    def now(self, back=0):
        v = self.base + self.k - back
        return v if self.i is None else v + self.per * self.i

    def enter(self, i, per):
        self.base += self.k
        self.k, self.i, self.per = 0, i, per

    def check(self):
        assert self.k == self.per, (self.k, self.per)

    def leave(self, trips):
        self.base += self.per * trips
        self.k, self.i = 0, None


def gnn_ffn(nc, x, src, dst, edge_weight, W6, b6, W7, b7, Wp, bp, Wr, br, W1a, b1a, W2a, b2a, gamma, beta,
            G1, g1, G2, g2, gate_w, gate_b, w1, b1, w2, b2, out):
    f32, i32, u32, i16, u8 = (mybir.dt.float32, mybir.dt.int32, mybir.dt.uint32, mybir.dt.int16, mybir.dt.uint8)
    ALU, ACT, AX, ENG = mybir.AluOpType, mybir.ActivationFunctionType, mybir.AxisListType, mybir.EngineType

    def ts(t, w):
        return bass.ds(t * w, w)

    def a_tile(t):
        return t.with_bounds(min_val=0, max_val=NT - 1)

    tab1 = nc.dram_tensor("tab1", [NP, ROW1], f32).ap()
    tab2 = nc.dram_tensor("tab2", [NP, D], f32).ap()
    tab3 = nc.dram_tensor("tab3", [NP, D], f32).ap()
    tab4 = nc.dram_tensor("tab4", [NP, D], f32).ap()
    slots_x = nc.dram_tensor("slots_x", [DUMP + NP, D], f32).ap()
    slots_y = nc.dram_tensor("slots_y", [DUMP, D], f32).ap()
    meta_d = nc.dram_tensor("meta_d", [2, EC], i32).ap()
    tab1_v = tab1.rearrange("(t p) d -> p t d", p=P)

    ctx = ExitStack()
    with ctx:
        def sb(name, shape, dt=f32):
            return ctx.enter_context(nc.sbuf_tensor(name, shape, dt))

        def sem(name):
            return ctx.enter_context(nc.semaphore(name))

        X = sb("X", [P, NT * D])
        ACC = sb("ACC", [P, NT * D])
        WORK = sb("WORK", [P, 14336])
        SRC = sb("SRC", [P, EC], i32)
        DST = sb("DST", [P, EC])
        EW = sb("EW", [P, EC])
        NRM = sb("NRM", [P, EC])
        XIN = sb("XIN", [P, U * D])
        XT = sb("XT", [P, U * D])
        WA = sb("WA", [P, KC * D])
        WB = sb("WB", [P, KC * D])
        WC = sb("WC", [P, KC * D])
        BA = sb("BA", [P, D])
        BB = sb("BB", [P, D])
        BC = sb("BC", [P, D])
        GAM = sb("GAM", [P, D])
        BET = sb("BET", [P, D])
        IDN = sb("IDN", [P, P])
        ONE = sb("ONE", [P, P])
        TRI = sb("TRI", [P, P])
        FIRST = sb("FIRST", [1, NG], i32)
        SPAN = sb("SPAN", [1, NG], i32)
        VALID = sb("VALID", [P, NT])
        MV = sb("MV", [P, NT * 2])
        RS = sb("RS", [P, NT])
        SD = sb("SD", [P, NT])
        DEGI = sb("DEGI", [P, NT])
        DINV = sb("DINV", [P, NT])
        DOX = sb("DOX", [P, NT * 4])
        ST7 = sb("ST7", [P, U * 6])
        MV7 = sb("MV7", [P, U * 2])
        R7 = sb("R7", [P, U])
        NR7 = sb("NR7", [P, U])
        SSQ = sb("SSQ", [P, NT])
        NRV = sb("NRV", [P, NT])
        IDX = sb("IDX", [P, G], i32)
        IDS = sb("IDS", [P, NT], i32)
        IDY = sb("IDY", [P, NT], i32)
        DIE = sb("DIE", [P, 2 * Q])
        DIX = sb("DIX", [P, Q])
        DRT = sb("DRT", [P, 2 * Q])
        DRI = sb("DRI", [P, 2 * Q])
        EPSL = sb("EPSL", [P, 1])
        EPSD = sb("EPSD", [P, 1])
        ZERO = sb("ZERO", [P, 1])
        SM = sb("SM", [1, 128])
        EXI = sb("EXI", [1, 4], i32)
        WAB = sb("WAB", [P, 2])
        MNT = sb("MNT", [P, KC])
        WRS = sb("WRS", [P, KC * E0])
        GWS = sb("GWS", [P, KC * E1])
        CNT = sb("CNT", [P, NT])
        GBS = sb("GBS", [P, E1])
        B1S = sb("B1S", [P, 2 * FC0])
        B1L = sb("B1L", [P, E1 * FC1])

        PS = [ctx.enter_context(nc.psum_tensor(f"PS{b}", [P, 512], f32)) for b in range(8)]

        def slot_t(u):
            return PS[u % BK][:, 0:D]

        def slot_o(u):
            return PS[BK + u % BK][:, 0:D]

        def gap(u):
            return BK if u >= BK else U - last_use(u) + u

        def last_use(u):
            return max(v for v in range(U) if v % BK == u % BK)

        at = [0]

        def carve(n):
            at[0] += n
            return ACC[:, at[0] - n:at[0]]
        E_SRC, E_DST = carve(EC).bitcast(i32), carve(EC).bitcast(i32)
        E_W, E_SF, E_DF = carve(EC), carve(EC), carve(EC)
        S_HI, S_LO, D_HI, D_LO = carve(EC), carve(EC), carve(EC), carve(EC)
        T_I = carve(EC).bitcast(i32)
        HS = 4
        SLO, DLO = carve(HS * P), carve(HS * P)
        SHW, DHW = carve(HS * NT), carve(HS * 2 * NT)
        assert at[0] <= NT * D
        ROWS = [WORK[:, j * ROW1:(j + 1) * ROW1] for j in range(G)]
        DIB = WORK[:, G * ROW1:G * ROW1 + NP]
        IOTA = WORK[:, G * ROW1 + NP:G * ROW1 + NP + NP // 2].bitcast(i16)
        ZB = WORK[:, 13568:13568 + D]
        ROWDG = [WORK[:, 2048:2560], WORK[:, 2560:3072]]
        MM = XIN[:, 0:3 * Q * P]
        AGAIN = 2
        DSEL = XT[:, 0:3 * Q * P]
        META = XT[0:1, :].bitcast(i32)
        GROUP1, GROUPN = XIN[0:1, 0:NG], XIN[0:1, NG:2 * NG]
        TT = WORK[:, 0:U * D]
        TU = WORK[:, U * D:2 * U * D]
        W1S = WORK[:, 0:2 * KC * F0]
        W2S = WORK[:, 2048:2048 + 2 * FC0 * D]
        XT0 = WORK[:, 4096:4096 + KC * GT]
        H0 = WORK[:, 5888:5888 + 2 * FC0 * GT]
        B2P = ACC[:, 0:2 * D]
        YT = ACC[:, 512:512 + U * D]
        YN = ACC[:, 2560:2560 + U * D]
        H1 = WORK[:, 0:FC1 * CAP]
        XT1 = WORK[:, 7824:7824 + KC * CAP]
        YS = WORK[:, 9780:9780 + 2 * RB * D]
        W1L = ACC[:, 0:2 * KC * F1]
        W2L = ACC[:, 4096:4096 + 2 * FC1 * D]
        RBF = ACC[:, 8192:8192 + 2 * RB * D]
        B2L = [GAM, BET]
        YV = WORK[:, 0:U * D]
        YC = WORK[:, U * D:2 * U * D]
        YE = WORK[:, 2 * U * D:3 * U * D]
        YM = WORK[:, 3 * U * D:4 * U * D].bitcast(i32)
        NX = NT * E1
        LG, TA, OH, CU, TO, PA, PB_, E8, E8I = (WORK[:, k * NX:(k + 1) * NX] for k in range(9))
        MX, SE, PRB, IXF, POS, KEP, SLT, DMP, NIDI, NID = (WORK[:, 9 * NX + k * 64:9 * NX + k * 64 + NT]
                                                          for k in range(10))
        SCL = NRM[:, 0:NT]

        s_pad, s_const = sem("pads_set"), sem("constants_ready")
        s_x, s_e, s_w, s_par = sem("x_loaded"), sem("edges_loaded"), sem("weights_loaded"), sem("parameters_loaded")
        s_ef, s_et, s_es = sem("edges_as_floats"), sem("edges_transposed"), sem("edge_columns_ready")
        s_meta, s_metad, s_metal = sem("chunk_tiles_ready"), sem("chunk_tiles_stored"), sem("chunk_tiles_loaded")
        s_hot, s_hist, s_histd = sem("onehots_ready"), sem("onehots_used"), sem("histograms_done")
        s_deg, s_cnt, s_root = sem("degrees_ready"), sem("counts_ready"), sem("count_roots_ready")
        s_diag, s_dib, s_dibd = sem("diagonals_ready"), sem("degree_rows_summed"), sem("degree_rows_ready")
        s_dost, s_accz, s_zf = sem("degree_column_stored"), sem("sums_cleared"), sem("slots_cleared")
        s_var, s_std = sem("variances_ready"), sem("deviations_ready")
        s_xin, s_xtp, s_xt = sem("tile_in"), sem("tile_transposed"), sem("transposed_tile_copied")
        s_mm, s_od, s_stg = sem("product_ready"), sem("product_taken"), sem("tile_stored")
        s_st = [sem(f"store_{u}") for u in range(U)]
        s_free, s_tick = sem("rows_used"), sem("pool_ticks")
        s_row = [sem(f"rows_gathered_{j}") for j in range(G)]
        s_idx = [sem(f"indices_staged_{q}") for q in range(G // Q)]
        s_m, s_me = sem("selection_ready"), sem("selection_more")
        s_p, s_pe = sem("sums_ready"), sem("sums_more")
        s_joined, s_aj = sem("sums_joined"), sem("more_joined")
        s_span = sem("spans_ready")
        s_di, s_dr = sem("incoming_degrees_ready"), sem("degree_roots_ready")
        s_dx, s_dj = sem("more_degrees_selected"), sem("more_degrees_joined")
        s_mean, s_rl, s_e1, s_x1 = sem("mean_ready"), sem("route_logits"), sem("exp_input"), sem("exp_done")
        s_ex, s_wab, s_wabp = sem("experts_chosen"), sem("expert_weights_row"), sem("expert_weights_spread")
        s_fw, s_fws = sem("chosen_experts_loaded"), sem("chosen_experts_scaled")
        s_up, s_hid = sem("up_product"), sem("hidden_ready")
        s_v7, s_d7 = sem("variances_of_7"), sem("deviations_of_7")
        s_w2, s_io, s_sq, s_nr = sem("second_weights_loaded"), sem("iota_ready"), sem("squares_ready"), sem("norms_ready")
        s_gate, s_glog = sem("gate_read"), sem("gate_logits_ready")
        s_b1 = sem("second_biases_loaded")
        s_wfree, s_nid = sem("work_free"), sem("numbers_ready")
        s_ei, s_eo = sem("gate_exp_input"), sem("gate_exp_done")
        s_oh, s_cum, s_ix = sem("choices_ready"), sem("positions_summed"), sem("slots_known")
        s_sc = [sem(f"scattered_{u}") for u in range(U)]
        s_lw = [sem(f"expert_loaded_{k}") for k in range(2)]
        s_1t, s_1x, s_1u = sem("rows_transposed"), sem("rows_copied"), sem("up1_product")
        s_1h, s_1d, s_1y = sem("hidden1_ready"), sem("down1_product"), sem("y_staged")
        s_ys = [sem(f"y_stored_{k}") for k in range(2)]
        s_yg = [sem(f"y_gathered_{u}") for u in range(U)]
        s_yu, s_fin, s_out = sem("y_used"), sem("tile_final"), sem("out_stored")
        s_vtick = sem("vector_ticks")
        s_dv = sem("vector_steps")
        dve = Count(s_dv)

        block = ctx.enter_context(nc.Block())

        T1, T2, T3, RT, FA, T4, T5, SG, SX = range(9)
        seq_in = {k: NT * n for n, k in enumerate([T1, T2, T3, RT, FA, T4, T5, SG])}
        seq_xt = {k: NT * n for n, k in enumerate([T1, T2, T3, FA, T4, T5, SG])}
        seq_mm = {k: NT * n for n, k in enumerate([T1, T2, T3, FA, T4, T5])}
        seq_st = {k: NT * n for n, k in enumerate([T1, T2, T4, T5])}
        NU = 2 * FC0 * 2
        NU1 = FC1 * 2
        PARTS = ((0, RB - 1, P), (RB - 1, RB, LASTR))
        ND = -(-NT // 4)

        def per_tile(v, width):
            return v.rearrange("p (t a) -> p t a", a=1).to_broadcast([P, NT, width])

        def by_expert(v):
            return v.rearrange("p (t e) -> p t e", e=E1)

        def by_block(v):
            return v.rearrange("p (c n) -> p c n", c=KC)

        @block.sync
        def _(sp):
            full = NT - 1
            sp.wait_ge(s_pad, 4)
            nb, blk = NE // (P * P), P * P
            rest = NE - nb * blk
            rr, tail = rest // P, rest % P
            for sb_t, dr in ((E_SRC, src), (E_DST, dst), (E_W, edge_weight)):
                sp.dma_start(sb_t[:, 0:nb * P].rearrange("p (k j) -> p k j", j=P),
                             dr[0:nb * blk].rearrange("(k p j) -> p k j", p=P, j=P)).then_inc(s_e, 16)
                sp.dma_start(sb_t[0:rr, nb * P:nb * P + P],
                             dr[nb * blk:nb * blk + rr * P].rearrange("(p j) -> p j", j=P)).then_inc(s_e, 16)
                sp.dma_start(sb_t[rr:rr + 1, nb * P:nb * P + tail],
                             dr[nb * blk + rr * P:NE].rearrange("(p j) -> p j", p=1)).then_inc(s_e, 16)
            sp.dma_start(X[:, 0:full * D].rearrange("p (t d) -> p t d", d=D),
                         x[0:full * P, :].rearrange("(t p) d -> p t d", p=P)).then_inc(s_x, 16)
            sp.dma_start(X[0:LAST, full * D:NT * D], x[full * P:N, :]).then_inc(s_x, 16)
            for sb_t, dr in ((WA, W6), (WB, W7), (WC, Wp)):
                sp.dma_start(sb_t[:, :].rearrange("p (k d) -> p k d", k=KC),
                             dr.rearrange("(k p) d -> p k d", p=P)).then_inc(s_w, 16)
            for sb_t, dr in ((BA, b6), (BB, b7), (BC, bp), (GAM, gamma), (BET, beta)):
                sp.dma_start(sb_t[:, :], dr.rearrange("(a d) -> a d", a=1).to_broadcast([P, D])).then_inc(s_par, 16)
            sp.dma_start(GBS[:, :], gate_b.rearrange("(a d) -> a d", a=1).to_broadcast([P, E1])).then_inc(s_par, 16)
            sp.dma_start(WRS[:, :].rearrange("p (k e) -> p k e", k=KC),
                         Wr.rearrange("(k p) e -> p k e", p=P)).then_inc(s_par, 16)
            sp.dma_start(GWS[:, :].rearrange("p (k e) -> p k e", k=KC),
                         gate_w.rearrange("(k p) e -> p k e", p=P)).then_inc(s_par, 16)
            sp.dma_start(SM[0:1, 8:8 + E0], br.rearrange("(a e) -> a e", a=1)).then_inc(s_par, 16)

            sp.wait_ge(s_meta, 1)
            with nc.allow_non_contiguous_dma(reason="2 x 896 elements, once"):
                for k in range(2):
                    sp.dma_start(meta_d[k:k + 1, :].rearrange("a (k p) -> p (a k)", p=P),
                                 T_I[:, k * NB:(k + 1) * NB]).then_inc(s_metad, 16)
            sp.sem_inc(s_stg, U)

            def store_table(k, tab, source):
                n, m = seq_mm[k], seq_st[k] // U
                with sp.Fori(0, NI) as i:
                    for u in range(U):
                        sp.wait_ge(s_od, U + n + U * i + u + 1)
                        sp.dma_start(tab[bass.ds((U * i + u) * P, P), 0:D], source(i, u)).then_inc(s_st[u], 16)
                    for u in range(U):
                        sp.wait_ge(s_st[u], 16 * (m + i + 1))
                        sp.sem_inc(s_stg, 1)

            def staged(i, u):
                return TT[:, u * D:(u + 1) * D]

            def in_acc(i, u):
                return ACC[:, ts(U * i + u, D)]

            def stage_indices(layer):
                n = NC * layer
                with sp.Fori(0, GI) as i:
                    for q in range(G // Q):
                        sp.wait_ge(s_free, n + G * i + Q * (q + 1))
                        sp.dma_start(IDX[:, q * Q:(q + 1) * Q], SRC[:, bass.ds(G * i + q * Q, Q)])\
                            .then_inc(s_idx[q], 16)

            store_table(T1, tab1, staged)
            sp.wait_ge(s_metad, 32)
            sp.wait_ge(s_mm, U + seq_mm[T1] + NT)
            sp.dma_start(META.rearrange("a (r c) -> a r c", r=2),
                         meta_d.rearrange("(a r) c -> a r c", a=1)).then_inc(s_metal, 16)
            sp.wait_ge(s_deg, 1)
            sp.dma_start(tab1_v[:, :, D:ROW1], DOX[:, :].rearrange("p (t c) -> p t c", c=4)).then_inc(s_dost, 16)
            sp.wait_ge(s_const, 11)
            for k in range(CLEAR):
                sp.dma_start(slots_x[k * 16 * P:(k + 1) * 16 * P, :].rearrange("(t p) d -> p t d", p=P),
                             ZB.rearrange("p (a d) -> p a d", a=1).to_broadcast([P, 16, D])).then_inc(s_zf, 16)
            with nc.allow_non_contiguous_dma(reason="8192 elements, once"):
                for e in range(E1):
                    sp.dma_start(B1L[:, e * FC1:(e + 1) * FC1], b1[e].rearrange("(f p) -> p f", p=P))\
                        .then_inc(s_b1, 16)
            stage_indices(0)
            store_table(T2, tab2, staged)
            stage_indices(1)

            sp.wait_ge(s_ex, 1)
            _, chosen = nc.values_load_multi_w_load_instructions(
                EXI[0:1, 0:2], engines=(ENG.SP,), min_val=0, max_val=E0 - 1,
                skip_runtime_bounds_check_because="an argmax over the experts")
            for k, e in enumerate(chosen):
                sp.dma_start(W1S[:, k * KC * F0:(k + 1) * KC * F0].rearrange("p (k f) -> p k f", k=KC),
                             W1a[bass.ds(e, 1), :, :].rearrange("e (k p) f -> p (e k) f", p=P)).then_inc(s_fw, 16)
                sp.dma_start(W2S[:, k * FC0 * D:(k + 1) * FC0 * D].rearrange("p (k f) -> p k f", k=FC0),
                             W2a[bass.ds(e, 1), :, :].rearrange("e (k p) f -> p (e k) f", p=P)).then_inc(s_fw, 16)
                sp.dma_start(B2P[:, k * D:(k + 1) * D], b2a[bass.ds(e, 1), :].to_broadcast([P, D])).then_inc(s_fw, 16)
                with nc.allow_non_contiguous_dma(reason="512 elements, once"):
                    sp.dma_start(B1S[:, k * FC0:(k + 1) * FC0],
                                 b1a[bass.ds(e, 1), :].rearrange("e (f p) -> p (e f)", p=P)).then_inc(s_fw, 16)
            for sb_t, dr in ((WA, G1), (WB, G2)):
                sp.dma_start(sb_t[:, :].rearrange("p (k d) -> p k d", k=KC),
                             dr.rearrange("(k p) d -> p k d", p=P)).then_inc(s_w2, 16)
            for sb_t, dr in ((BA, g1), (BB, g2)):
                sp.dma_start(sb_t[:, :], dr.rearrange("(a d) -> a d", a=1).to_broadcast([P, D])).then_inc(s_w2, 16)

            store_table(T4, tab3, in_acc)
            stage_indices(2)
            store_table(T5, tab4, in_acc)
            stage_indices(3)

            def store_y(e):
                k = e % 2
                sp.wait_ge(s_1y, RB * (e + 1))
                for r0, r1, rows in PARTS:
                    sp.dma_start(slots_y[e * CAP + r0 * P:e * CAP + (r1 - 1) * P + rows, :]
                                 .rearrange("(r p) d -> p r d", p=rows),
                                 YS[0:rows, (k * RB + r0) * D:(k * RB + r1) * D].rearrange("p (r d) -> p r d", d=D))\
                        .then_inc(s_ys[k], 16)

            for u in range(U):
                sp.wait_ge(s_sc[u], 16 * NI)
            for e in range(E1):
                k = e % 2
                if e >= 2:
                    store_y(e - 2)
                for r0, r1, rows in PARTS:
                    sp.dma_start(RBF[0:rows, (k * RB + r0) * D:(k * RB + r1) * D].rearrange("p (r d) -> p r d", d=D),
                                 slots_x[e * CAP + r0 * P:e * CAP + (r1 - 1) * P + rows, :]
                                 .rearrange("(r p) d -> p r d", p=rows)).then_inc(s_lw[k], 16)
                sp.dma_start(W1L[:, k * KC * F1:(k + 1) * KC * F1].rearrange("p (k f) -> p k f", k=KC),
                             w1[e].rearrange("(k p) f -> p k f", p=P)).then_inc(s_lw[k], 16)
                sp.dma_start(W2L[:, k * FC1 * D:(k + 1) * FC1 * D].rearrange("p (k f) -> p k f", k=FC1),
                             w2[e].rearrange("(k p) f -> p k f", p=P)).then_inc(s_lw[k], 16)
                sp.dma_start(B2L[k][:, :], b2[e:e + 1, :].to_broadcast([P, D])).then_inc(s_lw[k], 16)
            store_y(E1 - 2)
            store_y(E1 - 1)

            for t in range(NT):
                sp.wait_ge(s_fin, t + 1)
                rows = P if t < NT - 1 else LAST
                sp.dma_start(out[t * P:t * P + rows, :], X[0:rows, t * D:(t + 1) * D]).then_inc(s_out, 16)
            sp.wait_ge(s_out, 16 * NT)

        @block.gpsimd
        def _(po):
            for tile, value in ((IDN, 0.0), (ONE, 1.0), (EPSL, EPS_LN), (EPSD, EPS_DEG), (ZERO, 0.0), (VALID, 1.0)):
                po.memset(tile[:, :], value).then_inc(s_const, 1)
            po.memset(ZB, 0.0).then_inc(s_const, 1)
            po.iota(IOTA, pattern=[[1, NP]], base=0, channel_multiplier=0).then_inc(s_const, 1)
            po.wait_ge(s_const, 8)
            po.affine_select(out=IDN[:, :], in_=IDN[:, :], compare_op=ALU.not_equal, fill=1.0, base=0,
                             pattern=[[-1, P]], channel_multiplier=1).then_inc(s_const, 1)
            po.affine_select(out=TRI[:, :], in_=ONE[:, :], compare_op=ALU.is_ge, fill=0.0, base=0,
                             pattern=[[1, P]], channel_multiplier=-1).then_inc(s_const, 1)
            po.affine_select(out=VALID[:, NT - 1:NT], in_=VALID[:, NT - 1:NT], compare_op=ALU.is_ge, fill=0.0,
                             base=LAST - 1, pattern=[[0, 1]], channel_multiplier=-1).then_inc(s_const, 1)

            def hold(semaphore, value):
                po.wait_ge(semaphore, value)
                po.sem_inc(s_tick, 1)

            def gather_edges(layer, tab, width):
                n = NC * layer
                with po.Fori(0, GI) as i:
                    for j in range(G):
                        if j % Q == 0:
                            hold(s_idx[j // Q], 16 * (GI * layer + i + 1))
                        hold(s_free, n + G * i + j + 1)
                        po.indirect_dma_start(
                            out=ROWS[j][:, 0:width], out_offset=None, in_=tab[:, :],
                            in_offset=bass.IndirectOffsetOnAxis(ap=IDX[:, j:j + 1].bitcast(u32), axis=0))\
                            .then_inc(s_row[j], 16)

            def table_stored(k):
                po.wait_ge(s_stg, U + seq_st[k] + NT)

            po.wait_ge(s_histd, 1)
            po.memset(ACC[:, :], 0.0).then_inc(s_accz, 1)
            table_stored(T1)
            po.wait_ge(s_dost, 16)
            po.wait_ge(s_dibd, ND)
            gather_edges(0, tab1, ROW1)
            po.wait_ge(s_xin, seq_in[T2] + NT)
            po.memset(ACC[:, :], 0.0).then_inc(s_accz, 1)
            table_stored(T2)
            gather_edges(1, tab2, D)
            po.wait_ge(s_od, U + seq_mm[FA] + NT)
            po.iota(IOTA, pattern=[[1, NP]], base=0, channel_multiplier=0).then_inc(s_io, 1)
            table_stored(T4)
            gather_edges(2, tab3, D)
            table_stored(T5)
            gather_edges(3, tab4, D)

            po.wait_ge(s_wfree, 1)
            po.iota(NIDI.bitcast(i32), pattern=[[P, NT]], base=0, channel_multiplier=1).then_inc(s_nid, 1)
            po.iota(E8I.bitcast(i32), pattern=[[0, NT], [1, E1]], base=0, channel_multiplier=0).then_inc(s_nid, 1)

            po.wait_ge(s_zf, 16 * CLEAR)
            for t in range(NT):
                po.wait_ge(s_xin, seq_in[SG] + NT + t + 1)
                po.indirect_dma_start(
                    out=slots_x[:, :], out_offset=bass.IndirectOffsetOnAxis(ap=IDS[:, t:t + 1].bitcast(u32), axis=0),
                    in_=XIN[:, (t % U) * D:(t % U + 1) * D], in_offset=None).then_inc(s_sc[t % U], 16)

            for k in range(2):
                po.wait_ge(s_ys[k], 16 * 2 * (E1 // 2))
            for t in range(NT):
                if t >= U:
                    po.wait_ge(s_yu, t - U + 1)
                po.indirect_dma_start(
                    out=XIN[:, (t % U) * D:(t % U + 1) * D], out_offset=None, in_=slots_y[:, :],
                    in_offset=bass.IndirectOffsetOnAxis(ap=IDY[:, t:t + 1].bitcast(u32), axis=0))\
                    .then_inc(s_yg[t % U], 16)

        @block.tensor
        def _(pe):
            pe.wait_ge(s_const, 11)
            pe.wait_ge(s_e, 144)
            pe.wait_ge(s_ef, 2)
            for a, blk in enumerate((E_SF, E_DF, E_W)):
                for k in range(NB):
                    last = pe.transpose(PS[2 * a + k // 4][:, (k % 4) * P:(k % 4 + 1) * P], blk[:, k * P:(k + 1) * P],
                                        IDN[:, :])
                last.then_inc(s_et, 1)

            pe.sem_inc(s_xtp, U)
            pe.sem_inc(s_mm, U)

            def transpose_tile(k, i, u):
                n, m = seq_in[k] + U * i + u, seq_xt[k] + U * i + u
                pe.wait_ge(s_xin, n + 1)
                pe.wait_ge(s_xt, U + m + 1 - gap(u))
                for c in range(KC):
                    last = pe.transpose(slot_t(u)[:, c * P:(c + 1) * P], XIN[:, u * D + c * P:u * D + (c + 1) * P],
                                        IDN[:, :])
                last.then_inc(s_xtp, 1)

            def dense_pass(k, w):
                with pe.Fori(0, NI) as i:
                    for u in range(U):
                        transpose_tile(k, i, u)
                    for u in range(U):
                        pe.wait_ge(s_xt, U + seq_xt[k] + U * i + u + 1)
                        pe.wait_ge(s_od, U + seq_mm[k] + U * i + u + 1 - gap(u))
                        for c in range(KC):
                            last = pe.matmul(slot_o(u), XT[:, u * D + c * P:u * D + (c + 1) * P],
                                             w[:, c * D:(c + 1) * D], start=(c == 0), stop=(c == KC - 1))
                        last.then_inc(s_mm, 1)
                pe.wait_ge(s_xt, U + seq_xt[k] + NT)

            pe.wait_ge(s_es, 1)
            pe.wait_ge(s_w, 48)
            dense_pass(T1, WA)

            HSRC, HDST = PS[0][:, 0:NT], PS[1][:, 0:2 * NT]
            pe.matmul(HSRC, ZB[:, 0:P], ZB[:, 0:NT], start=True, stop=False)
            pe.matmul(HDST, ZB[:, 0:P], ZB[:, 0:2 * NT], start=True, stop=False)
            pe.sem_inc(s_hist, HS)
            with pe.Fori(0, NC // HS) as i:
                for j in range(HS):
                    pe.wait_ge(s_hot, HS * i + j + 1)
                    pe.matmul(HSRC, SLO[:, j * P:(j + 1) * P], SHW[:, j * NT:(j + 1) * NT], start=False, stop=False)
                    pe.matmul(HDST, DLO[:, j * P:(j + 1) * P], DHW[:, j * 2 * NT:(j + 1) * 2 * NT],
                              start=False, stop=False).then_inc(s_hist, 1)
            pe.matmul(HSRC, ZB[:, 0:P], ZB[:, 0:NT], start=False, stop=True)
            pe.matmul(HDST, ZB[:, 0:P], ZB[:, 0:2 * NT], start=False, stop=True).then_inc(s_histd, 1)

            for g in range(ND):
                w = P * min(4, NT - 4 * g)
                pe.wait_ge(s_diag, g + 1)
                if g >= 2:
                    pe.wait_ge(s_dibd, g - 1)
                pe.matmul(PS[2 + g % 2][:, 0:w], ONE[:, :], ROWDG[g % 2][:, 0:w], start=True, stop=True)\
                    .then_inc(s_dib, 1)

            more = pe.alloc_register("more_sums")
            pe.reg_mov(more, 1)

            def sum_edges(layer):
                with pe.Fori(0, GI) as i:
                    for q in range(G // Q):
                        def product(chosen, bank):
                            for k in range(Q):
                                m = Q * chosen + k
                                last = pe.matmul(PS[bank][:, 0:D], MM[:, m * P:(m + 1) * P],
                                                 ROWS[q * Q + k][:, 0:D], start=(k == 0), stop=(k == Q - 1))
                            return last

                        _, (span,) = nc.values_load_multi_w_load_instructions(
                            SPAN[0:1, bass.ds((G // Q) * i + q, 1)], engines=(ENG.PE,), min_val=0, max_val=NT - 1,
                            skip_runtime_bounds_check_because="a count of node tiles")
                        for k in range(Q):
                            pe.wait_ge(s_row[q * Q + k], 16 * (GI * layer + i + 1))
                        pe.wait_ge(s_m, (NC // Q + 1) * layer + (G // Q) * i + q + 1)
                        product(q % 2, q % 2).then_inc(s_p, 1)
                        with pe.If(span > 0):
                            with pe.Fori(0, span):
                                pe.wait_ge(s_me, pe.snap(more))
                                product(AGAIN, AGAIN).then_inc(s_pe, 1)
                                pe.reg_add(more, more, 1)
                            pe.nop()

            pe.wait_ge(s_span, 1)
            sum_edges(0)
            dense_pass(T2, WB)
            sum_edges(1)
            dense_pass(T3, WC)

            with pe.Fori(0, NI) as i:
                for u in range(U):
                    pe.wait_ge(s_xin, seq_in[RT] + U * i + u + 1)
                    for c in range(KC):
                        last = pe.matmul(PS[0][:, bass.ds(c * 64 + U * i + u, 1)],
                                         XIN[:, u * D + c * P:u * D + (c + 1) * P],
                                         VALID[:, bass.ds(U * i + u, 1)], start=True, stop=True)
                    last.then_inc(s_xtp, 1)
            pe.wait_ge(s_par, 144)
            pe.wait_ge(s_mean, 1)
            for c in range(KC):
                last = pe.matmul(PS[1][0:1, 0:E0], MNT[:, c:c + 1], WRS[:, c * E0:(c + 1) * E0],
                                 start=(c == 0), stop=(c == KC - 1))
            last.then_inc(s_rl, 1)
            pe.wait_ge(s_wab, 1)
            pe.matmul(PS[2][:, 0:2], ONE[0:1, :], SM[0:1, 120:122], start=True, stop=True).then_inc(s_wabp, 1)

            pe.wait_ge(s_fws, 1)
            pe.sem_inc(s_hid, NU)
            with pe.Fori(0, NI) as i:
                pe.wait_ge(s_hid, NU * i + NU)
                for u in range(U):
                    transpose_tile(FA, i, u)
                pe.wait_ge(s_xt, U + seq_xt[FA] + U * i + U)
                for q in range(NU):
                    fe, hf = q // 2, q % 2
                    if q >= 4:
                        pe.wait_ge(s_hid, NU * i + NU + q - 3)
                    for c in range(KC):
                        w = ((fe // FC0) * KC + c) * F0 + (fe % FC0) * P
                        last = pe.matmul(PS[q % 4][:, 0:GT // 2], W1S[:, w:w + P],
                                         XT0[:, c * GT + hf * (GT // 2):c * GT + (hf + 1) * (GT // 2)],
                                         start=(c == 0), stop=(c == KC - 1))
                    last.then_inc(s_up, 1)
                pe.wait_ge(s_hid, NU * i + 2 * NU)
                for u in range(U):
                    pe.wait_ge(s_od, U + seq_mm[FA] + U * i + u + 1 - gap(u))
                    for fe in range(2 * FC0):
                        last = pe.matmul(slot_o(u), H0[:, fe * GT + u * P:fe * GT + (u + 1) * P],
                                         W2S[:, fe * D:(fe + 1) * D], start=(fe == 0), stop=(fe == 2 * FC0 - 1))
                    last.then_inc(s_mm, 1)

            pe.wait_ge(s_w2, 64)
            dense_pass(T4, WA)
            sum_edges(2)
            dense_pass(T5, WB)
            sum_edges(3)

            pe.wait_ge(s_free, G + 4 * NC)
            pe.sem_inc(s_gate, U)
            with pe.Fori(0, NI) as i:
                for u in range(U):
                    transpose_tile(SG, i, u)
                for u in range(U):
                    pe.wait_ge(s_xt, U + seq_xt[SG] + U * i + u + 1)
                    for c in range(KC):
                        last = pe.matmul(PS[4][:, bass.ds((U * i + u) * E1, E1)],
                                         XT[:, u * D + c * P:u * D + (c + 1) * P],
                                         GWS[:, c * E1:(c + 1) * E1], start=(c == 0), stop=(c == KC - 1))
                    last.then_inc(s_gate, 1)
            pe.wait_ge(s_oh, 1)
            pe.matmul(PS[5][:, 0:NX], TRI[:, :], OH, start=True, stop=True)
            pe.matmul(PS[6][:, 0:NX], ONE[:, :], OH, start=True, stop=True).then_inc(s_cum, 1)

            for e in range(E1):
                k = e % 2
                pe.wait_ge(s_lw[k], 80 * (e // 2 + 1))
                if e:
                    pe.wait_ge(s_1h, NU1 * e)
                for r in range(RB):
                    rows = min(P, CAP - r * P)
                    if r >= BK:
                        pe.wait_ge(s_1x, RB * e + r - BK + 1)
                    for c in range(KC):
                        last = pe.transpose(PS[r % BK][:, c * P:c * P + rows],
                                            RBF[0:rows, (k * RB + r) * D + c * P:(k * RB + r) * D + (c + 1) * P],
                                            IDN[0:rows, 0:rows])
                    last.then_inc(s_1t, 1)
                pe.wait_ge(s_1x, RB * (e + 1))
                for q in range(NU1):
                    f, h0, hn = q // 2, (q % 2) * HALF, (HALF, CAP - HALF)[q % 2]
                    if q >= 4:
                        pe.wait_ge(s_1h, NU1 * e + q - 3)
                    for c in range(KC):
                        w = (k * KC + c) * F1 + f * P
                        last = pe.matmul(PS[q % 4][:, 0:hn], W1L[:, w:w + P],
                                         XT1[:, c * CAP + h0:c * CAP + h0 + hn],
                                         start=(c == 0), stop=(c == KC - 1))
                    last.then_inc(s_1u, 1)
                pe.wait_ge(s_1h, NU1 * (e + 1))
                for r in range(RB):
                    rows = min(P, CAP - r * P)
                    if e or r >= BK:
                        pe.wait_ge(s_1y, RB * e + r - BK + 1)
                    for f in range(FC1):
                        last = pe.matmul(PS[BK + r % BK][0:rows, 0:D],
                                         H1[:, f * CAP + r * P:f * CAP + r * P + rows],
                                         W2L[:, (k * FC1 + f) * D:(k * FC1 + f + 1) * D],
                                         start=(f == 0), stop=(f == FC1 - 1))
                    last.then_inc(s_1d, 1)

        @block.scalar
        def _(ac):
            ac.sem_inc(s_xt, U)

            def deviation(n):
                ac.wait_ge(s_var, n)
                ac.activation(SD[:, :].rearrange("p (t a) -> p t a", a=1),
                              MV[:, :].rearrange("p (t c) -> p t c", c=2)[:, :, 1:2],
                              ACT.Sqrt, bias=EPSL[:, :]).then_inc(s_std, 1)

            def copy_transposed(k, i, func, into):
                for u in range(U):
                    ac.wait_ge(s_xtp, U + seq_in[k] + U * i + u + 1)
                    if k in (T1, T2, T3, T4, T5):
                        ac.wait_ge(s_mm, seq_mm[k] + U * i + u + 1)
                    if k == SG:
                        ac.wait_ge(s_gate, U * i + u + 1)
                    ac.activation(into(u), by_block(slot_t(u)), func).then_inc(s_xt, 1)

            def to_slot(u):
                return by_block(XT[:, u * D:(u + 1) * D])

            def stage_products(k, i):
                for u in range(U):
                    ac.wait_ge(s_mm, U + seq_mm[k] + U * i + u + 1)
                    ac.wait_ge(s_stg, seq_st[k] + U * i + u + 1)
                    ac.activation(TT[:, u * D:(u + 1) * D], slot_o(u), ACT.Copy).then_inc(s_od, 1)

            ac.sem_inc(s_od, U)
            ac.wait_ge(s_const, 11)
            deviation(1)
            with ac.Fori(0, NI) as i:
                copy_transposed(T1, i, ACT.Copy, to_slot)
                stage_products(T1, i)

            ac.wait_ge(s_cnt, 1)
            ac.activation(DINV[:, :], CNT[:, :], ACT.Sqrt).then_inc(s_root, 1)
            for g in range(ND):
                w = P * min(4, NT - 4 * g)
                ac.wait_ge(s_dib, g + 1)
                ac.activation(DIB[:, g * 4 * P:g * 4 * P + w], PS[2 + g % 2][:, 0:w], ACT.Copy).then_inc(s_dibd, 1)

            with ac.Fori(0, GI) as i:
                for j in range(G):
                    k = j % (2 * Q)
                    ac.wait_ge(s_row[j], 16 * (i + 1))
                    if j % Q == 0:
                        ac.wait_ge(s_di, (G // Q) * i + j // Q + 1)
                    ac.activation(DRT[:, k:k + 1], DIE[:, k:k + 1], ACT.Sqrt,
                                  bias=EPSD[:, :], scale=ROWS[j][:, D:D + 1]).then_inc(s_dr, 1)
            k = NC % (2 * Q)
            ac.wait_ge(s_di, NC // Q + 1)
            ac.activation(DRT[:, k:k + Q], DIE[:, k:k + Q], ACT.Sqrt, bias=EPSD[:, :]).then_inc(s_dr, Q)

            with ac.Fori(0, NI) as i:
                copy_transposed(T2, i, ACT.Relu, to_slot)
                stage_products(T2, i)
            with ac.Fori(0, NI) as i:
                copy_transposed(T3, i, ACT.Relu, to_slot)
            deviation(2)

            ac.wait_ge(s_e1, 1)
            ac.activation(SM[0:1, 24:32], SM[0:1, 16:24], ACT.Exp, bias=SM[0:1, 1:2]).then_inc(s_x1, 1)
            ac.wait_ge(s_e1, 2)
            ac.activation(SM[0:1, 48:56], SM[0:1, 40:48], ACT.Exp, bias=SM[0:1, 3:4]).then_inc(s_x1, 1)
            ac.wait_ge(s_e1, 3)
            ac.activation(SM[0:1, 113:114], SM[0:1, 112:113], ACT.Exp).then_inc(s_x1, 1)

            def to_block(u):
                return by_block(XT0)[:, :, u * P:(u + 1) * P]

            def gelus(i):
                for q in range(NU):
                    fe, hf = q // 2, q % 2
                    ac.wait_ge(s_up, NU * i + q + 1)
                    ac.activation(H0[:, fe * GT + hf * (GT // 2):fe * GT + (hf + 1) * (GT // 2)],
                                  PS[q % 4][:, 0:GT // 2], ACT.Gelu, bias=B1S[:, fe:fe + 1]).then_inc(s_hid, 1)

            def deviation_of_7(n):
                ac.wait_ge(s_v7, n)
                ac.activation(NR7[:, :].rearrange("p (u a) -> p u a", a=1),
                              MV7[:, :].rearrange("p (u c) -> p u c", c=2)[:, :, 1:2],
                              ACT.Sqrt, bias=EPSL[:, :]).then_inc(s_d7, 1)

            ac.wait_ge(s_fw, 128)
            copy_transposed(FA, 0, ACT.Copy, to_block)
            gelus(0)
            with ac.Fori(1, NI) as i:
                copy_transposed(FA, i, ACT.Copy, to_block)
                gelus(i)
                deviation_of_7(i)
            deviation_of_7(NI)
            deviation(3)

            with ac.Fori(0, NI) as i:
                copy_transposed(T4, i, ACT.Copy, to_slot)
            with ac.Fori(0, NI) as i:
                copy_transposed(T5, i, ACT.Copy, to_slot)
                ac.wait_ge(s_sq, i + 1)
                ac.activation(NRV[:, ts(i, U)], SSQ[:, ts(i, U)], ACT.Sqrt).then_inc(s_nr, 1)
            deviation(4)
            with ac.Fori(0, NI) as i:
                copy_transposed(SG, i, ACT.Copy, to_slot)
            ac.wait_ge(s_ei, 1)
            ac.activation(TA, TA, ACT.Exp).then_inc(s_eo, 1)

            for e in range(E1):
                for r in range(RB):
                    ac.wait_ge(s_1t, RB * e + r + 1)
                    if e and r == 0:
                        ac.wait_ge(s_1u, NU1 * e)
                    rows = min(P, CAP - r * P)
                    ac.activation(by_block(XT1)[:, :, r * P:r * P + rows],
                                  by_block(PS[r % BK][:, 0:D])[:, :, 0:rows], ACT.Copy)\
                        .then_inc(s_1x, 1)
                if e:
                    ac.wait_ge(s_1d, RB * e)
                else:
                    ac.wait_ge(s_b1, 16 * E1)
                for q in range(NU1):
                    f, h0, hn = q // 2, (q % 2) * HALF, (HALF, CAP - HALF)[q % 2]
                    ac.wait_ge(s_1u, NU1 * e + q + 1)
                    ac.activation(H1[:, f * CAP + h0:f * CAP + h0 + hn],
                                  PS[q % 4][:, 0:hn], ACT.Relu, bias=B1L[:, e * FC1 + f:e * FC1 + f + 1])\
                        .then_inc(s_1h, 1)

        @block.vector
        def _(ve):
            def settle():
                ve.wait_ge(s_dv, dve.now())

            def hold(semaphore, value):
                ve.wait_ge(semaphore, value)
                ve.sem_inc(s_vtick, 1)

            step = dve.tell

            def loop(start, trips, per, body):
                with ve.Fori(start, trips) as i:
                    dve.enter(i - start if start else i, per)
                    body(i)
                    dve.check()
                dve.leave(trips - start)

            def tile(v, i, u):
                return v[:, ts(U * i + u, D)]

            def slot(v, u):
                return v[:, u * D:(u + 1) * D]

            def normalized(into, i, u):
                t = U * i + u
                return ve.tensor_scalar(into, tile(X, i, u), MV[:, bass.ds(2 * t, 1)], RS[:, bass.ds(t, 1)],
                                        ALU.subtract, ALU.mult)

            def moments(i):
                hold(s_dv, dve.now())
                for u in range(U):
                    last = ve.bn_stats(ST7[:, u * 6:(u + 1) * 6], tile(X, i, u))
                step(last)
                hold(s_dv, dve.now())
                for u in range(U):
                    last = ve.bn_aggr(MV7[:, 2 * u:2 * u + 2], ST7[:, u * 6:(u + 1) * 6])
                step(last)
                settle()
                step(ve.tensor_copy(MV[:, ts(i, 2 * U)], MV7[:, :]))

            def reciprocal_deviation(n):
                settle()
                ve.sem_inc(s_var, 1)
                ve.wait_ge(s_std, n)
                step(ve.reciprocal(RS[:, :], SD[:, :]))
                settle()

            def feed(k, i, make):
                for u in range(U):
                    ve.wait_ge(s_xtp, seq_in[k] + U * i + u + 1)
                    make(slot(XIN, u), i, u).then_inc(s_xin, 1)

            def feed_normalized(k, i):
                feed(k, i, normalized)

            def fed(k, i, consume):
                with_next = i is not None
                return with_next

            ve.memset(X[:, (NT - 1) * D:NT * D], 0.0).then_inc(s_pad, 1)
            ve.memset(E_SRC[:, (NB - 1) * P:NB * P], 0).then_inc(s_pad, 1)
            ve.memset(E_DST[:, (NB - 1) * P:NB * P], NP - 1).then_inc(s_pad, 1)
            ve.memset(E_W[:, (NB - 1) * P:NB * P], 0.0).then_inc(s_pad, 1)
            step(ve.memset(NRM[:, :], 0.0))
            step(ve.memset(DOX[:, :], 0.0))
            ve.sem_inc(s_free, G)
            ve.sem_inc(s_joined, 1)
            ve.sem_inc(s_aj, 1)
            ve.sem_inc(s_dj, 1)

            ve.wait_ge(s_e, 144)
            ve.tensor_copy(E_SF, E_SRC).then_inc(s_ef, 1)
            ve.tensor_copy(E_DF, E_DST).then_inc(s_ef, 1)
            ve.wait_ge(s_ef, 2)
            df3 = E_DF.rearrange("p (k j) -> p k j", j=P)
            ve.tensor_reduce(S_HI[:, 0:NB], df3, AX.X, ALU.min)
            step(ve.tensor_reduce(S_HI[:, NB:2 * NB], df3, AX.X, ALU.max))
            settle()
            step(ve.tensor_copy(D_HI[:, 0:2 * NB].bitcast(i32), S_HI[:, 0:2 * NB]))
            settle()
            ve.tensor_scalar(T_I[:, 0:2 * NB], D_HI[:, 0:2 * NB].bitcast(i32), 7, None, ALU.arith_shift_right)\
                .then_inc(s_meta, 1)

            for a, (into, n) in enumerate(((SRC, 1), (DST, 2), (EW, 3))):
                ve.wait_ge(s_et, n)
                ve.tensor_copy(into[:, 0:4 * P], PS[2 * a][:, :])
                last = ve.tensor_copy(into[:, 4 * P:NB * P], PS[2 * a + 1][:, 0:(NB - 4) * P])
            last.then_inc(s_es, 1)
            ve.wait_ge(s_es, 1)
            DSI = S_HI.bitcast(i32)
            ve.wait_ge(s_metad, 32)
            step(ve.tensor_scalar(T_I, SRC[:, :], 7, None, ALU.arith_shift_right))
            settle()
            step(ve.tensor_copy(S_HI, T_I))
            settle()
            step(ve.tensor_scalar(T_I, SRC[:, :], P - 1, None, ALU.bitwise_and))
            settle()
            step(ve.tensor_copy(S_LO, T_I))
            step(ve.tensor_copy(E_SRC, DST[:, :]))
            settle()
            step(ve.tensor_scalar(T_I, E_SRC, 7, None, ALU.arith_shift_right))
            settle()
            step(ve.tensor_copy(D_HI, T_I))
            settle()
            step(ve.tensor_scalar(T_I, E_SRC, P - 1, None, ALU.bitwise_and))
            settle()
            step(ve.tensor_copy(D_LO, T_I))

            ve.wait_ge(s_x, 32)
            settle()
            loop(0, NI, 3, moments)
            ve.wait_ge(s_const, 11)
            reciprocal_deviation(1)
            loop(0, NI, 0, lambda i: feed_normalized(T1, i))

            def onehots(i):
                for j in range(HS):
                    c = bass.ds(HS * i + j, 1)
                    ve.wait_ge(s_hist, HS * i + j + 1)
                    ve.tensor_scalar(SLO[:, j * P:(j + 1) * P], IOTA[:, 0:P], S_LO[:, c], None, ALU.is_equal)
                    ve.tensor_scalar(SHW[:, j * NT:(j + 1) * NT], IOTA[:, 0:NT], S_HI[:, c], EW[:, c],
                                     ALU.is_equal, ALU.mult)
                    ve.tensor_scalar(DLO[:, j * P:(j + 1) * P], IOTA[:, 0:P], D_LO[:, c], None, ALU.is_equal)
                    w = 2 * NT * j
                    ve.tensor_scalar(DHW[:, w:w + NT], IOTA[:, 0:NT], D_HI[:, c], EW[:, c], ALU.is_equal, ALU.mult)
                    ve.tensor_scalar(DHW[:, w + NT:w + 2 * NT], IOTA[:, 0:NT], D_HI[:, c], None, ALU.is_equal)\
                        .then_inc(s_hot, 1)

            loop(0, NC // HS, 0, onehots)
            ve.wait_ge(s_histd, 1)
            ve.tensor_copy(DOX[:, :].rearrange("p (t c) -> p t c", c=4)[:, :, 0:1],
                           PS[0][:, 0:NT].rearrange("p (t a) -> p t a", a=1))
            step(ve.tensor_copy(DEGI[:, :], PS[1][:, 0:NT]))
            settle()
            ve.sem_inc(s_deg, 1)
            ve.tensor_scalar(CNT[:, :], PS[1][:, NT:2 * NT], 1.0, 1e-12, ALU.add, ALU.max).then_inc(s_cnt, 1)
            ve.wait_ge(s_stg, U + seq_st[T1] + NT)
            for g in range(ND):
                tiles = min(4, NT - 4 * g)
                if g >= 2:
                    ve.wait_ge(s_dib, g - 1)
                ve.tensor_tensor(
                    ROWDG[g % 2][:, 0:tiles * P].rearrange("p (t n) -> p t n", n=P),
                    IDN[:, :].rearrange("p (a n) -> p a n", a=1).to_broadcast([P, tiles, P]),
                    DEGI[:, 4 * g:4 * g + tiles].rearrange("p (t a) -> p t a", a=1).to_broadcast([P, tiles, P]),
                    ALU.mult).then_inc(s_diag, 1)
            ve.wait_ge(s_root, 1)
            step(ve.reciprocal(DINV[:, :], DINV[:, :]))

            z = ve.alloc_register("more_selections")
            ve.reg_mov(z, 1)
            zd = ve.alloc_register("more_degrees")
            ve.reg_mov(zd, 1)

            def load_tile(row, g):
                return nc.values_load_multi_w_load_instructions(
                    row[0:1, bass.ds(g, 1)], engines=(ENG.DVE,), min_val=0, max_val=NT - 1,
                    skip_runtime_bounds_check_because="node tiles")[1][0]

            def sum_edges(layer, scale, find_norms):
                groups_before, made_before = NC // Q * layer, (NC // Q + 1) * layer

                def chunk(g, k):
                    return bass.ds(Q * g + k, 1)

                def select(g, chosen, t):
                    for k in range(Q):
                        c = chunk(g, k)
                        if scale is None:
                            last = ve.tensor_scalar(slot_p(MM, Q * chosen + k), IOTA[:, ts(t, P)], DST[:, c], None,
                                                    ALU.is_equal)
                        else:
                            last = ve.tensor_scalar(slot_p(MM, Q * chosen + k), IOTA[:, ts(t, P)], DST[:, c],
                                                    scale[:, c], ALU.is_equal, ALU.mult)
                    return last

                def join_further(t):
                    count = ve.snap(z)
                    a = ACC[:, ts(t, D)]
                    ve.wait_ge(s_pe, count)
                    ve.wait_ge(s_aj, count)
                    ve.tensor_tensor(a, a, PS[AGAIN][:, 0:D], ALU.add).then_inc(s_aj, 1)
                    ve.reg_add(z, z, 1)

                def collect(g, h):
                    count = g + groups_before
                    t, span = load_tile(FIRST, g), load_tile(SPAN, g)
                    a = ACC[:, ts(t, D)]
                    ve.wait_ge(s_p, count + 1)
                    ve.wait_ge(s_joined, count + 1)
                    ve.tensor_tensor(a, a, PS[h][:, 0:D], ALU.add).then_inc(s_joined, 1)
                    with ve.If(span > 0):
                        with ve.If(span > 1):
                            with ve.Fori(1, span) as e:
                                join_further(a_tile(t + e))
                                select(g, AGAIN, a_tile(t + e + 1)).then_inc(s_me, 1)
                        join_further(a_tile(t + span))
                    hold(s_aj, ve.snap(z))
                    ve.wait_ge(s_joined, count + 2)
                    ve.sem_inc(s_free, Q)

                def select_further(g):
                    t, span = load_tile(FIRST, g), load_tile(SPAN, g)
                    with ve.If(span > 0):
                        select(g, AGAIN, a_tile(t + 1)).then_inc(s_me, 1)

                def select_degrees(into, accum, g, t):
                    for k in range(Q):
                        last = ve.scalar_tensor_tensor(slot_p(DSEL, into + k), IOTA[:, ts(t, P)], DST[:, chunk(g, k)],
                                                       DIB[:, ts(t, P)], ALU.is_equal, ALU.mult,
                                                       accum_out=accum[:, k:k + 1])
                    return last

                def incoming_degrees(g, h):
                    d = DIE[:, Q * h:Q * (h + 1)]
                    t, span = load_tile(FIRST, g), load_tile(SPAN, g)
                    step(select_degrees(Q * h, d, g, t))
                    with ve.If(span > 0):
                        hold(s_dv, dve.now())
                        with ve.Fori(0, span) as e:
                            so_far = ve.snap(zd)
                            ve.wait_ge(s_dj, so_far)
                            select_degrees(Q * AGAIN, DIX, g, a_tile(t + e + 1)).then_inc(s_dx, 1)
                            ve.wait_ge(s_dx, so_far)
                            ve.tensor_tensor(d, d, DIX[:, :], ALU.add).then_inc(s_dj, 1)
                            ve.reg_add(zd, zd, 1)
                        hold(s_dj, ve.snap(zd))
                    hold(s_dv, dve.now())
                    ve.sem_inc(s_di, 1)

                def norms(g, h):
                    these, c = slice(Q * h, Q * (h + 1)), bass.ds(Q * g, Q)
                    ve.wait_ge(s_dr, Q * (g + 1))
                    step(ve.reciprocal(DRI[:, these], DRT[:, these]))
                    settle()
                    step(ve.tensor_tensor(NRM[:, c], DRI[:, these], EW[:, c], ALU.mult))
                    hold(s_dv, dve.now())

                def groups(i):
                    for h in range(2):
                        g = 2 * i + h
                        if find_norms:
                            incoming_degrees(g + 2, h)
                            norms(g + 1, 1 - h)
                        t = load_tile(FIRST, g + 1)
                        select(g + 1, 1 - h, t).then_inc(s_m, 1)
                        collect(g, h)
                        select_further(g + 1)

                if find_norms:
                    incoming_degrees(0, 0)
                    incoming_degrees(1, 1)
                    norms(0, 0)
                t = load_tile(FIRST, 0)
                select(0, 0, t).then_inc(s_m, 1)
                select_further(0)
                loop(0, NC // (2 * Q), 6 if find_norms else 0, groups)

            def slot_p(v, m):
                return v[:, m * P:(m + 1) * P]

            ve.wait_ge(s_metal, 16)
            step(ve.tensor_reduce(GROUP1, META[0:1, 0:EC].rearrange("p (g k) -> p g k", k=Q), AX.X, ALU.min))
            step(ve.tensor_reduce(GROUPN, META[0:1, EC:2 * EC].rearrange("p (g k) -> p g k", k=Q), AX.X, ALU.max))
            settle()
            step(ve.tensor_copy(FIRST[:, :], GROUP1))
            ve.tensor_tensor(SPAN[:, :], GROUPN, GROUP1, ALU.subtract).then_inc(s_span, 1)
            ve.wait_ge(s_span, 1)
            ve.wait_ge(s_accz, 1)
            sum_edges(0, NRM, True)
            ve.wait_ge(s_free, G + NC)

            ve.wait_ge(s_par, 144)

            def plus(bias):
                return lambda into, i, u: ve.tensor_tensor(into, tile(ACC, i, u), bias[:, :], ALU.add)

            loop(0, NI, 0, lambda i: feed(T2, i, plus(BA)))
            ve.wait_ge(s_accz, 2)
            ve.wait_ge(s_xtp, U + seq_in[T2] + NT)
            sum_edges(1, NRM, False)
            ve.wait_ge(s_free, G + 2 * NC)

            def ahead(k, make, take, per):
                feed(k, 0, make)

                def body(i):
                    feed(k, i + 1, make)
                    take(i)
                loop(0, NI - 1, per, body)
                take(NI - 1)

            def take_t3(i):
                for u in range(U):
                    ve.wait_ge(s_mm, U + seq_mm[T3] + U * i + u + 1)
                    ve.tensor_tensor(slot(TT, u), slot_o(u), BC[:, :], ALU.add).then_inc(s_od, 1)
                for u in range(U):
                    ve.wait_ge(s_od, U + seq_mm[T3] + U * i + u + 1)
                    last = ve.tensor_tensor(tile(X, i, u), tile(X, i, u), slot(TT, u), ALU.add)
                step(last)
                moments(i)

            ahead(T3, plus(BB), take_t3, 4)
            reciprocal_deviation(2)

            loop(0, NI, 0, lambda i: feed_normalized(RT, i))
            ve.wait_ge(s_xtp, U + seq_in[RT] + NT)
            step(ve.tensor_reduce(MNT[:, :], PS[0][:, 0:2 * 64].rearrange("p (c t) -> p c t", c=KC)[:, :, 0:NT],
                                  AX.X, ALU.add))
            settle()
            ve.tensor_scalar(MNT[:, :], MNT[:, :], 1.0 / N, None, ALU.mult).then_inc(s_mean, 1)

            def row(a, w=1):
                return SM[0:1, a:a + w]

            def softmax(logits, exps, probs, top, neg, total, turn):
                step(ve.tensor_reduce(row(top), logits, AX.X, ALU.max))
                settle()
                ve.tensor_scalar(row(neg), row(top), -1.0, None, ALU.mult).then_inc(s_e1, 1)
                ve.wait_ge(s_x1, turn)
                step(ve.tensor_reduce(row(total), exps, AX.X, ALU.add))
                settle()
                step(ve.reciprocal(row(total), row(total)))
                settle()
                step(ve.tensor_scalar(probs, exps, row(total), None, ALU.mult))
                settle()

            ve.wait_ge(s_rl, 1)
            step(ve.tensor_tensor(row(16, E0), PS[1][0:1, 0:E0], row(8, E0), ALU.add))
            settle()
            softmax(row(16, E0), row(24, E0), row(32, E0), 0, 1, 4, 1)
            step(ve.tensor_scalar(row(56, E0), row(32, E0), float(N), 1e-30, ALU.mult, ALU.max))
            settle()
            step(ve.reciprocal(row(64, E0), row(56, E0)))
            settle()
            step(ve.tensor_scalar(row(72, E0), row(64, E0), float(CAP), 1.0, ALU.mult, ALU.min))
            settle()
            step(ve.tensor_tensor(row(40, E0), row(32, E0), row(72, E0), ALU.mult))
            settle()
            softmax(row(40, E0), row(48, E0), row(80, E0), 2, 3, 5, 2)
            step(ve.tensor_scalar(row(96, E0), IOTA[0:1, 0:E0], -1.0, float(E0), ALU.mult, ALU.add))
            for k in range(2):
                step(ve.tensor_reduce(row(110 + k), row(80, E0), AX.X, ALU.max))
                settle()
                step(ve.scalar_tensor_tensor(row(88, E0), row(80, E0), row(110 + k), row(96, E0),
                                             ALU.is_equal, ALU.mult))
                settle()
                step(ve.tensor_reduce(row(114 + k), row(88, E0), AX.X, ALU.max))
                settle()
                step(ve.tensor_scalar(row(116 + k), row(114 + k), -1.0, float(E0), ALU.mult, ALU.add))
                step(ve.tensor_scalar(row(88, E0), row(96, E0), row(114 + k), -2.0, ALU.is_equal, ALU.mult))
                settle()
                step(ve.tensor_tensor(row(80, E0), row(80, E0), row(88, E0), ALU.add))
                settle()
            ve.tensor_copy(EXI[0:1, 0:2], row(116, 2)).then_inc(s_ex, 1)
            ve.tensor_tensor(row(112), row(111), row(110), ALU.subtract).then_inc(s_e1, 1)
            ve.wait_ge(s_x1, 3)
            step(ve.tensor_scalar(row(118), row(113), 1.0, None, ALU.add))
            settle()
            step(ve.reciprocal(row(120), row(118)))
            settle()
            ve.tensor_tensor(row(121), row(120), row(113), ALU.mult).then_inc(s_wab, 1)
            ve.wait_ge(s_wabp, 1)
            step(ve.tensor_copy(WAB[:, :], PS[2][:, 0:2]))
            settle()
            ve.wait_ge(s_fw, 128)
            for k in range(2):
                w2s = W2S[:, k * FC0 * D:(k + 1) * FC0 * D]
                ve.tensor_scalar(w2s, w2s, WAB[:, k:k + 1], None, ALU.mult)
            step(ve.tensor_scalar(BC[:, :], B2P[:, 0:D], WAB[:, 0:1], None, ALU.mult))
            settle()
            ve.scalar_tensor_tensor(BC[:, :], B2P[:, D:2 * D], WAB[:, 1:2], BC[:, :], ALU.mult, ALU.add)\
                .then_inc(s_fws, 1)
            ve.wait_ge(s_fws, 1)

            def take_ffn(i):
                for u in range(U):
                    ve.wait_ge(s_mm, U + seq_mm[FA] + U * i + u + 1)
                    ve.tensor_tensor(slot(YT, u), slot_o(u), BC[:, :], ALU.add).then_inc(s_od, 1)
                    last = normalized(slot(YN, u), i, u)
                step(last)
                settle()
                for u in range(U):
                    last = ve.tensor_tensor(slot(YT, u), slot(YT, u), slot(YN, u), ALU.add)
                step(last)
                hold(s_dv, dve.now())
                for u in range(U):
                    last = ve.bn_stats(ST7[:, u * 6:(u + 1) * 6], slot(YT, u))
                step(last)
                hold(s_dv, dve.now())
                for u in range(U):
                    last = ve.bn_aggr(MV7[:, 2 * u:2 * u + 2], ST7[:, u * 6:(u + 1) * 6])
                last.then_inc(s_v7, 1)
                ve.wait_ge(s_v7, i + 1)
                ve.wait_ge(s_d7, i + 1)
                step(ve.reciprocal(R7[:, :], NR7[:, :]))
                settle()
                for u in range(U):
                    last = ve.tensor_scalar(slot(YT, u), slot(YT, u), MV7[:, 2 * u:2 * u + 1], R7[:, u:u + 1],
                                            ALU.subtract, ALU.mult)
                step(last)
                settle()
                for other, op in ((GAM, ALU.mult), (BET, ALU.add)):
                    for u in range(U):
                        last = ve.tensor_tensor(slot(YT, u), slot(YT, u), other[:, :], op)
                    step(last)
                    settle()
                for u in range(U):
                    last = ve.tensor_tensor(tile(X, i, u), tile(X, i, u), slot(YT, u), ALU.add)
                step(last)
                moments(i)

            ahead(FA, normalized, take_ffn, 11)
            reciprocal_deviation(3)

            def take_t4(i):
                for u in range(U):
                    ve.wait_ge(s_mm, U + seq_mm[T4] + U * i + u + 1)
                    ve.tensor_scalar(tile(ACC, i, u), slot_o(u), DINV[:, bass.ds(U * i + u, 1)], None, ALU.mult)\
                        .then_inc(s_od, 1)

            ahead(T4, normalized, take_t4, 0)
            ve.wait_ge(s_io, 1)
            ve.wait_ge(s_stg, U + seq_st[T4] + NT)
            ve.wait_ge(s_xtp, U + seq_in[T4] + NT)
            sum_edges(2, None, False)
            ve.wait_ge(s_free, G + 3 * NC)

            def hidden(into, i, u):
                return ve.scalar_tensor_tensor(into, tile(ACC, i, u), DINV[:, bass.ds(U * i + u, 1)], BA[:, :],
                                               ALU.mult, ALU.add)

            def squares(i):
                for u in range(U):
                    ve.wait_ge(s_xin, seq_in[T5] + U * i + u + 1)
                    last = ve.scalar_tensor_tensor(slot(TT, u), slot(XIN, u), 1.0, slot(XIN, u), ALU.mult, ALU.mult,
                                                   accum_out=SSQ[:, bass.ds(U * i + u, 1)])
                last.then_inc(s_sq, 1)

            def take_t5(i):
                ve.wait_ge(s_nr, i + 1)
                nr = NRV[:, ts(i, U)]
                step(ve.tensor_scalar(nr, nr, 1e-12, None, ALU.max))
                hold(s_dv, dve.now())
                step(ve.reciprocal(nr, nr))
                settle()
                step(ve.tensor_tensor(nr, nr, DINV[:, ts(i, U)], ALU.mult))
                settle()
                for u in range(U):
                    ve.wait_ge(s_mm, U + seq_mm[T5] + U * i + u + 1)
                    ve.tensor_scalar(tile(ACC, i, u), slot_o(u), NRV[:, bass.ds(U * i + u, 1)], None, ALU.mult)\
                        .then_inc(s_od, 1)

            feed(T5, 0, hidden)
            squares(0)

            def body_t5(i):
                ve.wait_ge(s_sq, i + 1)
                feed(T5, i + 1, hidden)
                squares(i + 1)
                take_t5(i)
            loop(0, NI - 1, 3, body_t5)
            take_t5(NI - 1)
            ve.wait_ge(s_stg, U + seq_st[T5] + NT)
            ve.wait_ge(s_xtp, U + seq_in[T5] + NT)
            sum_edges(3, None, False)
            ve.wait_ge(s_free, G + 4 * NC)

            def finish_gnn(i):
                for u in range(U):
                    normalized(slot(TT, u), i, u)
                    last = ve.scalar_tensor_tensor(slot(TU, u), tile(ACC, i, u), DINV[:, bass.ds(U * i + u, 1)],
                                                   BB[:, :], ALU.mult, ALU.add)
                step(last)
                settle()
                for u in range(U):
                    last = ve.tensor_tensor(slot(TT, u), slot(TT, u), slot(TU, u), ALU.add)
                step(last)
                settle()
                for u in range(U):
                    last = ve.tensor_tensor(tile(X, i, u), tile(X, i, u), slot(TT, u), ALU.add)
                step(last)
                moments(i)

            loop(0, NI, 6, finish_gnn)
            reciprocal_deviation(4)
            ve.sem_inc(s_wfree, 1)

            loop(0, NI, 0, lambda i: feed_normalized(SG, i))
            ve.wait_ge(s_nid, 2)
            step(ve.tensor_copy(NID, NIDI.bitcast(i32)))
            step(ve.tensor_copy(E8, E8I.bitcast(i32)))
            ve.wait_ge(s_gate, U + NT)
            step(ve.tensor_tensor(by_expert(LG), by_expert(PS[4][:, 0:NX]),
                                  GBS[:, :].rearrange("p (a e) -> p a e", a=1).to_broadcast([P, NT, E1]), ALU.add))
            settle()
            step(ve.tensor_reduce(MX, by_expert(LG), AX.X, ALU.max))
            settle()
            ve.tensor_tensor(by_expert(TA), by_expert(LG), per_tile(MX, E1), ALU.subtract).then_inc(s_ei, 1)
            step(ve.tensor_tensor(by_expert(OH), by_expert(LG), per_tile(MX, E1), ALU.is_equal))
            step(ve.tensor_scalar(PA, E8, -1.0, float(E1), ALU.mult, ALU.add))
            settle()
            step(ve.tensor_tensor(OH, OH, PA, ALU.mult))
            settle()
            step(ve.tensor_reduce(IXF, by_expert(OH), AX.X, ALU.max))
            settle()
            step(ve.tensor_scalar(IXF, IXF, -1.0, float(E1), ALU.mult, ALU.add))
            settle()
            step(ve.tensor_tensor(by_expert(OH), by_expert(E8), per_tile(IXF, E1), ALU.is_equal))
            settle()
            ve.tensor_tensor(by_expert(OH), by_expert(OH), per_tile(VALID[:, :], E1), ALU.mult).then_inc(s_oh, 1)
            ve.wait_ge(s_eo, 1)
            step(ve.tensor_reduce(SE, by_expert(TA), AX.X, ALU.add))
            settle()
            step(ve.reciprocal(PRB, SE))
            ve.wait_ge(s_cum, 1)
            step(ve.tensor_copy(TO, PS[6][:, 0:NX]))
            step(ve.tensor_copy(PA, PS[6][:, 0:NX]))
            settle()
            a, b, shift = PA, PB_, 1
            while shift < NT:
                w = shift * E1
                ve.tensor_copy(b[:, 0:w], a[:, 0:w])
                step(ve.tensor_tensor(b[:, w:NX], a[:, w:NX], a[:, 0:NX - w], ALU.add))
                settle()
                a, b, shift = b, a, 2 * shift
            step(ve.tensor_tensor(a, a, TO, ALU.subtract))
            settle()
            step(ve.tensor_tensor(CU, a, PS[5][:, 0:NX], ALU.add))
            settle()
            step(ve.tensor_tensor(CU, CU, OH, ALU.mult))
            settle()
            step(ve.tensor_reduce(POS, by_expert(CU), AX.X, ALU.add))
            settle()
            step(ve.tensor_scalar(KEP, POS, float(CAP), None, ALU.is_le))
            step(ve.tensor_scalar(SLT, POS, -1.0, 0.0, ALU.add, ALU.max))
            settle()
            step(ve.tensor_tensor(KEP, KEP, VALID[:, :], ALU.mult))
            step(ve.tensor_scalar(SLT, SLT, float(CAP - 1), None, ALU.min))
            settle()
            step(ve.scalar_tensor_tensor(SLT, IXF, float(CAP), SLT, ALU.mult, ALU.add))
            step(ve.tensor_scalar(DMP, NID, float(DUMP), None, ALU.add))
            settle()
            step(ve.tensor_copy(IDY[:, :], SLT))
            step(ve.tensor_tensor(SLT, SLT, DMP, ALU.subtract))
            step(ve.tensor_tensor(SCL, PRB, KEP, ALU.mult))
            settle()
            step(ve.tensor_tensor(SLT, SLT, KEP, ALU.mult))
            settle()
            step(ve.tensor_tensor(SLT, SLT, DMP, ALU.add))
            settle()
            step(ve.tensor_copy(IDS[:, :], SLT))
            settle()
            ve.sem_inc(s_ix, 1)
            for t in range(NT):
                if t >= U:
                    ve.wait_ge(s_sc[t % U], 16 * (t // U))
                normalized(slot(XIN, t % U), 0, t).then_inc(s_xin, 1)

            for e in range(E1):
                k = e % 2
                for r in range(RB):
                    rows = min(P, CAP - r * P)
                    ve.wait_ge(s_1d, RB * e + r + 1)
                    if r == 0 and e >= 2:
                        ve.wait_ge(s_ys[k], 32 * (e // 2))
                    ve.tensor_tensor(YS[0:rows, (k * RB + r) * D:(k * RB + r + 1) * D],
                                     PS[BK + r % BK][0:rows, 0:D], B2L[k][0:rows, :], ALU.add)\
                        .then_inc(s_1y, 1)

            ve.wait_ge(s_1y, RB * E1)
            for g in range(NI):
                for u in range(U):
                    t = U * g + u
                    ve.wait_ge(s_yg[u], 16 * (g + 1))
                    ve.tensor_scalar(slot(YV, u), slot(XIN, u), SCL[:, t:t + 1], None, ALU.mult).then_inc(s_yu, 1)
                ve.wait_ge(s_yu, U * (g + 1))
                for u in range(U):
                    ve.tensor_scalar(slot(YC, u), slot(YV, u), -1e4, 1e4, ALU.max, ALU.min)
                    ve.tensor_tensor(slot(YE, u), slot(YV, u), slot(YV, u), ALU.is_equal)
                    last = ve.tensor_scalar(slot(YM, u), slot(YV, u), 0.0, 0.0, ALU.mult, ALU.is_equal)
                step(last)
                settle()
                for u in range(U):
                    last = ve.tensor_tensor(slot(YC, u), slot(YC, u), slot(YE, u), ALU.mult)
                step(last)
                settle()
                for u in range(U):
                    last = ve.copy_predicated(slot(YC, u), slot(YM, u), slot(YV, u))
                step(last)
                settle()
                for u in range(U):
                    t = U * g + u
                    ve.tensor_tensor(X[:, t * D:(t + 1) * D], X[:, t * D:(t + 1) * D], slot(YC, u), ALU.add)\
                        .then_inc(s_fin, 1)


_INS = ['x', 'src', 'dst', 'edge_weight', 'L0_gnn_W6', 'L0_gnn_b6', 'L0_gnn_W7', 'L0_gnn_b7', 'L0_gnn_Wp', 'L0_gnn_bp',
        'L0_ffn_Wr', 'L0_ffn_br', 'L0_ffn_W1', 'L0_ffn_b1', 'L0_ffn_W2', 'L0_ffn_b2', 'L0_ffn_gamma', 'L0_ffn_beta',
        'L1_gnn_W1', 'L1_gnn_b1', 'L1_gnn_W2', 'L1_gnn_b2', 'L1_ffn_gate_w', 'L1_ffn_gate_b', 'L1_ffn_w1', 'L1_ffn_b1',
        'L1_ffn_w2', 'L1_ffn_b2']


def kernel(**inputs):
    import numpy as _np
    import concourse.bacc as _bacc
    from concourse import mybir as _mybir
    from concourse.bass_utils import run_bass_kernel_spmd as _run

    nc = _bacc.Bacc("TRN2", target_bir_lowering=False, num_devices=1)
    arrays, args = {}, []
    for name in _INS:
        a = _np.ascontiguousarray(inputs[name])
        arrays[f"in_{name}"] = a
        args.append(nc.dram_tensor(f"in_{name}", a.shape, _mybir.dt.from_np(a.dtype), kind="ExternalInput").ap())
    args.append(nc.dram_tensor("out_x", (N, D), _mybir.dt.float32, kind="ExternalOutput").ap())
    gnn_ffn(nc, *args)
    r = _run(nc, [arrays], core_ids=[0])
    return r.results[0]["out_x"]
```

```python
import concourse.bass as bass
from concourse import mybir
from contextlib import ExitStack

N = 6250
D = 256
NE = 106250
P = 128
NT = -(-N // P)
NP = NT * P
LAST = N - (NT - 1) * P
U = 7
NI = NT // U
KC = D // P
ROW1 = D + 4
G = 16
NB = -(-NE // (P * P))
NC = -(-(-(-NE // P)) // G) * G
GI = NC // G
Q = 4
HB = 4
NG = -(-NE // (P * P)) * P // Q
BK = 4
EC = NB * P
E0, F0 = 8, 512
E1, F1 = 8, 1024
FC0, FC1 = F0 // P, F1 // P
CAP = -(-(5 * N) // (4 * E1))
RB = -(-CAP // P)
LASTR = CAP - (RB - 1) * P
HALF = (CAP + 1) // 2
DUMP = E1 * CAP
CLEAR = -(-DUMP // (16 * P))
GT = U * P
WORKC = 14336
EPS_LN = 1e-5
EPS_DEG = 1e-12


class Count:

    def __init__(self, sem):
        self.sem, self.base, self.k, self.i, self.per = sem, 0, 0, None, 0

    def tell(self, ins):
        ins.then_inc(self.sem, 1)
        self.k += 1
        return ins

    def now(self):
        v = self.base + self.k
        return v if self.i is None else v + self.per * self.i

    def enter(self, i, per):
        self.base += self.k
        self.k, self.i, self.per = 0, i, per

    def check(self):
        assert self.k == self.per, (self.k, self.per)

    def leave(self, trips):
        self.base += self.per * trips
        self.k, self.i = 0, None


def gnn_ffn(nc, x, src, dst, edge_weight, W6, b6, W7, b7, Wp, bp, Wr, br, W1a, b1a, W2a, b2a, gamma, beta,
            G1, g1, G2, g2, gate_w, gate_b, w1, b1, w2, b2, out):
    f32, i32, u32, i16, bf16 = (mybir.dt.float32, mybir.dt.int32, mybir.dt.uint32, mybir.dt.int16, mybir.dt.bfloat16)
    ALU, ACT, AX, ENG = mybir.AluOpType, mybir.ActivationFunctionType, mybir.AxisListType, mybir.EngineType

    def ts(t, w):
        return bass.ds(t * w, w)

    def a_tile(t):
        return t.with_bounds(min_val=0, max_val=NT - 1)

    tab1 = nc.dram_tensor("tab1", [NP, ROW1], f32).ap()
    tab2 = nc.dram_tensor("tab2", [NP, D], f32).ap()
    tab3 = nc.dram_tensor("tab3", [NP, D], f32).ap()
    tab4 = nc.dram_tensor("tab4", [NP, D], f32).ap()
    slots_x = nc.dram_tensor("slots_x", [DUMP + NP, D], f32).ap()
    slots_y = nc.dram_tensor("slots_y", [DUMP, D], f32).ap()
    meta_d = nc.dram_tensor("meta_d", [2, EC], i32).ap()
    tab1_v = tab1.rearrange("(t p) d -> p t d", p=P)

    ctx = ExitStack()
    with ctx:
        def sb(name, shape, dt=f32):
            return ctx.enter_context(nc.sbuf_tensor(name, shape, dt))

        def sem(name):
            return ctx.enter_context(nc.semaphore(name))

        X = sb("X", [P, NT * D])
        ACC = sb("ACC", [P, NT * D])
        WORK = sb("WORK", [P, WORKC])
        SRC = sb("SRC", [P, EC], i32)
        DST = sb("DST", [P, EC])
        EW = sb("EW", [P, EC])
        NRM = sb("NRM", [P, EC])
        XIN = sb("XIN", [P, U * D])
        XT = sb("XT", [P, U * D])
        WA = sb("WA", [P, KC * D])
        WB = sb("WB", [P, KC * D])
        WC = sb("WC", [P, KC * D])
        BA = sb("BA", [P, D])
        BB = sb("BB", [P, D])
        BC = sb("BC", [P, D])
        GAM = sb("GAM", [P, D])
        BET = sb("BET", [P, D])
        IDN = sb("IDN", [P, P])
        ONE = sb("ONE", [P, P])
        TRI = sb("TRI", [P, P])
        FIRST = sb("FIRST", [1, NG], i32)
        SPAN = sb("SPAN", [1, NG], i32)
        VALID = sb("VALID", [P, NT])
        MV = sb("MV", [P, NT * 2])
        RS = sb("RS", [P, NT])
        SD = sb("SD", [P, NT])
        DEGI = sb("DEGI", [P, NT])
        DINV = sb("DINV", [P, NT])
        DOX = sb("DOX", [P, NT * 4])
        ST7 = sb("ST7", [P, U * 6])
        MV7 = sb("MV7", [P, U * 2])
        R7 = sb("R7", [P, U])
        NR7 = sb("NR7", [P, U])
        SSQ = sb("SSQ", [P, NT])
        NRV = sb("NRV", [P, NT])
        IDX = sb("IDX", [P, G], i32)
        IDS = sb("IDS", [P, NT], i32)
        IDY = sb("IDY", [P, NT], i32)
        DIE = sb("DIE", [P, 2 * Q])
        DIX = sb("DIX", [P, Q])
        DRT = sb("DRT", [P, 2 * Q])
        DRI = sb("DRI", [P, 2 * Q])
        EPSL = sb("EPSL", [P, 1])
        EPSD = sb("EPSD", [P, 1])
        SM = sb("SM", [1, 128])
        EXI = sb("EXI", [1, 4], i32)
        WAB = sb("WAB", [P, 2])
        MNT = sb("MNT", [P, KC])
        WRS = sb("WRS", [P, KC * E0])
        GWS = sb("GWS", [P, KC * E1])
        CNT = sb("CNT", [P, NT])
        GBS = sb("GBS", [P, E1])
        B1S = sb("B1S", [P, 2 * FC0])
        B1L = sb("B1L", [P, E1 * FC1])

        PS = [ctx.enter_context(nc.psum_tensor(f"PS{b}", [P, 512], f32)) for b in range(8)]

        def slot_t(u):
            return PS[u % BK][:, 0:D]

        def slot_o(u):
            return PS[BK + u % BK][:, 0:D]

        def gap(u):
            return BK if u >= BK else U - last_use(u) + u

        def last_use(u):
            return max(v for v in range(U) if v % BK == u % BK)

        at = [0]

        def carve(n):
            at[0] += n
            return ACC[:, at[0] - n:at[0]]
        E_SRC, E_DST = carve(EC).bitcast(i32), carve(EC).bitcast(i32)
        E_W, E_SF, E_DF = carve(EC), carve(EC), carve(EC)
        TEMP, TEMP_I = carve(2 * NB), carve(2 * NB).bitcast(i32)
        S_HI, S_LO, D_HI, D_LO = (carve(EC // 2).bitcast(i16) for _ in range(4))
        T_I = carve(EC).bitcast(i32)
        W_1, W_2, W_3 = E_W, E_SF, E_DF
        NH = 8 * NT
        DLO, HI = carve(HB * Q * P // 2).bitcast(bf16), carve(HB * Q * NH // 2).bitcast(bf16)
        SLO = XIN[:, 0:HB * Q * P // 2].bitcast(bf16)
        HT = XIN[:, 1024:1024 + 6 * NT]
        assert at[0] <= NT * D
        ROWS = [WORK[:, j * ROW1:(j + 1) * ROW1] for j in range(G)]
        DIB = WORK[:, G * ROW1:G * ROW1 + NP + P]
        DIB_END = DIB[:, NP:NP + P]
        IOTA = WORK[:, G * ROW1 + NP + P:G * ROW1 + NP + P + (NP + P) // 2].bitcast(i16)
        ZB = WORK[:, WORKC - D:WORKC]
        ZB16 = ZB.bitcast(bf16)
        ROWDG = [WORK[:, 2048:2560], WORK[:, 2560:3072]]
        MM = [XIN[:, 0:Q * P], XIN[:, Q * P:2 * Q * P], XIN[:, 2 * Q * P:3 * Q * P], XT[:, 0:Q * P]]
        DSEL = XT[:, Q * P:3 * Q * P]
        META = XT[0:1, :].bitcast(i32)
        GROUP1, GROUPN = XIN[0:1, 0:NG], XIN[0:1, NG:2 * NG]
        TT = WORK[:, 0:U * D]
        TU = WORK[:, U * D:2 * U * D]
        W1S = WORK[:, 0:2 * KC * F0]
        W2S = WORK[:, 2048:2048 + 2 * FC0 * D]
        XT0 = WORK[:, 4096:4096 + KC * GT]
        H0 = WORK[:, 5888:5888 + 2 * FC0 * GT]
        B2P = ACC[:, 0:2 * D]
        YT = ACC[:, 512:512 + U * D]
        YN = ACC[:, 2560:2560 + U * D]
        H1 = WORK[:, 0:FC1 * CAP]
        XT1 = WORK[:, 7824:7824 + KC * CAP]
        YS = WORK[:, 9780:9780 + 2 * RB * D]
        W1L = ACC[:, 0:2 * KC * F1]
        W2L = ACC[:, 4096:4096 + 2 * FC1 * D]
        RBF = ACC[:, 8192:8192 + 2 * RB * D]
        B2L = [GAM, BET]
        YV = WORK[:, 0:U * D]
        YC = WORK[:, U * D:2 * U * D]
        YE = WORK[:, 2 * U * D:3 * U * D]
        YM = WORK[:, 3 * U * D:4 * U * D].bitcast(i32)
        NX = NT * E1
        LG, TA, OH, CU, TO, PA, PB_, E8, E8I = (WORK[:, k * NX:(k + 1) * NX] for k in range(9))
        MX, SE, PRB, IXF, POS, KEP, SLT, DMP, NIDI, NID = (WORK[:, 9 * NX + k * 64:9 * NX + k * 64 + NT]
                                                          for k in range(10))
        SCL = NRM[:, 0:NT]

        s_pad, s_const = sem("pads_set"), sem("constants_ready")
        s_x, s_e, s_w, s_par = sem("x_loaded"), sem("edges_loaded"), sem("weights_loaded"), sem("parameters_loaded")
        s_ef, s_et, s_es = sem("edges_as_floats"), sem("edges_transposed"), sem("edge_columns_ready")
        s_meta, s_metad, s_metal = sem("chunk_tiles_ready"), sem("chunk_tiles_stored"), sem("chunk_tiles_loaded")
        s_hot, s_hist, s_histd = sem("onehots_ready"), sem("onehots_used"), sem("histograms_done")
        s_hotw, s_hotp = sem("weighted_onehots_ready"), sem("more_weighted_onehots_ready")
        s_deg, s_cnt, s_root = sem("degrees_ready"), sem("counts_ready"), sem("count_roots_ready")
        s_diag, s_dib, s_dibd = sem("diagonals_ready"), sem("degree_rows_summed"), sem("degree_rows_ready")
        s_dost, s_accz, s_zf = sem("degree_column_stored"), sem("sums_cleared"), sem("slots_cleared")
        s_var, s_std = sem("variances_ready"), sem("deviations_ready")
        s_xin, s_xtp, s_xt = sem("tile_in"), sem("tile_transposed"), sem("transposed_tile_copied")
        s_mm, s_od, s_stg = sem("product_ready"), sem("product_taken"), sem("tile_stored")
        s_st = [sem(f"store_{u}") for u in range(U)]
        s_free, s_tick = sem("rows_used"), sem("pool_ticks")
        s_row = [sem(f"rows_gathered_{j}") for j in range(G)]
        s_idx = [sem(f"indices_staged_{q}") for q in range(G // Q)]
        s_m, s_me, s_mx = sem("first_tile_selected"), sem("second_tile_selected"), sem("more_tiles_selected")
        s_p, s_pe = sem("first_sum_ready"), sem("more_sums_ready")
        s_joined, s_aj = sem("sums_joined"), sem("more_sums_joined")
        s_span = sem("spans_ready")
        s_di, s_dr = sem("incoming_degrees_ready"), sem("degree_roots_ready")
        s_dx, s_dj = sem("more_degrees_selected"), sem("more_degrees_joined")
        s_nm, s_scl = sem("norms_ready"), sem("rows_scaled")
        s_mean, s_rl, s_e1, s_x1 = sem("mean_ready"), sem("route_logits"), sem("exp_input"), sem("exp_done")
        s_ex, s_wab, s_wabp = sem("experts_chosen"), sem("expert_weights_row"), sem("expert_weights_spread")
        s_fw, s_fws = sem("chosen_experts_loaded"), sem("chosen_experts_scaled")
        s_up, s_hid = sem("up_product"), sem("hidden_ready")
        s_v7, s_d7 = sem("variances_of_7"), sem("deviations_of_7")
        s_w2, s_io, s_sq, s_nr = sem("second_weights_loaded"), sem("iota_ready"), sem("squares_ready"), sem("lengths_ready")
        s_gate = sem("gate_read")
        s_b1 = sem("second_biases_loaded")
        s_wfree, s_nid = sem("work_free"), sem("numbers_ready")
        s_ei, s_eo = sem("gate_exp_input"), sem("gate_exp_done")
        s_oh, s_cum, s_ix = sem("choices_ready"), sem("positions_summed"), sem("slots_known")
        s_sct = [sem(f"scattered_{u}") for u in range(U)]
        s_lw = [sem(f"expert_loaded_{k}") for k in range(2)]
        s_1t, s_1x, s_1u = sem("rows_transposed"), sem("rows_copied"), sem("up1_product")
        s_1h, s_1d, s_1y = sem("hidden1_ready"), sem("down1_product"), sem("y_staged")
        s_ys = [sem(f"y_stored_{k}") for k in range(2)]
        s_yg = [sem(f"y_gathered_{u}") for u in range(U)]
        s_yu, s_fin, s_out = sem("y_used"), sem("tile_final"), sem("out_stored")
        s_vtick = sem("vector_ticks")
        s_dv = sem("vector_steps")
        dve = Count(s_dv)

        block = ctx.enter_context(nc.Block())

        T1, T2, T3, RT, FA, T4, T5, SG = range(8)
        seq_in = {k: NT * n for n, k in enumerate([T1, T2, T3, RT, FA, T4, T5, SG])}
        seq_xt = {k: NT * n for n, k in enumerate([T1, T2, T3, FA, T4, T5, SG])}
        seq_mm = {k: NT * n for n, k in enumerate([T1, T2, T3, FA, T4, T5])}
        seq_st = {k: NT * n for n, k in enumerate([T1, T2, T4, T5])}
        NU = 2 * FC0 * 2
        NU1 = FC1 * 2
        PARTS = ((0, RB - 1, P), (RB - 1, RB, LASTR))
        ND = -(-NT // 4)

        def per_tile(v, width):
            return v.rearrange("p (t a) -> p t a", a=1).to_broadcast([P, NT, width])

        def by_expert(v):
            return v.rearrange("p (t e) -> p t e", e=E1)

        def by_block(v):
            return v.rearrange("p (c n) -> p c n", c=KC)

        @block.sync
        def _(sp):
            full = NT - 1
            sp.wait_ge(s_pad, 4)
            nb, blk = NE // (P * P), P * P
            rest = NE - nb * blk
            rr, tail = rest // P, rest % P
            for sb_t, dr in ((E_SRC, src), (E_DST, dst), (E_W, edge_weight)):
                sp.dma_start(sb_t[:, 0:nb * P].rearrange("p (k j) -> p k j", j=P),
                             dr[0:nb * blk].rearrange("(k p j) -> p k j", p=P, j=P)).then_inc(s_e, 16)
                sp.dma_start(sb_t[0:rr, nb * P:nb * P + P],
                             dr[nb * blk:nb * blk + rr * P].rearrange("(p j) -> p j", j=P)).then_inc(s_e, 16)
                sp.dma_start(sb_t[rr:rr + 1, nb * P:nb * P + tail],
                             dr[nb * blk + rr * P:NE].rearrange("(p j) -> p j", p=1)).then_inc(s_e, 16)
            sp.dma_start(X[:, 0:full * D].rearrange("p (t d) -> p t d", d=D),
                         x[0:full * P, :].rearrange("(t p) d -> p t d", p=P)).then_inc(s_x, 16)
            sp.dma_start(X[0:LAST, full * D:NT * D], x[full * P:N, :]).then_inc(s_x, 16)
            for sb_t, dr in ((WA, W6), (WB, W7), (WC, Wp)):
                sp.dma_start(sb_t[:, :].rearrange("p (k d) -> p k d", k=KC),
                             dr.rearrange("(k p) d -> p k d", p=P)).then_inc(s_w, 16)
            for sb_t, dr in ((BA, b6), (BB, b7), (BC, bp), (GAM, gamma), (BET, beta)):
                sp.dma_start(sb_t[:, :], dr.rearrange("(a d) -> a d", a=1).to_broadcast([P, D])).then_inc(s_par, 16)
            sp.dma_start(GBS[:, :], gate_b.rearrange("(a d) -> a d", a=1).to_broadcast([P, E1])).then_inc(s_par, 16)
            sp.dma_start(WRS[:, :].rearrange("p (k e) -> p k e", k=KC),
                         Wr.rearrange("(k p) e -> p k e", p=P)).then_inc(s_par, 16)
            sp.dma_start(GWS[:, :].rearrange("p (k e) -> p k e", k=KC),
                         gate_w.rearrange("(k p) e -> p k e", p=P)).then_inc(s_par, 16)
            sp.dma_start(SM[0:1, 8:8 + E0], br.rearrange("(a e) -> a e", a=1)).then_inc(s_par, 16)

            sp.wait_ge(s_meta, 1)
            with nc.allow_non_contiguous_dma(reason="2 x 896 elements, once"):
                for k in range(2):
                    sp.dma_start(meta_d[k:k + 1, :].rearrange("a (k p) -> p (a k)", p=P),
                                 T_I[:, k * NB:(k + 1) * NB]).then_inc(s_metad, 16)
            sp.sem_inc(s_stg, U)

            def store_table(k, tab, source):
                n, m = seq_mm[k], seq_st[k] // U
                with sp.Fori(0, NI) as i:
                    for u in range(U):
                        sp.wait_ge(s_od, U + n + U * i + u + 1)
                        sp.dma_start(tab[bass.ds((U * i + u) * P, P), 0:D], source(i, u)).then_inc(s_st[u], 16)
                    for u in range(U):
                        sp.wait_ge(s_st[u], 16 * (m + i + 1))
                        sp.sem_inc(s_stg, 1)

            def staged(i, u):
                return TT[:, u * D:(u + 1) * D]

            def in_acc(i, u):
                return ACC[:, ts(U * i + u, D)]

            def stage_indices(layer):
                def iteration(i):
                    for q in range(G // Q):
                        if layer or not isinstance(i, int):
                            for k in range(Q):
                                sp.wait_ge(s_row[q * Q + k], 16 * (GI * layer + i))
                        sp.dma_start(IDX[:, q * Q:(q + 1) * Q], SRC[:, bass.ds(G * i + q * Q, Q)])\
                            .then_inc(s_idx[q], 16)

                if not layer:
                    iteration(0)
                with sp.Fori(0 if layer else 1, GI) as i:
                    iteration(i)

            store_table(T1, tab1, staged)
            sp.wait_ge(s_metad, 32)
            sp.wait_ge(s_mm, U + seq_mm[T1] + NT)
            sp.dma_start(META.rearrange("a (r c) -> a r c", r=2),
                         meta_d.rearrange("(a r) c -> a r c", a=1)).then_inc(s_metal, 16)
            sp.wait_ge(s_deg, 1)
            sp.dma_start(tab1_v[:, :, D:ROW1], DOX[:, :].rearrange("p (t c) -> p t c", c=4)).then_inc(s_dost, 16)
            sp.wait_ge(s_const, 11)
            for k in range(CLEAR):
                sp.dma_start(slots_x[k * 16 * P:(k + 1) * 16 * P, :].rearrange("(t p) d -> p t d", p=P),
                             ZB.rearrange("p (a d) -> p a d", a=1).to_broadcast([P, 16, D])).then_inc(s_zf, 16)
            with nc.allow_non_contiguous_dma(reason="8192 elements, once"):
                for e in range(E1):
                    sp.dma_start(B1L[:, e * FC1:(e + 1) * FC1], b1[e].rearrange("(f p) -> p f", p=P))\
                        .then_inc(s_b1, 16)
            stage_indices(0)
            store_table(T2, tab2, staged)
            stage_indices(1)

            sp.wait_ge(s_ex, 1)
            _, chosen = nc.values_load_multi_w_load_instructions(
                EXI[0:1, 0:2], engines=(ENG.SP,), min_val=0, max_val=E0 - 1,
                skip_runtime_bounds_check_because="an argmax over the experts")
            for k, e in enumerate(chosen):
                sp.dma_start(W1S[:, k * KC * F0:(k + 1) * KC * F0].rearrange("p (k f) -> p k f", k=KC),
                             W1a[bass.ds(e, 1), :, :].rearrange("e (k p) f -> p (e k) f", p=P)).then_inc(s_fw, 16)
                sp.dma_start(W2S[:, k * FC0 * D:(k + 1) * FC0 * D].rearrange("p (k f) -> p k f", k=FC0),
                             W2a[bass.ds(e, 1), :, :].rearrange("e (k p) f -> p (e k) f", p=P)).then_inc(s_fw, 16)
                sp.dma_start(B2P[:, k * D:(k + 1) * D], b2a[bass.ds(e, 1), :].to_broadcast([P, D])).then_inc(s_fw, 16)
                with nc.allow_non_contiguous_dma(reason="512 elements, once"):
                    sp.dma_start(B1S[:, k * FC0:(k + 1) * FC0],
                                 b1a[bass.ds(e, 1), :].rearrange("e (f p) -> p (e f)", p=P)).then_inc(s_fw, 16)
            for sb_t, dr in ((WA, G1), (WB, G2)):
                sp.dma_start(sb_t[:, :].rearrange("p (k d) -> p k d", k=KC),
                             dr.rearrange("(k p) d -> p k d", p=P)).then_inc(s_w2, 16)
            for sb_t, dr in ((BA, g1), (BB, g2)):
                sp.dma_start(sb_t[:, :], dr.rearrange("(a d) -> a d", a=1).to_broadcast([P, D])).then_inc(s_w2, 16)

            store_table(T4, tab3, in_acc)
            stage_indices(2)
            store_table(T5, tab4, in_acc)
            stage_indices(3)

            def store_y(e):
                k = e % 2
                sp.wait_ge(s_1y, RB * (e + 1))
                for r0, r1, rows in PARTS:
                    sp.dma_start(slots_y[e * CAP + r0 * P:e * CAP + (r1 - 1) * P + rows, :]
                                 .rearrange("(r p) d -> p r d", p=rows),
                                 YS[0:rows, (k * RB + r0) * D:(k * RB + r1) * D].rearrange("p (r d) -> p r d", d=D))\
                        .then_inc(s_ys[k], 16)

            def load_expert(e):
                k = e % 2
                sp.dma_start(W1L[:, k * KC * F1:(k + 1) * KC * F1].rearrange("p (k f) -> p k f", k=KC),
                             w1[e].rearrange("(k p) f -> p k f", p=P)).then_inc(s_lw[k], 16)
                sp.dma_start(W2L[:, k * FC1 * D:(k + 1) * FC1 * D].rearrange("p (k f) -> p k f", k=FC1),
                             w2[e].rearrange("(k p) f -> p k f", p=P)).then_inc(s_lw[k], 16)
                sp.dma_start(B2L[k][:, :], b2[e:e + 1, :].to_broadcast([P, D])).then_inc(s_lw[k], 16)

            sp.wait_ge(s_wfree, 1)
            load_expert(0)
            load_expert(1)
            for u in range(U):
                sp.wait_ge(s_sct[u], 16 * NI)
            for e in range(E1):
                k = e % 2
                if e >= 2:
                    store_y(e - 2)
                    load_expert(e)
                for r0, r1, rows in PARTS:
                    sp.dma_start(RBF[0:rows, (k * RB + r0) * D:(k * RB + r1) * D].rearrange("p (r d) -> p r d", d=D),
                                 slots_x[e * CAP + r0 * P:e * CAP + (r1 - 1) * P + rows, :]
                                 .rearrange("(r p) d -> p r d", p=rows)).then_inc(s_lw[k], 16)
            store_y(E1 - 2)
            store_y(E1 - 1)

            for g in range(NI):
                sp.wait_ge(s_fin, g + 1)
                tiles = min(U, NT - 1 - U * g)
                sp.dma_start(out[U * g * P:(U * g + tiles) * P, :].rearrange("(t p) d -> p t d", p=P),
                             X[:, U * g * D:(U * g + tiles) * D].rearrange("p (t d) -> p t d", d=D)).then_inc(s_out, 16)
            sp.dma_start(out[(NT - 1) * P:N, :], X[0:LAST, (NT - 1) * D:NT * D]).then_inc(s_out, 16)
            sp.wait_ge(s_out, 16 * (NI + 1))

        @block.gpsimd
        def _(po):
            for tile, value in ((IDN, 0.0), (ONE, 1.0), (EPSL, EPS_LN), (EPSD, EPS_DEG), (VALID, 1.0)):
                po.memset(tile[:, :], value).then_inc(s_const, 1)
            po.memset(ZB, 0.0).then_inc(s_const, 1)
            po.memset(DIB_END, 0.0).then_inc(s_const, 1)
            po.iota(IOTA, pattern=[[1, NP + P]], base=0, channel_multiplier=0).then_inc(s_const, 1)
            po.wait_ge(s_const, 8)
            po.affine_select(out=IDN[:, :], in_=IDN[:, :], compare_op=ALU.not_equal, fill=1.0, base=0,
                             pattern=[[-1, P]], channel_multiplier=1).then_inc(s_const, 1)
            po.affine_select(out=TRI[:, :], in_=ONE[:, :], compare_op=ALU.is_ge, fill=0.0, base=0,
                             pattern=[[1, P]], channel_multiplier=-1).then_inc(s_const, 1)
            po.affine_select(out=VALID[:, NT - 1:NT], in_=VALID[:, NT - 1:NT], compare_op=ALU.is_ge, fill=0.0,
                             base=LAST - 1, pattern=[[0, 1]], channel_multiplier=-1).then_inc(s_const, 1)

            def hold(semaphore, value):
                po.wait_ge(semaphore, value)
                po.sem_inc(s_tick, 1)

            def gather_edges(layer, tab, width):
                n = NC * layer
                with po.Fori(0, GI) as i:
                    for j in range(G):
                        if j % Q == 0:
                            hold(s_idx[j // Q], 16 * (GI * layer + i + 1))
                        hold(s_free, n + G * i + j + 1)
                        po.indirect_dma_start(
                            out=ROWS[j][:, 0:width], out_offset=None, in_=tab[:, :],
                            in_offset=bass.IndirectOffsetOnAxis(ap=IDX[:, j:j + 1].bitcast(u32), axis=0))\
                            .then_inc(s_row[j], 16)

            def table_stored(k):
                po.wait_ge(s_stg, U + seq_st[k] + NT)

            with po.Fori(0, NC // (HB * Q)) as i:
                for h in range(HB):
                    hi = HI[:, h * Q * NH:(h + 1) * Q * NH].rearrange("p (j a t) -> p j a t", j=Q, a=8)
                    po.wait_ge(s_hot, HB * i + h + 1)
                    for k, part in ((2, W_2), (3, W_3)):
                        w = part[:, bass.ds(HB * Q * i + Q * h, Q)].rearrange("p (j a b) -> p j a b", a=1, b=1)
                        last = po.tensor_tensor(hi[:, :, k:k + 4:3, :], hi[:, :, 0:8:7, :],
                                                w.to_broadcast([P, Q, 2, NT]), ALU.mult)
                    last.then_inc(s_hotp, 1)

            po.wait_ge(s_histd, 1)
            po.memset(ACC[:, :], 0.0).then_inc(s_accz, 1)
            table_stored(T1)
            po.wait_ge(s_dost, 16)
            po.wait_ge(s_dibd, ND)
            gather_edges(0, tab1, ROW1)
            po.wait_ge(s_xin, seq_in[T2] + NT)
            po.memset(ACC[:, :], 0.0).then_inc(s_accz, 1)
            table_stored(T2)
            gather_edges(1, tab2, D)
            po.wait_ge(s_od, U + seq_mm[FA] + NT)
            po.iota(IOTA, pattern=[[1, NP + P]], base=0, channel_multiplier=0).then_inc(s_io, 1)
            table_stored(T4)
            gather_edges(2, tab3, D)
            table_stored(T5)
            gather_edges(3, tab4, D)

            po.wait_ge(s_wfree, 1)
            po.iota(NIDI.bitcast(i32), pattern=[[P, NT]], base=0, channel_multiplier=1).then_inc(s_nid, 1)
            po.iota(E8I.bitcast(i32), pattern=[[0, NT], [1, E1]], base=0, channel_multiplier=0).then_inc(s_nid, 1)

            po.wait_ge(s_zf, 16 * CLEAR)
            for t in range(NT):
                po.wait_ge(s_xin, seq_in[SG] + NT + t + 1)
                po.indirect_dma_start(
                    out=slots_x[:, :], out_offset=bass.IndirectOffsetOnAxis(ap=IDS[:, t:t + 1].bitcast(u32), axis=0),
                    in_=XIN[:, (t % U) * D:(t % U + 1) * D], in_offset=None).then_inc(s_sct[t % U], 16)

            for k in range(2):
                po.wait_ge(s_ys[k], 16 * 2 * (E1 // 2))
            for t in range(NT):
                if t >= U:
                    po.wait_ge(s_yu, t - U + 1)
                po.indirect_dma_start(
                    out=XIN[:, (t % U) * D:(t % U + 1) * D], out_offset=None, in_=slots_y[:, :],
                    in_offset=bass.IndirectOffsetOnAxis(ap=IDY[:, t:t + 1].bitcast(u32), axis=0))\
                    .then_inc(s_yg[t % U], 16)

        @block.tensor
        def _(pe):
            pe.wait_ge(s_const, 11)
            pe.wait_ge(s_e, 144)
            pe.wait_ge(s_ef, 2)
            for a, blk in enumerate((E_SF, E_DF, E_W)):
                for k in range(NB):
                    last = pe.transpose(PS[2 * a + k // 4][:, (k % 4) * P:(k % 4 + 1) * P], blk[:, k * P:(k + 1) * P],
                                        IDN[:, :])
                last.then_inc(s_et, 1)

            pe.sem_inc(s_xtp, U)
            pe.sem_inc(s_mm, U)

            def transpose_tile(k, i, u):
                n, m = seq_in[k] + U * i + u, seq_xt[k] + U * i + u
                pe.wait_ge(s_xin, n + 1)
                pe.wait_ge(s_xt, U + m + 1 - gap(u))
                for c in range(KC):
                    last = pe.transpose(slot_t(u)[:, c * P:(c + 1) * P], XIN[:, u * D + c * P:u * D + (c + 1) * P],
                                        IDN[:, :])
                last.then_inc(s_xtp, 1)

            def dense_pass(k, w):
                with pe.Fori(0, NI) as i:
                    for u in range(U):
                        transpose_tile(k, i, u)
                    for u in range(U):
                        pe.wait_ge(s_xt, U + seq_xt[k] + U * i + u + 1)
                        pe.wait_ge(s_od, U + seq_mm[k] + U * i + u + 1 - gap(u))
                        for c in range(KC):
                            last = pe.matmul(slot_o(u), XT[:, u * D + c * P:u * D + (c + 1) * P],
                                             w[:, c * D:(c + 1) * D], start=(c == 0), stop=(c == KC - 1))
                        last.then_inc(s_mm, 1)
                pe.wait_ge(s_xt, U + seq_xt[k] + NT)

            pe.wait_ge(s_es, 1)
            pe.wait_ge(s_w, 48)
            dense_pass(T1, WA)

            HSRC, HDST = PS[0][:, 0:3 * NT], PS[1][:, 0:4 * NT]
            pe.matmul(HSRC, ZB16[:, 0:P], ZB16[:, 0:3 * NT], start=True, stop=False)
            pe.matmul(HDST, ZB16[:, 0:P], ZB16[:, 0:4 * NT], start=True, stop=False)
            with pe.Fori(0, NC // (HB * Q)) as i:
                for h in range(HB):
                    pe.wait_ge(s_hot, HB * i + h + 1)
                    pe.wait_ge(s_hotw, HB * i + h + 1)
                    pe.wait_ge(s_hotp, HB * i + h + 1)
                    for j in range(h * Q, (h + 1) * Q):
                        pe.matmul(HSRC, SLO[:, j * P:(j + 1) * P], HI[:, j * NH + 4 * NT:j * NH + 7 * NT],
                                  start=False, stop=False)
                        last = pe.matmul(HDST, DLO[:, j * P:(j + 1) * P], HI[:, j * NH:j * NH + 4 * NT],
                                         start=False, stop=False)
                    last.then_inc(s_hist, 1)
            pe.matmul(HSRC, ZB16[:, 0:P], ZB16[:, 0:3 * NT], start=False, stop=True)
            pe.matmul(HDST, ZB16[:, 0:P], ZB16[:, 0:4 * NT], start=False, stop=True).then_inc(s_histd, 1)

            for g in range(ND):
                w = P * min(4, NT - 4 * g)
                pe.wait_ge(s_diag, g + 1)
                if g >= 2:
                    pe.wait_ge(s_dibd, g - 1)
                pe.matmul(PS[2 + g % 2][:, 0:w], ONE[:, :], ROWDG[g % 2][:, 0:w], start=True, stop=True)\
                    .then_inc(s_dib, 1)

            second, more = pe.alloc_register("second_tiles"), pe.alloc_register("more_tiles")
            pe.reg_mov(second, 1)
            pe.reg_mov(more, 1)

            def sum_edges(layer):
                with pe.Fori(0, GI) as i:
                    for q in range(G // Q):
                        h = q % 2

                        def product(chosen, wait=False):
                            for k in range(Q):
                                j = q * Q + k
                                if wait and layer < 2:
                                    pe.wait_ge(s_scl, NC * layer + G * i + j + 1)
                                elif wait:
                                    pe.wait_ge(s_row[j], 16 * (GI * layer + i + 1))
                                last = pe.matmul(PS[chosen][:, 0:D], MM[chosen][:, k * P:(k + 1) * P],
                                                 ROWS[j][:, 0:D], start=(k == 0), stop=(k == Q - 1))
                            return last

                        _, (span,) = nc.values_load_multi_w_load_instructions(
                            SPAN[0:1, bass.ds((G // Q) * i + q, 1)], engines=(ENG.PE,), min_val=0, max_val=NT - 1,
                            skip_runtime_bounds_check_because="a count of node tiles")
                        pe.wait_ge(s_m, (NC // Q + 2) * layer + (G // Q) * i + q + 1)
                        product(h, wait=True).then_inc(s_p, 1)
                        with pe.If(span > 0):
                            pe.wait_ge(s_me, pe.snap(second))
                            product(2 + h).then_inc(s_pe, 1)
                            pe.reg_add(second, second, 1)
                            with pe.If(span > 1):
                                with pe.Fori(1, span):
                                    pe.wait_ge(s_mx, pe.snap(more))
                                    product(2 + h).then_inc(s_pe, 1)
                                    pe.reg_add(more, more, 1)
                                pe.nop()
                            pe.nop()

            pe.wait_ge(s_span, 1)
            sum_edges(0)
            dense_pass(T2, WB)
            sum_edges(1)
            dense_pass(T3, WC)

            with pe.Fori(0, NI) as i:
                for u in range(U):
                    pe.wait_ge(s_xin, seq_in[RT] + U * i + u + 1)
                    for c in range(KC):
                        last = pe.matmul(PS[0][:, bass.ds(c * 64 + U * i + u, 1)],
                                         XIN[:, u * D + c * P:u * D + (c + 1) * P],
                                         VALID[:, bass.ds(U * i + u, 1)], start=True, stop=True)
                    last.then_inc(s_xtp, 1)
            pe.wait_ge(s_par, 144)
            pe.wait_ge(s_mean, 1)
            for c in range(KC):
                last = pe.matmul(PS[1][0:1, 0:E0], MNT[:, c:c + 1], WRS[:, c * E0:(c + 1) * E0],
                                 start=(c == 0), stop=(c == KC - 1))
            last.then_inc(s_rl, 1)
            pe.wait_ge(s_wab, 1)
            pe.matmul(PS[2][:, 0:2], ONE[0:1, :], SM[0:1, 120:122], start=True, stop=True).then_inc(s_wabp, 1)

            pe.wait_ge(s_fws, 1)
            pe.sem_inc(s_hid, NU)
            with pe.Fori(0, NI) as i:
                pe.wait_ge(s_hid, NU * i + NU)
                for u in range(U):
                    transpose_tile(FA, i, u)
                pe.wait_ge(s_xt, U + seq_xt[FA] + U * i + U)
                for q in range(NU):
                    fe, hf = q // 2, q % 2
                    if q >= 4:
                        pe.wait_ge(s_hid, NU * i + NU + q - 3)
                    for c in range(KC):
                        w = ((fe // FC0) * KC + c) * F0 + (fe % FC0) * P
                        last = pe.matmul(PS[q % 4][:, 0:GT // 2], W1S[:, w:w + P],
                                         XT0[:, c * GT + hf * (GT // 2):c * GT + (hf + 1) * (GT // 2)],
                                         start=(c == 0), stop=(c == KC - 1))
                    last.then_inc(s_up, 1)
                pe.wait_ge(s_hid, NU * i + 2 * NU)
                for u in range(U):
                    pe.wait_ge(s_od, U + seq_mm[FA] + U * i + u + 1 - gap(u))
                    for fe in range(2 * FC0):
                        last = pe.matmul(slot_o(u), H0[:, fe * GT + u * P:fe * GT + (u + 1) * P],
                                         W2S[:, fe * D:(fe + 1) * D], start=(fe == 0), stop=(fe == 2 * FC0 - 1))
                    last.then_inc(s_mm, 1)

            pe.wait_ge(s_w2, 64)
            dense_pass(T4, WA)
            sum_edges(2)
            dense_pass(T5, WB)
            sum_edges(3)

            pe.wait_ge(s_free, G + 4 * NC)
            pe.sem_inc(s_gate, U)
            with pe.Fori(0, NI) as i:
                for u in range(U):
                    transpose_tile(SG, i, u)
                for u in range(U):
                    pe.wait_ge(s_xt, U + seq_xt[SG] + U * i + u + 1)
                    for c in range(KC):
                        last = pe.matmul(PS[4][:, bass.ds((U * i + u) * E1, E1)],
                                         XT[:, u * D + c * P:u * D + (c + 1) * P],
                                         GWS[:, c * E1:(c + 1) * E1], start=(c == 0), stop=(c == KC - 1))
                    last.then_inc(s_gate, 1)
            pe.wait_ge(s_oh, 1)
            pe.matmul(PS[5][:, 0:NX], TRI[:, :], OH, start=True, stop=True)
            pe.matmul(PS[6][:, 0:NX], ONE[:, :], OH, start=True, stop=True).then_inc(s_cum, 1)

            for e in range(E1):
                k = e % 2
                pe.wait_ge(s_lw[k], 80 * (e // 2 + 1))
                if e:
                    pe.wait_ge(s_1h, NU1 * e)
                for r in range(RB):
                    rows = min(P, CAP - r * P)
                    if r >= BK:
                        pe.wait_ge(s_1x, RB * e + r - BK + 1)
                    for c in range(KC):
                        last = pe.transpose(PS[r % BK][:, c * P:c * P + rows],
                                            RBF[0:rows, (k * RB + r) * D + c * P:(k * RB + r) * D + (c + 1) * P],
                                            IDN[0:rows, 0:rows])
                    last.then_inc(s_1t, 1)
                pe.wait_ge(s_1x, RB * (e + 1))
                for q in range(NU1):
                    f, h0, hn = q // 2, (q % 2) * HALF, (HALF, CAP - HALF)[q % 2]
                    if q >= 4:
                        pe.wait_ge(s_1h, NU1 * e + q - 3)
                    for c in range(KC):
                        w = (k * KC + c) * F1 + f * P
                        last = pe.matmul(PS[q % 4][:, 0:hn], W1L[:, w:w + P],
                                         XT1[:, c * CAP + h0:c * CAP + h0 + hn],
                                         start=(c == 0), stop=(c == KC - 1))
                    last.then_inc(s_1u, 1)
                pe.wait_ge(s_1h, NU1 * (e + 1))
                for r in range(RB):
                    rows = min(P, CAP - r * P)
                    if e or r >= BK:
                        pe.wait_ge(s_1y, RB * e + r - BK + 1)
                    for f in range(FC1):
                        last = pe.matmul(PS[BK + r % BK][0:rows, 0:D],
                                         H1[:, f * CAP + r * P:f * CAP + r * P + rows],
                                         W2L[:, (k * FC1 + f) * D:(k * FC1 + f + 1) * D],
                                         start=(f == 0), stop=(f == FC1 - 1))
                    last.then_inc(s_1d, 1)

        @block.scalar
        def _(ac):
            ac.sem_inc(s_xt, U)

            def deviation(n):
                ac.wait_ge(s_var, n)
                ac.activation(SD[:, :].rearrange("p (t a) -> p t a", a=1),
                              MV[:, :].rearrange("p (t c) -> p t c", c=2)[:, :, 1:2],
                              ACT.Sqrt, bias=EPSL[:, :]).then_inc(s_std, 1)

            def copy_transposed(k, i, func, into):
                for u in range(U):
                    ac.wait_ge(s_xtp, U + seq_in[k] + U * i + u + 1)
                    if k in (T1, T2, T3, T4, T5):
                        ac.wait_ge(s_mm, seq_mm[k] + U * i + u + 1)
                    if k == SG:
                        ac.wait_ge(s_gate, U * i + u + 1)
                    ac.activation(into(u), by_block(slot_t(u)), func).then_inc(s_xt, 1)

            def to_slot(u):
                return by_block(XT[:, u * D:(u + 1) * D])

            def stage_products(k, i):
                for u in range(U):
                    ac.wait_ge(s_mm, U + seq_mm[k] + U * i + u + 1)
                    ac.wait_ge(s_stg, seq_st[k] + U * i + u + 1)
                    ac.activation(TT[:, u * D:(u + 1) * D], slot_o(u), ACT.Copy).then_inc(s_od, 1)

            ac.sem_inc(s_od, U)
            ac.wait_ge(s_const, 11)
            deviation(1)
            with ac.Fori(0, NI) as i:
                copy_transposed(T1, i, ACT.Copy, to_slot)
                stage_products(T1, i)

            with ac.Fori(0, NC // (HB * Q)) as i:
                for h in range(HB):
                    ac.wait_ge(s_hot, HB * i + h + 1)
                    for j in range(h * Q, (h + 1) * Q):
                        hi = HI[:, j * NH:(j + 1) * NH].rearrange("p (a t) -> p a t", a=8)
                        last = ac.activation(hi[:, 1:5:3, :], hi[:, 0:8:7, :], ACT.Copy,
                                             scale=W_1[:, bass.ds(HB * Q * i + j, 1)])
                    last.then_inc(s_hotw, 1)

            ac.wait_ge(s_cnt, 1)
            ac.activation(DINV[:, :], CNT[:, :], ACT.Sqrt).then_inc(s_root, 1)
            for g in range(ND):
                w = P * min(4, NT - 4 * g)
                ac.wait_ge(s_dib, g + 1)
                ac.activation(DIB[:, g * 4 * P:g * 4 * P + w], PS[2 + g % 2][:, 0:w], ACT.Copy).then_inc(s_dibd, 1)

            def roots(i, q):
                for j in range(q * Q, (q + 1) * Q):
                    k = j % (2 * Q)
                    ac.wait_ge(s_row[j], 16 * (i + 1))
                    if j % Q == 0:
                        ac.wait_ge(s_di, (G // Q) * i + q + 1)
                    ac.activation(DRT[:, k:k + 1], DIE[:, k:k + 1], ACT.Sqrt,
                                  bias=EPSD[:, :], scale=ROWS[j][:, D:D + 1]).then_inc(s_dr, 1)

            def scale_rows(layer, i, q):
                for j in range(q * Q, (q + 1) * Q):
                    if layer:
                        ac.wait_ge(s_row[j], 16 * (GI * layer + i + 1))
                    elif j % Q == 0:
                        ac.wait_ge(s_nm, (G // Q) * i + q + 1)
                    ac.activation(ROWS[j][:, 0:D], ROWS[j][:, 0:D], ACT.Copy,
                                  scale=NRM[:, bass.ds(G * i + j, 1)]).then_inc(s_scl, 1)

            roots(0, 0)
            with ac.Fori(0, GI - 1) as i:
                for q in range(G // Q):
                    scale_rows(0, i, q)
                    roots(i + (q + 1) // (G // Q), (q + 1) % (G // Q))
            for q in range(G // Q):
                scale_rows(0, GI - 1, q)
                if q < G // Q - 1:
                    roots(GI - 1, q + 1)
            k = NC % (2 * Q)
            ac.wait_ge(s_di, NC // Q + 1)
            ac.activation(DRT[:, k:k + Q], DIE[:, k:k + Q], ACT.Sqrt, bias=EPSD[:, :]).then_inc(s_dr, Q)

            with ac.Fori(0, NI) as i:
                copy_transposed(T2, i, ACT.Relu, to_slot)
                stage_products(T2, i)
            with ac.Fori(0, GI) as i:
                for q in range(G // Q):
                    scale_rows(1, i, q)
            with ac.Fori(0, NI) as i:
                copy_transposed(T3, i, ACT.Relu, to_slot)
            deviation(2)

            ac.wait_ge(s_e1, 1)
            ac.activation(SM[0:1, 24:32], SM[0:1, 16:24], ACT.Exp, bias=SM[0:1, 1:2]).then_inc(s_x1, 1)
            ac.wait_ge(s_e1, 2)
            ac.activation(SM[0:1, 48:56], SM[0:1, 40:48], ACT.Exp, bias=SM[0:1, 3:4]).then_inc(s_x1, 1)
            ac.wait_ge(s_e1, 3)
            ac.activation(SM[0:1, 113:114], SM[0:1, 112:113], ACT.Exp).then_inc(s_x1, 1)

            def to_block(u):
                return by_block(XT0)[:, :, u * P:(u + 1) * P]

            def gelus(i):
                for q in range(NU):
                    fe, hf = q // 2, q % 2
                    ac.wait_ge(s_up, NU * i + q + 1)
                    ac.activation(H0[:, fe * GT + hf * (GT // 2):fe * GT + (hf + 1) * (GT // 2)],
                                  PS[q % 4][:, 0:GT // 2], ACT.Gelu, bias=B1S[:, fe:fe + 1]).then_inc(s_hid, 1)

            def deviation_of_7(n):
                ac.wait_ge(s_v7, n)
                ac.activation(NR7[:, :].rearrange("p (u a) -> p u a", a=1),
                              MV7[:, :].rearrange("p (u c) -> p u c", c=2)[:, :, 1:2],
                              ACT.Sqrt, bias=EPSL[:, :]).then_inc(s_d7, 1)

            ac.wait_ge(s_fw, 128)
            copy_transposed(FA, 0, ACT.Copy, to_block)
            gelus(0)
            with ac.Fori(1, NI) as i:
                copy_transposed(FA, i, ACT.Copy, to_block)
                gelus(i)
                deviation_of_7(i)
            deviation_of_7(NI)
            deviation(3)

            with ac.Fori(0, NI) as i:
                copy_transposed(T4, i, ACT.Copy, to_slot)
            with ac.Fori(0, NI) as i:
                copy_transposed(T5, i, ACT.Copy, to_slot)
                ac.wait_ge(s_sq, i + 1)
                ac.activation(NRV[:, ts(i, U)], SSQ[:, ts(i, U)], ACT.Sqrt).then_inc(s_nr, 1)
            deviation(4)
            with ac.Fori(0, NI) as i:
                copy_transposed(SG, i, ACT.Copy, to_slot)
            ac.wait_ge(s_ei, 1)
            ac.activation(TA, TA, ACT.Exp).then_inc(s_eo, 1)

            for e in range(E1):
                for r in range(RB):
                    ac.wait_ge(s_1t, RB * e + r + 1)
                    if e and r == 0:
                        ac.wait_ge(s_1u, NU1 * e)
                    rows = min(P, CAP - r * P)
                    ac.activation(by_block(XT1)[:, :, r * P:r * P + rows],
                                  by_block(PS[r % BK][:, 0:D])[:, :, 0:rows], ACT.Copy)\
                        .then_inc(s_1x, 1)
                if e:
                    ac.wait_ge(s_1d, RB * e)
                else:
                    ac.wait_ge(s_b1, 16 * E1)
                for q in range(NU1):
                    f, h0, hn = q // 2, (q % 2) * HALF, (HALF, CAP - HALF)[q % 2]
                    ac.wait_ge(s_1u, NU1 * e + q + 1)
                    ac.activation(H1[:, f * CAP + h0:f * CAP + h0 + hn],
                                  PS[q % 4][:, 0:hn], ACT.Relu, bias=B1L[:, e * FC1 + f:e * FC1 + f + 1])\
                        .then_inc(s_1h, 1)

        @block.vector
        def _(ve):
            def settle():
                ve.wait_ge(s_dv, dve.now())

            def hold(semaphore, value):
                ve.wait_ge(semaphore, value)
                ve.sem_inc(s_vtick, 1)

            step = dve.tell

            def loop(start, trips, per, body):
                with ve.Fori(start, trips) as i:
                    dve.enter(i - start if start else i, per)
                    body(i)
                    dve.check()
                dve.leave(trips - start)

            def tile(v, i, u):
                return v[:, ts(U * i + u, D)]

            def slot(v, u):
                return v[:, u * D:(u + 1) * D]

            def normalized(into, i, u):
                t = U * i + u
                return ve.tensor_scalar(into, tile(X, i, u), MV[:, bass.ds(2 * t, 1)], RS[:, bass.ds(t, 1)],
                                        ALU.subtract, ALU.mult)

            def moments(i):
                hold(s_dv, dve.now())
                for u in range(U):
                    last = ve.bn_stats(ST7[:, u * 6:(u + 1) * 6], tile(X, i, u))
                step(last)
                hold(s_dv, dve.now())
                for u in range(U):
                    last = ve.bn_aggr(MV7[:, 2 * u:2 * u + 2], ST7[:, u * 6:(u + 1) * 6])
                step(last)
                settle()
                step(ve.tensor_copy(MV[:, ts(i, 2 * U)], MV7[:, :]))

            def reciprocal_deviation(n):
                settle()
                ve.sem_inc(s_var, 1)
                ve.wait_ge(s_std, n)
                step(ve.reciprocal(RS[:, :], SD[:, :]))
                settle()

            def feed(k, i, make):
                for u in range(U):
                    ve.wait_ge(s_xtp, seq_in[k] + U * i + u + 1)
                    make(slot(XIN, u), i, u).then_inc(s_xin, 1)

            def feed_normalized(k, i):
                feed(k, i, normalized)

            ve.memset(X[:, (NT - 1) * D:NT * D], 0.0).then_inc(s_pad, 1)
            ve.memset(E_SRC[:, (NB - 1) * P:NB * P], 0).then_inc(s_pad, 1)
            ve.memset(E_DST[:, (NB - 1) * P:NB * P], NP - 1).then_inc(s_pad, 1)
            ve.memset(E_W[:, (NB - 1) * P:NB * P], 0.0).then_inc(s_pad, 1)
            step(ve.memset(NRM[:, :], 0.0))
            step(ve.memset(DOX[:, :], 0.0))
            ve.sem_inc(s_free, G)
            ve.sem_inc(s_joined, 1)
            ve.sem_inc(s_aj, 1)
            ve.sem_inc(s_dj, 1)

            ve.wait_ge(s_e, 144)
            ve.tensor_copy(E_SF, E_SRC).then_inc(s_ef, 1)
            ve.tensor_copy(E_DF, E_DST).then_inc(s_ef, 1)
            ve.wait_ge(s_ef, 2)
            df3 = E_DF.rearrange("p (k j) -> p k j", j=P)
            ve.tensor_reduce(TEMP[:, 0:NB], df3, AX.X, ALU.min)
            step(ve.tensor_reduce(TEMP[:, NB:2 * NB], df3, AX.X, ALU.max))
            settle()
            step(ve.tensor_copy(TEMP_I, TEMP))
            settle()
            ve.tensor_scalar(T_I[:, 0:2 * NB], TEMP_I, 7, None, ALU.arith_shift_right)\
                .then_inc(s_meta, 1)

            for a, (into, n) in enumerate(((SRC, 1), (DST, 2), (EW, 3))):
                ve.wait_ge(s_et, n)
                ve.tensor_copy(into[:, 0:4 * P], PS[2 * a][:, :])
                last = ve.tensor_copy(into[:, 4 * P:NB * P], PS[2 * a + 1][:, 0:(NB - 4) * P])
            last.then_inc(s_es, 1)
            ve.wait_ge(s_es, 1)
            ve.wait_ge(s_metad, 32)
            step(ve.tensor_scalar(T_I, SRC[:, :], 7, None, ALU.arith_shift_right))
            settle()
            step(ve.tensor_copy(S_HI, T_I))
            settle()
            step(ve.tensor_scalar(T_I, SRC[:, :], P - 1, None, ALU.bitwise_and))
            settle()
            step(ve.tensor_copy(S_LO, T_I))
            step(ve.tensor_copy(E_SRC, DST[:, :]))
            settle()
            step(ve.tensor_scalar(T_I, E_SRC, 7, None, ALU.arith_shift_right))
            settle()
            step(ve.tensor_copy(D_HI, T_I))
            settle()
            step(ve.tensor_scalar(T_I, E_SRC, P - 1, None, ALU.bitwise_and))
            settle()
            step(ve.tensor_copy(D_LO, T_I))
            rounded = E_DST.bitcast(bf16)[:, 0:EC]
            step(ve.tensor_copy(rounded, EW[:, :]))
            settle()
            step(ve.tensor_copy(W_1, rounded))
            settle()
            step(ve.tensor_tensor(W_2, EW[:, :], W_1, ALU.subtract))
            settle()
            step(ve.tensor_copy(rounded, W_2))
            settle()
            step(ve.tensor_tensor(W_3, W_2, rounded, ALU.subtract))
            settle()
            step(ve.tensor_copy(W_2, rounded))

            ve.wait_ge(s_x, 32)
            settle()
            loop(0, NI, 3, moments)
            ve.wait_ge(s_const, 11)
            reciprocal_deviation(1)
            loop(0, NI, 0, lambda i: feed_normalized(T1, i))

            def bits(into, values, width, i, h):
                ins = ve.tensor_tensor(
                    into, IOTA[:, 0:width].rearrange("p (a n) -> p a n", a=1).to_broadcast([P, Q, width]),
                    values[:, bass.ds(HB * Q * i + Q * h, Q)].rearrange("p (j a) -> p j a", a=1)
                    .to_broadcast([P, Q, width]), ALU.is_equal)
                return ins

            def onehots(i):
                for h in range(HB):
                    lows, highs = slice(h * Q * P, (h + 1) * Q * P), slice(h * Q * NH, (h + 1) * Q * NH)
                    hi = HI[:, highs].rearrange("p (j m) -> p j m", m=NH)
                    ve.wait_ge(s_hist, HB * i + h + 1)
                    bits(hi[:, :, 0:NT], D_HI, NT, i, h)
                    bits(hi[:, :, 7 * NT:8 * NT], S_HI, NT, i, h)
                    bits(SLO[:, lows].rearrange("p (j n) -> p j n", n=P), S_LO, P, i, h)
                    bits(DLO[:, lows].rearrange("p (j n) -> p j n", n=P), D_LO, P, i, h).then_inc(s_hot, 1)

            ve.wait_ge(s_xtp, U + seq_in[T1] + NT)
            ve.sem_inc(s_hist, HB)
            loop(0, NC // (HB * Q), 0, onehots)
            ve.wait_ge(s_histd, 1)
            step(ve.tensor_copy(HT[:, 0:3 * NT], PS[0][:, 0:3 * NT]))
            step(ve.tensor_copy(HT[:, 3 * NT:6 * NT], PS[1][:, NT:4 * NT]))
            settle()
            ht = HT.rearrange("p (s k t) -> p s k t", s=2, k=3)
            step(ve.tensor_tensor(ht[:, :, 1:2, :], ht[:, :, 1:2, :], ht[:, :, 2:3, :], ALU.add))
            settle()
            ve.tensor_tensor(DOX[:, :].rearrange("p (t c) -> p t c", c=4)[:, :, 0:1],
                             HT[:, 0:NT].rearrange("p (t a) -> p t a", a=1),
                             HT[:, NT:2 * NT].rearrange("p (t a) -> p t a", a=1), ALU.add)
            step(ve.tensor_tensor(DEGI[:, :], HT[:, 3 * NT:4 * NT], HT[:, 4 * NT:5 * NT], ALU.add))
            settle()
            ve.sem_inc(s_deg, 1)
            ve.tensor_scalar(CNT[:, :], PS[1][:, 0:NT], 1.0, 1e-12, ALU.add, ALU.max).then_inc(s_cnt, 1)
            ve.wait_ge(s_stg, U + seq_st[T1] + NT)
            for g in range(ND):
                tiles = min(4, NT - 4 * g)
                if g >= 2:
                    ve.wait_ge(s_dib, g - 1)
                ve.tensor_tensor(
                    ROWDG[g % 2][:, 0:tiles * P].rearrange("p (t n) -> p t n", n=P),
                    IDN[:, :].rearrange("p (a n) -> p a n", a=1).to_broadcast([P, tiles, P]),
                    DEGI[:, 4 * g:4 * g + tiles].rearrange("p (t a) -> p t a", a=1).to_broadcast([P, tiles, P]),
                    ALU.mult).then_inc(s_diag, 1)
            ve.wait_ge(s_root, 1)
            step(ve.reciprocal(DINV[:, :], DINV[:, :]))

            z = ve.alloc_register("more_selections")
            ve.reg_mov(z, 1)
            tile_of = [ve.alloc_register(f"first_tile_{h}") for h in range(2)]
            span_of = [ve.alloc_register(f"span_{h}") for h in range(2)]
            next_tile, next_span = ve.alloc_register("next_tile"), ve.alloc_register("next_span")
            zd = ve.alloc_register("more_degrees")
            ve.reg_mov(zd, 1)

            def load_tile(row, g):
                return nc.values_load_multi_w_load_instructions(
                    row[0:1, bass.ds(g, 1)], engines=(ENG.DVE,), min_val=0, max_val=NT - 1,
                    skip_runtime_bounds_check_because="node tiles")[1][0]

            def sum_edges(layer):
                groups_before = NC // Q * layer
                find_norms = layer == 0

                def chunk(g, k):
                    return bass.ds(Q * g + k, 1)

                def select(g, chosen, t):
                    return ve.tensor_tensor(
                        MM[chosen].rearrange("p (k n) -> p k n", n=P),
                        IOTA[:, ts(t, P)].rearrange("p (a n) -> p a n", a=1).to_broadcast([P, Q, P]),
                        DST[:, bass.ds(Q * g, Q)].rearrange("p (k a) -> p k a", a=1).to_broadcast([P, Q, P]),
                        ALU.is_equal)

                def select_degrees(accum, g, t, tiles):
                    for k in range(Q):
                        nodes = bass.ds(t * P, tiles * P)
                        last = ve.scalar_tensor_tensor(DSEL[:, 2 * P * k:2 * P * k + tiles * P], IOTA[:, nodes],
                                                       DST[:, chunk(g, k)], DIB[:, nodes], ALU.is_equal, ALU.mult,
                                                       accum_out=accum[:, k:k + 1])
                    return last

                def prepare(g, h, t, span):
                    select(g, h, t).then_inc(s_m, 1)
                    with ve.If(span > 0):
                        select(g, 2 + h, a_tile(t + 1)).then_inc(s_me, 1)
                        if find_norms:
                            with ve.If(span > 1):
                                d = DIE[:, Q * h:Q * (h + 1)]
                                hold(s_dv, dve.now())
                                with ve.Fori(1, span) as e:
                                    so_far = ve.snap(zd)
                                    ve.wait_ge(s_dj, so_far)
                                    select_degrees(DIX, g, a_tile(t + e + 1), 1).then_inc(s_dx, 1)
                                    ve.wait_ge(s_dx, so_far)
                                    ve.tensor_tensor(d, d, DIX[:, :], ALU.add).then_inc(s_dj, 1)
                                    ve.reg_add(zd, zd, 1)
                                hold(s_dj, ve.snap(zd))
                    if find_norms:
                        hold(s_dv, dve.now())
                        ve.sem_inc(s_di, 1)

                def incoming_degrees(g, h, t):
                    step(select_degrees(DIE[:, Q * h:Q * (h + 1)], g, t, 2))

                def join_further(t, h):
                    count = ve.snap(z)
                    a = ACC[:, ts(t, D)]
                    ve.wait_ge(s_pe, count)
                    ve.wait_ge(s_aj, count)
                    ve.tensor_tensor(a, a, PS[2 + h][:, 0:D], ALU.add).then_inc(s_aj, 1)
                    ve.reg_add(z, z, 1)

                def collect(g, h):
                    count = g + groups_before
                    t, span = a_tile(ve.snap(tile_of[h])), a_tile(ve.snap(span_of[h]))
                    a = ACC[:, ts(t, D)]
                    ve.wait_ge(s_p, count + 1)
                    ve.wait_ge(s_joined, count + 1)
                    ve.tensor_tensor(a, a, PS[h][:, 0:D], ALU.add).then_inc(s_joined, 1)
                    with ve.If(span > 0):
                        with ve.If(span > 1):
                            with ve.Fori(1, span) as e:
                                join_further(a_tile(t + e), h)
                                select(g, 2 + h, a_tile(t + e + 1)).then_inc(s_mx, 1)
                        join_further(a_tile(t + span), h)
                        hold(s_aj, ve.snap(z))
                    ve.wait_ge(s_joined, count + 2)
                    ve.sem_inc(s_free, Q)

                def load_next(g):
                    ve.reg_mov(next_tile, load_tile(FIRST, g))
                    ve.reg_mov(next_span, load_tile(SPAN, g))

                def norms(g, h):
                    these, c = slice(Q * h, Q * (h + 1)), bass.ds(Q * g, Q)
                    ve.wait_ge(s_dr, Q * (g + 1))
                    step(ve.reciprocal(DRI[:, these], DRT[:, these]))
                    load_next(g + 2)
                    settle()
                    ve.tensor_tensor(NRM[:, c], DRI[:, these], EW[:, c], ALU.mult).then_inc(s_nm, 1)

                def groups(i):
                    for k in range(G // Q):
                        g, h = (G // Q) * i + k, k % 2
                        t, span = a_tile(ve.snap(next_tile)), a_tile(ve.snap(next_span))
                        if find_norms:
                            incoming_degrees(g + 2, h, t)
                            norms(g + 1, 1 - h)
                        else:
                            load_next(g + 3)
                        collect(g, h)
                        prepare(g + 2, h, t, span)
                        ve.reg_mov(tile_of[h], t)
                        ve.reg_mov(span_of[h], span)

                for h in range(2):
                    t, span = load_tile(FIRST, h), load_tile(SPAN, h)
                    if find_norms:
                        incoming_degrees(h, h, t)
                    prepare(h, h, t, span)
                    ve.reg_mov(tile_of[h], t)
                    ve.reg_mov(span_of[h], span)
                if find_norms:
                    norms(0, 0)
                else:
                    load_next(2)
                loop(0, GI, 2 * (G // Q) if find_norms else 0, groups)
                ve.wait_ge(s_m, (NC // Q + 2) * (layer + 1))

            def slot_p(v, m):
                return v[:, m * P:(m + 1) * P]

            ve.wait_ge(s_metal, 16)
            step(ve.tensor_reduce(GROUP1, META[0:1, 0:EC].rearrange("p (g k) -> p g k", k=Q), AX.X, ALU.min))
            step(ve.tensor_reduce(GROUPN, META[0:1, EC:2 * EC].rearrange("p (g k) -> p g k", k=Q), AX.X, ALU.max))
            settle()
            step(ve.tensor_copy(FIRST[:, :], GROUP1))
            ve.tensor_tensor(SPAN[:, :], GROUPN, GROUP1, ALU.subtract).then_inc(s_span, 1)
            ve.wait_ge(s_span, 1)
            ve.wait_ge(s_accz, 1)
            sum_edges(0)
            ve.wait_ge(s_free, G + NC)

            ve.wait_ge(s_par, 144)

            def plus(bias):
                return lambda into, i, u: ve.tensor_tensor(into, tile(ACC, i, u), bias[:, :], ALU.add)

            loop(0, NI, 0, lambda i: feed(T2, i, plus(BA)))
            ve.wait_ge(s_accz, 2)
            ve.wait_ge(s_mm, U + seq_mm[T2] + NT)
            sum_edges(1)
            ve.wait_ge(s_free, G + 2 * NC)

            def ahead(k, make, take, per):
                feed(k, 0, make)

                def body(i):
                    feed(k, i + 1, make)
                    take(i)
                loop(0, NI - 1, per, body)
                take(NI - 1)

            def take_t3(i):
                for u in range(U):
                    ve.wait_ge(s_mm, U + seq_mm[T3] + U * i + u + 1)
                    ve.tensor_tensor(slot(TT, u), slot_o(u), BC[:, :], ALU.add).then_inc(s_od, 1)
                ve.wait_ge(s_od, U + seq_mm[T3] + U * i + U)
                x7 = X[:, ts(i, U * D)]
                step(ve.tensor_tensor(x7, x7, TT, ALU.add))
                moments(i)

            ahead(T3, plus(BB), take_t3, 4)
            reciprocal_deviation(2)

            loop(0, NI, 0, lambda i: feed_normalized(RT, i))
            ve.wait_ge(s_xtp, U + seq_in[RT] + NT)
            step(ve.tensor_reduce(MNT[:, :], PS[0][:, 0:2 * 64].rearrange("p (c t) -> p c t", c=KC)[:, :, 0:NT],
                                  AX.X, ALU.add))
            settle()
            ve.tensor_scalar(MNT[:, :], MNT[:, :], 1.0 / N, None, ALU.mult).then_inc(s_mean, 1)

            def row(a, w=1):
                return SM[0:1, a:a + w]

            def softmax(logits, exps, probs, top, neg, total, turn):
                step(ve.tensor_reduce(row(top), logits, AX.X, ALU.max))
                settle()
                ve.tensor_scalar(row(neg), row(top), -1.0, None, ALU.mult).then_inc(s_e1, 1)
                ve.wait_ge(s_x1, turn)
                step(ve.tensor_reduce(row(total), exps, AX.X, ALU.add))
                settle()
                step(ve.reciprocal(row(total), row(total)))
                settle()
                step(ve.tensor_scalar(probs, exps, row(total), None, ALU.mult))
                settle()

            ve.wait_ge(s_rl, 1)
            step(ve.tensor_tensor(row(16, E0), PS[1][0:1, 0:E0], row(8, E0), ALU.add))
            settle()
            softmax(row(16, E0), row(24, E0), row(32, E0), 0, 1, 4, 1)
            step(ve.tensor_scalar(row(56, E0), row(32, E0), float(N), 1e-30, ALU.mult, ALU.max))
            settle()
            step(ve.reciprocal(row(64, E0), row(56, E0)))
            settle()
            step(ve.tensor_scalar(row(72, E0), row(64, E0), float(CAP), 1.0, ALU.mult, ALU.min))
            settle()
            step(ve.tensor_tensor(row(40, E0), row(32, E0), row(72, E0), ALU.mult))
            settle()
            softmax(row(40, E0), row(48, E0), row(80, E0), 2, 3, 5, 2)
            step(ve.tensor_scalar(row(96, E0), IOTA[0:1, 0:E0], -1.0, float(E0), ALU.mult, ALU.add))
            for k in range(2):
                step(ve.tensor_reduce(row(110 + k), row(80, E0), AX.X, ALU.max))
                settle()
                step(ve.scalar_tensor_tensor(row(88, E0), row(80, E0), row(110 + k), row(96, E0),
                                             ALU.is_equal, ALU.mult))
                settle()
                step(ve.tensor_reduce(row(114 + k), row(88, E0), AX.X, ALU.max))
                settle()
                step(ve.tensor_scalar(row(116 + k), row(114 + k), -1.0, float(E0), ALU.mult, ALU.add))
                step(ve.tensor_scalar(row(88, E0), row(96, E0), row(114 + k), -2.0, ALU.is_equal, ALU.mult))
                settle()
                step(ve.tensor_tensor(row(80, E0), row(80, E0), row(88, E0), ALU.add))
                settle()
            ve.tensor_copy(EXI[0:1, 0:2], row(116, 2)).then_inc(s_ex, 1)
            ve.tensor_tensor(row(112), row(111), row(110), ALU.subtract).then_inc(s_e1, 1)
            ve.wait_ge(s_x1, 3)
            step(ve.tensor_scalar(row(118), row(113), 1.0, None, ALU.add))
            settle()
            step(ve.reciprocal(row(120), row(118)))
            settle()
            ve.tensor_tensor(row(121), row(120), row(113), ALU.mult).then_inc(s_wab, 1)
            ve.wait_ge(s_wabp, 1)
            step(ve.tensor_copy(WAB[:, :], PS[2][:, 0:2]))
            settle()
            ve.wait_ge(s_fw, 128)
            for k in range(2):
                w2s = W2S[:, k * FC0 * D:(k + 1) * FC0 * D]
                ve.tensor_scalar(w2s, w2s, WAB[:, k:k + 1], None, ALU.mult)
            step(ve.tensor_scalar(BC[:, :], B2P[:, 0:D], WAB[:, 0:1], None, ALU.mult))
            settle()
            ve.scalar_tensor_tensor(BC[:, :], B2P[:, D:2 * D], WAB[:, 1:2], BC[:, :], ALU.mult, ALU.add)\
                .then_inc(s_fws, 1)
            ve.wait_ge(s_fws, 1)

            def take_ffn(i):
                for u in range(U):
                    ve.wait_ge(s_mm, U + seq_mm[FA] + U * i + u + 1)
                    ve.tensor_tensor(slot(YT, u), slot_o(u), BC[:, :], ALU.add).then_inc(s_od, 1)
                    last = normalized(slot(YN, u), i, u)
                step(last)
                settle()
                step(ve.tensor_tensor(YT, YT, YN, ALU.add))
                hold(s_dv, dve.now())
                for u in range(U):
                    last = ve.bn_stats(ST7[:, u * 6:(u + 1) * 6], slot(YT, u))
                step(last)
                hold(s_dv, dve.now())
                for u in range(U):
                    last = ve.bn_aggr(MV7[:, 2 * u:2 * u + 2], ST7[:, u * 6:(u + 1) * 6])
                last.then_inc(s_v7, 1)
                ve.wait_ge(s_v7, i + 1)
                ve.wait_ge(s_d7, i + 1)
                step(ve.reciprocal(R7[:, :], NR7[:, :]))
                settle()
                for u in range(U):
                    last = ve.tensor_scalar(slot(YT, u), slot(YT, u), MV7[:, 2 * u:2 * u + 1], R7[:, u:u + 1],
                                            ALU.subtract, ALU.mult)
                step(last)
                settle()
                for other, op in ((GAM, ALU.mult), (BET, ALU.add)):
                    y3 = YT.rearrange("p (u d) -> p u d", d=D)
                    step(ve.tensor_tensor(y3, y3, other[:, :].rearrange("p (a d) -> p a d", a=1)
                                          .to_broadcast([P, U, D]), op))
                    settle()
                x7 = X[:, ts(i, U * D)]
                step(ve.tensor_tensor(x7, x7, YT, ALU.add))
                moments(i)

            ahead(FA, normalized, take_ffn, 11)
            reciprocal_deviation(3)

            def take_t4(i):
                for u in range(U):
                    ve.wait_ge(s_mm, U + seq_mm[T4] + U * i + u + 1)
                    ve.tensor_scalar(tile(ACC, i, u), slot_o(u), DINV[:, bass.ds(U * i + u, 1)], None, ALU.mult)\
                        .then_inc(s_od, 1)

            ahead(T4, normalized, take_t4, 0)
            ve.wait_ge(s_io, 1)
            ve.wait_ge(s_stg, U + seq_st[T4] + NT)
            ve.wait_ge(s_mm, U + seq_mm[T4] + NT)
            sum_edges(2)
            ve.wait_ge(s_free, G + 3 * NC)

            def hidden(into, i, u):
                return ve.scalar_tensor_tensor(into, tile(ACC, i, u), DINV[:, bass.ds(U * i + u, 1)], BA[:, :],
                                               ALU.mult, ALU.add)

            def squares(i):
                for u in range(U):
                    ve.wait_ge(s_xin, seq_in[T5] + U * i + u + 1)
                    last = ve.scalar_tensor_tensor(slot(TT, u), slot(XIN, u), 1.0, slot(XIN, u), ALU.mult, ALU.mult,
                                                   accum_out=SSQ[:, bass.ds(U * i + u, 1)])
                last.then_inc(s_sq, 1)

            def take_t5(i):
                ve.wait_ge(s_nr, i + 1)
                nr = NRV[:, ts(i, U)]
                step(ve.tensor_scalar(nr, nr, 1e-12, None, ALU.max))
                hold(s_dv, dve.now())
                step(ve.reciprocal(nr, nr))
                settle()
                step(ve.tensor_tensor(nr, nr, DINV[:, ts(i, U)], ALU.mult))
                settle()
                for u in range(U):
                    ve.wait_ge(s_mm, U + seq_mm[T5] + U * i + u + 1)
                    ve.tensor_scalar(tile(ACC, i, u), slot_o(u), NRV[:, bass.ds(U * i + u, 1)], None, ALU.mult)\
                        .then_inc(s_od, 1)

            feed(T5, 0, hidden)
            squares(0)

            def body_t5(i):
                ve.wait_ge(s_sq, i + 1)
                feed(T5, i + 1, hidden)
                squares(i + 1)
                take_t5(i)
            loop(0, NI - 1, 3, body_t5)
            take_t5(NI - 1)
            ve.wait_ge(s_stg, U + seq_st[T5] + NT)
            ve.wait_ge(s_mm, U + seq_mm[T5] + NT)
            sum_edges(3)
            ve.wait_ge(s_free, G + 4 * NC)

            def finish_gnn(i):
                for u in range(U):
                    normalized(slot(TT, u), i, u)
                    last = ve.scalar_tensor_tensor(slot(TU, u), tile(ACC, i, u), DINV[:, bass.ds(U * i + u, 1)],
                                                   BB[:, :], ALU.mult, ALU.add)
                step(last)
                settle()
                step(ve.tensor_tensor(TT, TT, TU, ALU.add))
                settle()
                x7 = X[:, ts(i, U * D)]
                step(ve.tensor_tensor(x7, x7, TT, ALU.add))
                moments(i)

            loop(0, NI, 6, finish_gnn)
            reciprocal_deviation(4)
            ve.sem_inc(s_wfree, 1)

            loop(0, NI, 0, lambda i: feed_normalized(SG, i))
            ve.wait_ge(s_nid, 2)
            step(ve.tensor_copy(NID, NIDI.bitcast(i32)))
            step(ve.tensor_copy(E8, E8I.bitcast(i32)))
            ve.wait_ge(s_gate, U + NT)
            step(ve.tensor_tensor(by_expert(LG), by_expert(PS[4][:, 0:NX]),
                                  GBS[:, :].rearrange("p (a e) -> p a e", a=1).to_broadcast([P, NT, E1]), ALU.add))
            settle()
            step(ve.tensor_reduce(MX, by_expert(LG), AX.X, ALU.max))
            settle()
            ve.tensor_tensor(by_expert(TA), by_expert(LG), per_tile(MX, E1), ALU.subtract).then_inc(s_ei, 1)
            step(ve.tensor_tensor(by_expert(OH), by_expert(LG), per_tile(MX, E1), ALU.is_equal))
            step(ve.tensor_scalar(PA, E8, -1.0, float(E1), ALU.mult, ALU.add))
            settle()
            step(ve.tensor_tensor(OH, OH, PA, ALU.mult))
            settle()
            step(ve.tensor_reduce(IXF, by_expert(OH), AX.X, ALU.max))
            settle()
            step(ve.tensor_scalar(IXF, IXF, -1.0, float(E1), ALU.mult, ALU.add))
            settle()
            step(ve.tensor_tensor(by_expert(OH), by_expert(E8), per_tile(IXF, E1), ALU.is_equal))
            settle()
            ve.tensor_tensor(by_expert(OH), by_expert(OH), per_tile(VALID[:, :], E1), ALU.mult).then_inc(s_oh, 1)
            ve.wait_ge(s_eo, 1)
            step(ve.tensor_reduce(SE, by_expert(TA), AX.X, ALU.add))
            settle()
            step(ve.reciprocal(PRB, SE))
            ve.wait_ge(s_cum, 1)
            step(ve.tensor_copy(TO, PS[6][:, 0:NX]))
            step(ve.tensor_copy(PA, PS[6][:, 0:NX]))
            settle()
            a, b, shift = PA, PB_, 1
            while shift < NT:
                w = shift * E1
                ve.tensor_copy(b[:, 0:w], a[:, 0:w])
                step(ve.tensor_tensor(b[:, w:NX], a[:, w:NX], a[:, 0:NX - w], ALU.add))
                settle()
                a, b, shift = b, a, 2 * shift
            step(ve.tensor_tensor(a, a, TO, ALU.subtract))
            settle()
            step(ve.tensor_tensor(CU, a, PS[5][:, 0:NX], ALU.add))
            settle()
            step(ve.tensor_tensor(CU, CU, OH, ALU.mult))
            settle()
            step(ve.tensor_reduce(POS, by_expert(CU), AX.X, ALU.add))
            settle()
            step(ve.tensor_scalar(KEP, POS, float(CAP), None, ALU.is_le))
            step(ve.tensor_scalar(SLT, POS, -1.0, 0.0, ALU.add, ALU.max))
            settle()
            step(ve.tensor_tensor(KEP, KEP, VALID[:, :], ALU.mult))
            step(ve.tensor_scalar(SLT, SLT, float(CAP - 1), None, ALU.min))
            settle()
            step(ve.scalar_tensor_tensor(SLT, IXF, float(CAP), SLT, ALU.mult, ALU.add))
            step(ve.tensor_scalar(DMP, NID, float(DUMP), None, ALU.add))
            settle()
            step(ve.tensor_copy(IDY[:, :], SLT))
            step(ve.tensor_tensor(SLT, SLT, DMP, ALU.subtract))
            step(ve.tensor_tensor(SCL, PRB, KEP, ALU.mult))
            settle()
            step(ve.tensor_tensor(SLT, SLT, KEP, ALU.mult))
            settle()
            step(ve.tensor_tensor(SLT, SLT, DMP, ALU.add))
            settle()
            step(ve.tensor_copy(IDS[:, :], SLT))
            settle()
            ve.sem_inc(s_ix, 1)
            for t in range(NT):
                if t >= U:
                    ve.wait_ge(s_sct[t % U], 16 * (t // U))
                normalized(slot(XIN, t % U), 0, t).then_inc(s_xin, 1)

            for e in range(E1):
                k = e % 2
                for r in range(RB):
                    rows = min(P, CAP - r * P)
                    ve.wait_ge(s_1d, RB * e + r + 1)
                    if r == 0 and e >= 2:
                        ve.wait_ge(s_ys[k], 32 * (e // 2))
                    ve.tensor_tensor(YS[0:rows, (k * RB + r) * D:(k * RB + r + 1) * D],
                                     PS[BK + r % BK][0:rows, 0:D], B2L[k][0:rows, :], ALU.add)\
                        .then_inc(s_1y, 1)

            ve.wait_ge(s_1y, RB * E1)
            for g in range(NI):
                for u in range(U):
                    t = U * g + u
                    ve.wait_ge(s_yg[u], 16 * (g + 1))
                    ve.tensor_scalar(slot(YV, u), slot(XIN, u), SCL[:, t:t + 1], None, ALU.mult).then_inc(s_yu, 1)
                ve.wait_ge(s_yu, U * (g + 1))
                ve.tensor_scalar(YC, YV, -1e4, 1e4, ALU.max, ALU.min)
                ve.tensor_tensor(YE, YV, YV, ALU.is_equal)
                step(ve.tensor_scalar(YM, YV, 0.0, 0.0, ALU.mult, ALU.is_equal))
                settle()
                step(ve.tensor_tensor(YC, YC, YE, ALU.mult))
                settle()
                step(ve.copy_predicated(YC, YM, YV))
                settle()
                x7 = X[:, U * g * D:U * (g + 1) * D]
                ve.tensor_tensor(x7, x7, YC, ALU.add).then_inc(s_fin, 1)


_INS = ['x', 'src', 'dst', 'edge_weight', 'L0_gnn_W6', 'L0_gnn_b6', 'L0_gnn_W7', 'L0_gnn_b7', 'L0_gnn_Wp', 'L0_gnn_bp',
        'L0_ffn_Wr', 'L0_ffn_br', 'L0_ffn_W1', 'L0_ffn_b1', 'L0_ffn_W2', 'L0_ffn_b2', 'L0_ffn_gamma', 'L0_ffn_beta',
        'L1_gnn_W1', 'L1_gnn_b1', 'L1_gnn_W2', 'L1_gnn_b2', 'L1_ffn_gate_w', 'L1_ffn_gate_b', 'L1_ffn_w1', 'L1_ffn_b1',
        'L1_ffn_w2', 'L1_ffn_b2']


def kernel(**inputs):
    import numpy as _np
    import concourse.bacc as _bacc
    from concourse import mybir as _mybir
    from concourse.bass_utils import run_bass_kernel_spmd as _run

    nc = _bacc.Bacc("TRN2", target_bir_lowering=False, num_devices=1)
    arrays, args = {}, []
    for name in _INS:
        a = _np.ascontiguousarray(inputs[name])
        arrays[f"in_{name}"] = a
        args.append(nc.dram_tensor(f"in_{name}", a.shape, _mybir.dt.from_np(a.dtype), kind="ExternalInput").ap())
    args.append(nc.dram_tensor("out_x", (N, D), _mybir.dt.float32, kind="ExternalOutput").ap())
    gnn_ffn(nc, *args)
    r = _run(nc, [arrays], core_ids=[0])
    return r.results[0]["out_x"]
```
